# Optimizing a Trainium2 kernel written in Bass

```python
import numpy as np
import jax
import jax.numpy as jnp

def _softmax(x, axis=-1):
    return jax.nn.softmax(x, axis=axis)

def _gelu(x):
    return jax.nn.gelu(x, approximate=True)

def _silu(x):
    return jax.nn.silu(x)

def _sigmoid(x):
    return jax.nn.sigmoid(x)

def _layernorm(x, axis=-1, eps=1e-05):
    m = jnp.mean(x, axis=axis, keepdims=True)
    v = jnp.var(x, axis=axis, keepdims=True)
    return (x - m) / jnp.sqrt(v + eps)

def _scatter_add(tgt, idx, src, axis=0):
    return tgt.at[idx].add(src)

def _segment_sum(src, seg, n):
    return jax.ops.segment_sum(src, seg, n)
kernel_name = 'mk_adaln_ffn_d2_seqx_r2_d96e78'

def setup_inputs(seed: int=0):
    np.random.seed(seed)
    _w = jnp.asarray

    def _rec_inputs():
        import jax
        import jax.numpy as jnp
        _rk = jax.random.key(seed)
        x = -0.000125 + 0.9999 * jax.random.normal(jax.random.fold_in(_rk, 1), (32, 128, 2048), jnp.float32)
        _lenS = 128 - jax.random.randint(jax.random.fold_in(_rk, 7), (32,), 0, max(1, 128 // 4) + 1, jnp.int32)
        _lenS2 = 128 - jax.random.randint(jax.random.fold_in(_rk, 8), (32,), 0, max(1, 128 // 4) + 1, jnp.int32)
        cond_128 = 0.0061147 + 1.02565 * jax.random.normal(jax.random.fold_in(_rk, 11), (32, 128), jnp.float32)
        fside_S_0 = -0.022604 + 0.987366 * jax.random.normal(jax.random.fold_in(_rk, 12), (128,), jnp.float32)
        return (x, cond_128, fside_S_0)
    x, cond_128, fside_S_0 = _rec_inputs()

    def _L0_cond_setup():
        import jax, jax.numpy as jnp
        import numpy as np
        from jax import lax
        N, C_IN, L = (32, 128, 2048)
        C_OUT, K, GROUPS = (128, 9, 4)
        C_DIM, PAD, STRIDE = (128, 4, 1)
        key = jax.random.key(seed)
        k1, k2, k3, k4, k5 = jax.random.split(key, 5)
        x = jax.random.normal(k1, (N, C_IN, L), dtype=jnp.float32)
        c = jax.random.normal(k2, (N, C_DIM), dtype=jnp.float32)
        weight = jax.random.normal(k3, (C_OUT, C_IN // GROUPS, K), dtype=jnp.float32)
        c_weight = jax.random.normal(k4, (C_OUT, C_DIM), dtype=jnp.float32)
        bias = jax.random.normal(k5, (C_OUT,), dtype=jnp.float32)
        return {'x': x, 'c': c, 'weight': weight, 'c_weight': c_weight, 'bias': bias}
    _L0_cond_all = _L0_cond_setup()
    _L0_cond_in = {k: v for k, v in _L0_cond_all.items() if k in ('weight', 'c_weight')}
    del _L0_cond_all

    def _L0_ffn_setup():
        import jax, jax.numpy as jnp
        import numpy as np
        B, T, D_IN, D_OUT = (8, 1024, 2048, 2048)
        N_LORAS, RANK = (16, 32)
        SCALING = 1.0
        key = jax.random.key(seed)
        ks = jax.random.split(key, 8)
        std = 1.0 / D_IN ** 0.5
        x = jax.random.normal(ks[0], (B, T, D_IN), dtype=jnp.float32)
        idx = jax.random.randint(ks[1], (B,), 0, N_LORAS)
        gate = jax.nn.one_hot(idx, N_LORAS, dtype=jnp.float32)
        kernel = jax.random.normal(ks[2], (D_IN, D_OUT), dtype=jnp.float32) * std
        bias = jnp.zeros((D_OUT,), dtype=jnp.float32)
        lora_A = jax.random.normal(ks[3], (N_LORAS, RANK, D_IN), dtype=jnp.float32) * std
        lora_B = jax.random.normal(ks[4], (N_LORAS, D_OUT, RANK), dtype=jnp.float32) * 0.01
        lora_A_shared = jax.random.normal(ks[5], (RANK, D_IN), dtype=jnp.float32) * std
        lora_B_shared = jax.random.normal(ks[6], (D_OUT, RANK), dtype=jnp.float32) * 0.01
        return {'x': x, 'gate': gate, 'kernel': kernel, 'bias': bias, 'lora_A': lora_A, 'lora_B': lora_B, 'lora_A_shared': lora_A_shared, 'lora_B_shared': lora_B_shared}
    _L0_ffn_all = _L0_ffn_setup()
    _L0_ffn_in = {k: v for k, v in _L0_ffn_all.items() if k in ('gate', 'kernel', 'bias', 'lora_A', 'lora_B', 'lora_A_shared', 'lora_B_shared')}
    del _L0_ffn_all

    def _L1_cond_setup():
        import jax, jax.numpy as jnp
        import numpy as np
        K = 8
        T = 1.0
        D_EMBD = 128
        IN_C = 128
        OUT_C = 128
        BS = 32
        H = 2048
        HID = 128
        key = jax.random.key(seed)
        ks = jax.random.split(key, 10)
        s = lambda fan_in: 1.0 / np.sqrt(fan_in)
        return {'x': jax.random.normal(ks[0], (BS, IN_C, H), dtype=jnp.float32), 'embedding': jax.random.normal(ks[1], (BS, D_EMBD), dtype=jnp.float32), 'W0': jax.random.normal(ks[2], (D_EMBD, HID), dtype=jnp.float32) * s(D_EMBD), 'b0': jnp.zeros((HID,), dtype=jnp.float32), 'W1': jax.random.normal(ks[3], (HID, HID), dtype=jnp.float32) * s(HID), 'b1': jnp.zeros((HID,), dtype=jnp.float32), 'W2': jax.random.normal(ks[4], (HID, K), dtype=jnp.float32) * s(HID), 'b2': jnp.zeros((K,), dtype=jnp.float32), 'weight': jax.random.normal(ks[5], (K, OUT_C, IN_C, 1), dtype=jnp.float32) * s(IN_C), 'bias_k': jax.random.normal(ks[6], (K, OUT_C), dtype=jnp.float32) * 0.1}
    _L1_cond_all = _L1_cond_setup()
    _L1_cond_in = {k: v for k, v in _L1_cond_all.items() if k in ('W0', 'b0', 'W1', 'b1', 'W2', 'b2', 'weight', 'bias_k')}
    del _L1_cond_all

    def _L1_ffn_setup():
        import jax, jax.numpy as jnp
        import numpy as np
        HID, BOT, RDIM, NSLOT, K, VB = (2048, 64, 48, 512, 8, 128)
        TAU_LOW, TAU_HIGH, EARLY_EXIT = (0.5, 2.0, 0.05)

        def _uncertainty(h, Wu1, bu1, Wu2, bu2):
            var = jnp.var(h, axis=-1)
            log_var = jnp.log1p(var)
            norm_var = log_var / (jnp.mean(log_var) + 1e-06)
            learned = (jax.nn.gelu(h @ Wu1.T + bu1) @ Wu2.T + bu2)[..., 0]
            return jnp.clip(norm_var * 0.5 + jax.nn.sigmoid(learned) * 2.5, 0.0, 5.0)
        key = jax.random.key(seed)
        ks = jax.random.split(key, 12)
        B, S = (2, 1024)
        return {'hidden_states': jax.random.normal(ks[0], (B, S, HID), dtype=jnp.float32), 'Wq': jax.random.normal(ks[1], (BOT, HID), dtype=jnp.float32) / np.sqrt(HID), 'Wr': jax.random.normal(ks[2], (RDIM, BOT), dtype=jnp.float32) / np.sqrt(BOT), 'aux_keys': jax.random.normal(ks[3], (NSLOT, BOT), dtype=jnp.float32) * 0.01, 'aux_values': jax.random.normal(ks[4], (NSLOT, HID), dtype=jnp.float32) * 0.02, 'Wvd': jax.random.normal(ks[5], (VB, HID), dtype=jnp.float32) * 0.1 / np.sqrt(HID), 'Wvu': jax.random.normal(ks[6], (HID, VB), dtype=jnp.float32) * 0.1 / np.sqrt(VB), 'Wu1': jax.random.normal(ks[7], (HID // 4, HID), dtype=jnp.float32) / np.sqrt(HID), 'bu1': jnp.zeros((HID // 4,), dtype=jnp.float32), 'Wu2': jax.random.normal(ks[8], (1, HID // 4), dtype=jnp.float32) * 0.01, 'bu2': jnp.zeros((1,), dtype=jnp.float32), 'gate_w1': jnp.float32(0.5), 'gate_bias': jnp.float32(-1.0), 'log_rel': jnp.zeros((NSLOT,), dtype=jnp.float32)}
    _L1_ffn_all = _L1_ffn_setup()
    _L1_ffn_in = {k: v for k, v in _L1_ffn_all.items() if k in ('Wq', 'Wr', 'aux_keys', 'aux_values', 'Wvd', 'Wvu', 'Wu1', 'bu1', 'Wu2', 'bu2', 'gate_w1', 'gate_bias', 'log_rel')}
    del _L1_ffn_all
    return {'x': x, 'cond_128': cond_128, 'fside_S_0': fside_S_0, 'L0_cond_weight': _L0_cond_in['weight'], 'L0_cond_c_weight': _L0_cond_in['c_weight'], 'L0_ffn_gate': _L0_ffn_in['gate'], 'L0_ffn_kernel': _L0_ffn_in['kernel'], 'L0_ffn_bias': _L0_ffn_in['bias'], 'L0_ffn_lora_A': _L0_ffn_in['lora_A'], 'L0_ffn_lora_B': _L0_ffn_in['lora_B'], 'L0_ffn_lora_A_shared': _L0_ffn_in['lora_A_shared'], 'L0_ffn_lora_B_shared': _L0_ffn_in['lora_B_shared'], 'L1_cond_W0': _L1_cond_in['W0'], 'L1_cond_b0': _L1_cond_in['b0'], 'L1_cond_W1': _L1_cond_in['W1'], 'L1_cond_b1': _L1_cond_in['b1'], 'L1_cond_W2': _L1_cond_in['W2'], 'L1_cond_b2': _L1_cond_in['b2'], 'L1_cond_weight': _L1_cond_in['weight'], 'L1_cond_bias_k': _L1_cond_in['bias_k'], 'L1_ffn_Wq': _L1_ffn_in['Wq'], 'L1_ffn_Wr': _L1_ffn_in['Wr'], 'L1_ffn_aux_keys': _L1_ffn_in['aux_keys'], 'L1_ffn_aux_values': _L1_ffn_in['aux_values'], 'L1_ffn_Wvd': _L1_ffn_in['Wvd'], 'L1_ffn_Wvu': _L1_ffn_in['Wvu'], 'L1_ffn_Wu1': _L1_ffn_in['Wu1'], 'L1_ffn_bu1': _L1_ffn_in['bu1'], 'L1_ffn_Wu2': _L1_ffn_in['Wu2'], 'L1_ffn_bu2': _L1_ffn_in['bu2'], 'L1_ffn_gate_w1': _L1_ffn_in['gate_w1'], 'L1_ffn_gate_bias': _L1_ffn_in['gate_bias'], 'L1_ffn_log_rel': _L1_ffn_in['log_rel']}

def reference(x, cond_128, fside_S_0, L0_cond_weight, L0_cond_c_weight, L0_ffn_gate, L0_ffn_kernel, L0_ffn_bias, L0_ffn_lora_A, L0_ffn_lora_B, L0_ffn_lora_A_shared, L0_ffn_lora_B_shared, L1_cond_W0, L1_cond_b0, L1_cond_W1, L1_cond_b1, L1_cond_W2, L1_cond_b2, L1_cond_weight, L1_cond_bias_k, L1_ffn_Wq, L1_ffn_Wr, L1_ffn_aux_keys, L1_ffn_aux_values, L1_ffn_Wvd, L1_ffn_Wvu, L1_ffn_Wu1, L1_ffn_bu1, L1_ffn_Wu2, L1_ffn_bu2, L1_ffn_gate_w1, L1_ffn_gate_bias, L1_ffn_log_rel):
    import jax
    import jax.numpy as jnp

    def _L0_cond_ref(x, c, weight, c_weight, bias):
        import jax, jax.numpy as jnp
        import numpy as np
        from jax import lax
        N, C_IN, L = (32, 128, 2048)
        C_OUT, K, GROUPS = (128, 9, 4)
        C_DIM, PAD, STRIDE = (128, 4, 1)
        out = lax.conv_general_dilated(x, weight, window_strides=(STRIDE,), padding=[(PAD, PAD)], dimension_numbers=('NCH', 'OIH', 'NCH'), feature_group_count=GROUPS)
        ctx = jnp.einsum('nd,od->no', c, c_weight)
        out = out + ctx[:, :, None] + bias[None, :, None]
        return out

    def _L0_ffn_ref(x, gate, kernel, bias, lora_A, lora_B, lora_A_shared, lora_B_shared):
        import jax, jax.numpy as jnp
        import numpy as np
        B, T, D_IN, D_OUT = (8, 1024, 2048, 2048)
        N_LORAS, RANK = (16, 32)
        SCALING = 1.0
        base_out = jnp.matmul(x, kernel) + bias
        b = gate.shape[0]
        x_flat = x.reshape(b, -1, x.shape[-1])
        A_eff = jnp.einsum('bn,nri->bri', gate, lora_A)
        B_eff = jnp.einsum('bn,nor->bor', gate, lora_B)
        Ax = jnp.einsum('bri,bti->btr', A_eff, x_flat)
        delta_flat = jnp.einsum('bor,btr->bto', B_eff, Ax)
        Ax_s = jnp.einsum('ri,bti->btr', lora_A_shared, x_flat)
        delta_flat = delta_flat + jnp.einsum('or,btr->bto', lora_B_shared, Ax_s)
        delta = delta_flat.reshape(x.shape[:-1] + (kernel.shape[-1],))
        return base_out + (SCALING * delta).astype(base_out.dtype)

    def _L1_cond_ref(x, embedding, W0, b0, W1, b1, W2, b2, weight, bias_k):
        import jax, jax.numpy as jnp
        import numpy as np
        K = 8
        T = 1.0
        D_EMBD = 128
        IN_C = 128
        OUT_C = 128
        BS = 32
        H = 2048
        HID = 128
        h = jax.nn.gelu(embedding @ W0 + b0, approximate=False)
        h = jax.nn.gelu(h @ W1 + b1, approximate=False)
        att = jax.nn.softmax((h @ W2 + b2) / T, axis=-1)
        agg_w = jnp.einsum('bk,koi->boi', att, weight[..., 0])
        agg_b = att @ bias_k
        out = jnp.einsum('boi,bih->boh', agg_w, x) + agg_b[:, :, None]
        return out

    def _L1_ffn_ref(hidden_states, Wq, Wr, aux_keys, aux_values, Wvd, Wvu, Wu1, bu1, Wu2, bu2, gate_w1, gate_bias, log_rel):
        import jax, jax.numpy as jnp
        import numpy as np
        HID, BOT, RDIM, NSLOT, K, VB = (2048, 64, 48, 512, 8, 128)
        TAU_LOW, TAU_HIGH, EARLY_EXIT = (0.5, 2.0, 0.05)

        def _uncertainty(h, Wu1, bu1, Wu2, bu2):
            var = jnp.var(h, axis=-1)
            log_var = jnp.log1p(var)
            norm_var = log_var / (jnp.mean(log_var) + 1e-06)
            learned = (jax.nn.gelu(h @ Wu1.T + bu1) @ Wu2.T + bu2)[..., 0]
            return jnp.clip(norm_var * 0.5 + jax.nn.sigmoid(learned) * 2.5, 0.0, 5.0)
        query = hidden_states @ Wq.T
        rq = query @ Wr.T
        rk = aux_keys @ Wr.T
        router_scores = jnp.einsum('bsr,nr->bsn', rq, rk) / np.sqrt(RDIM) + log_rel
        top_scores, top_idx = jax.lax.top_k(router_scores, K)
        sel_keys = aux_keys[top_idx]
        attn = jnp.einsum('bsd,bskd->bsk', query, sel_keys) / np.sqrt(BOT) + log_rel[top_idx]
        w = jax.nn.softmax(attn, axis=-1)
        sel_vals = aux_values[top_idx]
        aux_out = jnp.einsum('bsk,bskh->bsh', w, sel_vals)
        aux_out = aux_out @ Wvd.T @ Wvu.T
        u = _uncertainty(hidden_states, Wu1, bu1, Wu2, bu2)
        u_norm = jnp.clip((u - TAU_LOW) / (TAU_HIGH - TAU_LOW), 0.0, 1.0)
        gate = jax.nn.sigmoid(gate_w1 * u_norm + gate_bias)
        gate = jnp.where(gate < EARLY_EXIT, 0.0, gate)
        return hidden_states + gate[..., None] * aux_out
    x = x + _L0_ffn_ref(_L0_cond_ref(x, cond_128, L0_cond_weight, L0_cond_c_weight, fside_S_0), L0_ffn_gate, L0_ffn_kernel, L0_ffn_bias, L0_ffn_lora_A, L0_ffn_lora_B, L0_ffn_lora_A_shared, L0_ffn_lora_B_shared)
    x = x + _L1_ffn_ref(_L1_cond_ref(x, cond_128, L1_cond_W0, L1_cond_b0, L1_cond_W1, L1_cond_b1, L1_cond_W2, L1_cond_b2, L1_cond_weight, L1_cond_bias_k), L1_ffn_Wq, L1_ffn_Wr, L1_ffn_aux_keys, L1_ffn_aux_values, L1_ffn_Wvd, L1_ffn_Wvu, L1_ffn_Wu1, L1_ffn_bu1, L1_ffn_Wu2, L1_ffn_bu2, L1_ffn_gate_w1, L1_ffn_gate_bias, L1_ffn_log_rel)
    return x

_drawn_inputs = setup_inputs


def setup_inputs(seed=0):
    import zlib

    import numpy as np

    out = dict(_drawn_inputs(seed))
    spreads = {'L0_ffn_bias': (0.0, 0.8),
     'L1_cond_b0': (0.0, 0.627),
     'L1_cond_b1': (0.0, 0.446),
     'L1_cond_b2': (0.0, 0.347),
     'L1_ffn_bu1': (0.0, 2.0),
     'L1_ffn_log_rel': (0.0, 2.0)}
    factors = {'L1_cond_bias_k': 33.676,
     'L1_ffn_Wq': 64.0,
     'L1_ffn_Wr': 64.0,
     'L1_ffn_aux_keys': 64.0,
     'L1_ffn_aux_values': 64.0,
     'L1_ffn_Wvd': 64.0,
     'L1_ffn_Wvu': 64.0,
     'L1_ffn_Wu1': 64.0,
     'L1_ffn_Wu2': 64.0}
    for name, (base, spread) in spreads.items():
        noise = np.random.default_rng([zlib.crc32(name.encode()), seed]).standard_normal(out[name].shape)
        drawn = base * np.exp(spread * noise) if base else spread * noise
        out[name] = jnp.asarray(drawn.astype(out[name].dtype))
    for name, factor in factors.items():
        out[name] = (out[name] * factor).astype(out[name].dtype)
    return out
```

```python
from contextlib import ExitStack

import concourse.bass as bass
from concourse import mybir

P = 128
N, C, L = 32, 128, 2048
TAPS, PAD, GROUPS = 9, 4, 4
GC = C // GROUPS
PH = P // GC
M = L // PH
MC = M // P
KC = L // P
B, SPB = 8, N // 8
NL, R = 16, 32
NJ = NL * R // P
HALF = L // 2
NE = 8
BOT, RD, NS, VB, UH = 64, 48, 512, 128, 512
TAU_LOW, TAU_HIGH, EARLY_EXIT = 0.5, 2.0, 0.05
STEPS = 8
FAR = -3.0e38
BANK = 512

F32 = mybir.dt.float32
F32R = mybir.dt.float32r
ALU = mybir.AluOpType
ACT = mybir.ActivationFunctionType
AX_X = mybir.AxisListType.X


class Places:

    def __init__(self, nc, ctx, stage):
        self.nc, self.ctx, self.stage = nc, ctx, stage

    def sb(self, name, shape, dt=F32):
        return self.ctx.enter_context(self.nc.sbuf_tensor(f"{self.stage}_{name}", shape, dt))

    def sem(self, name):
        return self.ctx.enter_context(self.nc.semaphore(f"{self.stage}_{name}"))


def prologue(nc, ps, a, scr):
    with ExitStack() as ctx:
        at = Places(nc, ctx, "pro")
        ident = at.sb("ident", [P, P])
        mask = at.sb("mask", [P, R])
        gcol = at.sb("gcol", [P, NJ, B])
        G = at.sb("G", [P, NJ, B * R])
        condT = at.sb("condT", [P, N])
        cwT = at.sb("cwT", [P, C])
        bias_bc = at.sb("bias_bc", [N, C])
        crow = at.sb("crow", [N, C])
        W0 = at.sb("W0", [P, P])
        W1 = at.sb("W1", [P, P])
        W2 = at.sb("W2", [P, NE])
        b0 = at.sb("b0", [P, 1])
        b1 = at.sb("b1", [P, 1])
        b2_bc = at.sb("b2_bc", [N, NE])
        bias_k = at.sb("bias_k", [NE, C])
        h1 = at.sb("h1", [P, N])
        h2 = at.sb("h2", [P, N])
        lg = at.sb("lg", [N, NE])
        mx = at.sb("mx", [N, 1])
        nmx = at.sb("nmx", [N, 1])
        ex = at.sb("ex", [N, NE])
        sm = at.sb("sm", [N, 1])
        rs = at.sb("rs", [N, 1])
        att = at.sb("att", [N, NE])
        attT = at.sb("attT", [NE, N])
        aggb = at.sb("aggb", [N, C])
        wk = at.sb("wk", [NE, C * C])
        aggst = at.sb("aggst", [N, 2, 4 * BANK])
        loraA = at.sb("loraA", [P, NJ, L])
        loraB = at.sb("loraB", [P, NJ, L])
        ash = at.sb("ash", [P, KC, R])
        aout = at.sb("aout", [P, KC, B, 2 * R])
        bout = at.sb("bout", [P, 2, L // 2])

        small_in, gate_in, la_in, lb_in, wk_in, ash_in = (
            at.sem(s) for s in ("small_in", "gate_in", "la_in", "lb_in", "wk_in", "ash_in"))
        id0, id1, mask_ok, G_ok = (at.sem(s) for s in ("id0", "id1", "mask_ok", "G_ok"))
        mlp_mm, mlp_act, soft, soft_act, crow_mm, crow_ok = (
            at.sem(s) for s in ("mlp_mm", "mlp_act", "soft", "soft_act", "crow_mm", "crow_ok"))
        fa_mm, fa_ok, shared_ok, fb_mm, fb_ok, ag_mm, ag_ok = (
            at.sem(s) for s in ("fa_mm", "fa_ok", "shared_ok", "fb_mm", "fb_ok", "ag_mm", "ag_ok"))
        stored = at.sem("stored")
        bst = [at.sem(f"bst{i}") for i in range(2)]
        gst = [at.sem(f"gst{i}") for i in range(2)]
        block = ctx.enter_context(nc.Block())

        @block.sync
        def _(sp):
            small = [(condT[:, :], a["condT"]), (cwT[:, :], a["cwT"]),
                     (bias_bc[:, :], a["conv_bias"].to_broadcast([N, C])),
                     (W0[:, :], a["W0"]), (W1[:, :], a["W1"]), (W2[:, :], a["W2"]),
                     (b0[:, :], a["b0"].unsqueeze(1)), (b1[:, :], a["b1"].unsqueeze(1)),
                     (b2_bc[:, :], a["b2"].to_broadcast([N, NE])),
                     (bias_k[:, :], a["bias_k"])]
            for dst, src in small:
                sp.dma_start(dst, src).then_inc(small_in, 16)
            sp.dma_start(loraA[:, :, :], a["loraA"].rearrange("(j p) l -> p j l", p=P)).then_inc(la_in, 16)
            sp.dma_start(wk[:, :], a["wk"]).then_inc(wk_in, 16)
            sp.dma_start(loraB[:, :, :], a["loraB"].rearrange("(j p) l -> p j l", p=P)).then_inc(lb_in, 16)
            sp.wait_ge(crow_ok, 1)
            sp.dma_start(scr["crow"], crow[:, :]).then_inc(stored, 16)
            sp.wait_ge(fa_ok, KC)
            sp.wait_ge(shared_ok, B)
            for b in range(B):
                sp.dma_start(scr["la"][b], aout[:, :, b, :]).then_inc(stored, 16)
            lb = scr["lb"].rearrange("b r l -> (b r) l")
            for t in range(4):
                sp.wait_ge(fb_ok, 2 * (t + 1))
                sp.dma_start(lb[(t // 2) * P:(t // 2 + 1) * P, (t % 2) * (L // 2):(t % 2 + 1) * (L // 2)],
                             bout[:, t % 2, :]).then_inc(bst[t % 2], 16)
            sp.wait_ge(soft, 9)
            sp.dma_start(scr["aggb"], aggb[:, :]).then_inc(stored, 16)
            for t in range(8):
                sp.wait_ge(ag_ok, 4 * (t + 1))
                sp.dma_start(scr["agg"][:, t * 4 * BANK:(t + 1) * 4 * BANK],
                             aggst[:, t % 2, :]).then_inc(gst[t % 2], 16)
            sp.wait_ge(stored, 16 * (B + 2))
            for i in range(2):
                sp.wait_ge(bst[i], 32)
                sp.wait_ge(gst[i], 64)

        @block.gpsimd
        def _(pool):
            pool.memset(ident[:, :], 0.0).then_inc(id0, 1)
            for j in range(NJ):
                for n in range(P // R):
                    k = j * (P // R) + n
                    pool.dma_start(gcol[n * R:(n + 1) * R, j, :],
                                   a["gateT"][k:k + 1, :].to_broadcast([R, B])).then_inc(gate_in, 16)
            pool.dma_start(ash[:, :, :].rearrange("p (c q) r -> p c q r", q=PH),
                           a["laS"].rearrange("(c m q) r -> m c q r", m=P, q=PH)).then_inc(ash_in, 16)
            pool.wait_ge(id0, 1)
            pool.affine_select(out=ident[:, :], in_=ident[:, :], compare_op=ALU.not_equal, fill=1.0,
                               base=0, pattern=[[-1, P]], channel_multiplier=1).then_inc(id1, 1)

        @block.scalar
        def _(act):
            act.wait_ge(mlp_mm, 1)
            act.activation(h1[:, :], ps[0][:, 0:N], ACT.Gelu, bias=b0[:, 0:1]).then_inc(mlp_act, 1)
            act.wait_ge(mlp_mm, 2)
            act.activation(h2[:, :], ps[1][:, 0:N], ACT.Gelu, bias=b1[:, 0:1]).then_inc(mlp_act, 1)
            act.wait_ge(soft, 3)
            act.activation(ex[:, :], lg[:, :], ACT.Exp, bias=nmx[:, 0:1]).then_inc(soft_act, 1)

        @block.tensor
        def _(pe):
            pe.wait_ge(small_in, 160)
            pe.matmul(ps[0][:, 0:N], W0[:, :], condT[:, :], start=True, stop=True).then_inc(mlp_mm, 1)
            pe.matmul(ps[2][0:N, 0:C], condT[:, :], cwT[:, :], start=True, stop=True).then_inc(crow_mm, 1)
            pe.wait_ge(mlp_act, 1)
            pe.matmul(ps[1][:, 0:N], W1[:, :], h1[:, :], start=True, stop=True).then_inc(mlp_mm, 1)
            pe.wait_ge(mlp_act, 2)
            pe.matmul(ps[3][0:N, 0:NE], h2[:, :], W2[:, :], start=True, stop=True).then_inc(mlp_mm, 1)
            pe.wait_ge(G_ok, NJ * B)
            pe.wait_ge(la_in, 16)
            for kc in range(KC):
                if kc >= 2:
                    pe.wait_ge(fa_ok, kc - 1)
                mc, q = divmod(kc, PH)
                for j in range(NJ):
                    lhs = loraA[:, j, :].rearrange("p (c m q) -> p c q m", m=P, q=PH)[:, mc, q, :]
                    mm = pe.matmul(ps[4 + kc % 2][:, 0:B * R], lhs, G[:, j, :], start=(j == 0), stop=(j == NJ - 1))
                mm.then_inc(fa_mm, 1)
            pe.wait_ge(lb_in, 16)
            for t in range(8):
                if t >= 2:
                    pe.wait_ge(fb_ok, t - 1)
                for j in range(NJ):
                    mm = pe.matmul(ps[6 + t % 2][:, :], G[:, j, (t // 4) * P:(t // 4 + 1) * P],
                                   loraB[:, j, (t % 4) * BANK:(t % 4 + 1) * BANK],
                                   start=(j == 0), stop=(j == NJ - 1))
                mm.then_inc(fb_mm, 1)
            pe.wait_ge(soft, 7)
            pe.transpose(ps[0][0:NE, 0:N], att[:, :], ident[0:N, 0:N]).then_inc(mlp_mm, 1)
            pe.wait_ge(soft, 8)
            pe.matmul(ps[1][0:N, 0:C], attT[:, :], bias_k[:, :], start=True, stop=True).then_inc(mlp_mm, 1)
            pe.wait_ge(wk_in, 16)
            for t in range(C * C // BANK):
                if t >= 2:
                    pe.wait_ge(ag_ok, t - 1)
                pe.matmul(ps[2 + t % 2][0:N, :], attT[:, :], wk[:, t * BANK:(t + 1) * BANK],
                          start=True, stop=True).then_inc(ag_mm, 1)

        @block.vector
        def _(dve):
            dve.wait_ge(id1, 1)
            dve.tensor_reduce(mask[:, :], ident[:, :].rearrange("p (n r) -> p r n", r=R), AX_X,
                              ALU.add).then_inc(mask_ok, 1)
            dve.wait_ge(mask_ok, 1)
            dve.wait_ge(gate_in, 16 * NL)
            for j in range(NJ):
                for b in range(B):
                    dve.tensor_scalar(G[:, j, b * R:(b + 1) * R], mask[:, :], gcol[:, j, b:b + 1], None,
                                      ALU.mult).then_inc(G_ok, 1)
            dve.wait_ge(crow_mm, 1)
            dve.tensor_tensor(crow[:, :], ps[2][0:N, 0:C], bias_bc[:, :], ALU.add).then_inc(crow_ok, 1)
            dve.wait_ge(mlp_mm, 3)
            dve.tensor_tensor(lg[:, :], ps[3][0:N, 0:NE], b2_bc[:, :], ALU.add).then_inc(soft, 1)
            dve.wait_ge(soft, 1)
            dve.tensor_reduce(mx[:, :], lg[:, :], AX_X, ALU.max).then_inc(soft, 1)
            dve.wait_ge(soft, 2)
            dve.tensor_scalar(nmx[:, :], mx[:, :], -1.0, None, ALU.mult).then_inc(soft, 1)
            dve.wait_ge(soft_act, 1)
            dve.tensor_reduce(sm[:, :], ex[:, :], AX_X, ALU.add).then_inc(soft, 1)
            dve.wait_ge(soft, 4)
            dve.reciprocal(rs[:, :], sm[:, :]).then_inc(soft, 1)
            dve.wait_ge(soft, 5)
            dve.tensor_scalar(att[:, :], ex[:, :], rs[:, 0:1], None, ALU.mult).then_inc(soft, 2)
            dve.wait_ge(ash_in, 16)
            for b in range(B):
                dve.tensor_copy(aout[:, :, b, R:2 * R], ash[:, :, :]).then_inc(shared_ok, 1)
            for kc in range(KC):
                dve.wait_ge(fa_mm, kc + 1)
                dve.tensor_copy(aout[:, kc, :, 0:R],
                                ps[4 + kc % 2][:, 0:B * R].rearrange("p (b r) -> p b r", r=R)).then_inc(fa_ok, 1)
            for t in range(8):
                dve.wait_ge(fb_mm, t + 1)
                if t >= 4:
                    dve.wait_ge(bst[(t // 2) % 2], 16)
                dve.tensor_copy(bout[:, (t // 2) % 2, (t % 2) * BANK:(t % 2 + 1) * BANK],
                                ps[6 + t % 2][:, :]).then_inc(fb_ok, 1)
            dve.wait_ge(mlp_mm, 4)
            dve.tensor_copy(attT[:, :], ps[0][0:NE, 0:N]).then_inc(soft, 1)
            dve.wait_ge(mlp_mm, 5)
            dve.tensor_copy(aggb[:, :], ps[1][0:N, 0:C]).then_inc(soft, 1)
            for t in range(C * C // BANK):
                dve.wait_ge(ag_mm, t + 1)
                if t // 4 >= 2:
                    dve.wait_ge(gst[(t // 4) % 2], 16 * (t // 8))
                dve.tensor_copy(aggst[:, (t // 4) % 2, (t % 4) * BANK:(t % 4 + 1) * BANK],
                                ps[2 + t % 2][0:N, :]).then_inc(ag_ok, 1)


def convolve(nc, ps, a, scr):
    BODY = 2 * SPB
    with ExitStack() as ctx:
        at = Places(nc, ctx, "conv")
        taps = at.sb("taps", [P, 3, GROUPS, PH * GC])
        xb = [at.sb(f"xb{i}", [P, GROUPS, M + 2]) for i in range(2)]
        ct = [at.sb(f"ct{i}", [P, KC, C]) for i in range(2)]
        crow_bc = at.sb("crow_bc", [P, N, C])
        la = [at.sb(f"la{i}", [P, KC, 2 * R]) for i in range(2)]
        axs = [at.sb(f"axs{i}", [2 * R, P]) for i in range(2)]

        zeroed, taps_in, crow_in = at.sem("zeroed"), at.sem("taps_in"), at.sem("crow_in")
        x_in = [at.sem(f"x_in{i}") for i in range(2)]
        la_in = [at.sem(f"la_in{i}") for i in range(2)]
        conv_mm = at.sem("conv_mm")
        conv_out = at.sem("conv_out")
        ax_mm = at.sem("ax_mm")
        ax_out = at.sem("ax_out")
        ct_st = [at.sem(f"ct_st{i}") for i in range(2)]
        ax_st = [at.sem(f"ax_st{i}") for i in range(2)]
        block = ctx.enter_context(nc.Block())

        @block.sync
        def _(sp):
            sp.wait_ge(zeroed, 3)
            for p in range(PH):
                for q in range(PH):
                    for s in (-1, 0, 1):
                        k = PH * s + p - q + PAD
                        if 0 <= k < TAPS:
                            sp.dma_start(taps[p * GC:(p + 1) * GC, s + 1, :, q * GC:(q + 1) * GC],
                                         a["taps"][k]).then_inc(taps_in, 16)

            def load_x(n, u):
                sp.dma_start(xb[u % 2][:, :, 1:M + 1],
                             a["xph"][n].rearrange("p (g m) -> p g m", g=GROUPS)).then_inc(x_in[u % 2], 16)

            load_x(0, 0)
            load_x(1, 1)
            with sp.Fori(1, N // 2) as i:
                for u in range(2):
                    sp.wait_ge(conv_mm, MC * (2 * i + u - 1))
                    load_x(2 * i + u, u)
            for i in range(2):
                sp.wait_ge(ct_st[i], 16 + 16 * N // 2)
                sp.wait_ge(ax_st[i], 16 + 16 * N // 2)

        @block.gpsimd
        def _(pool):
            pool.dma_start(crow_bc[:, :, :], scr["crow"].unsqueeze(0).to_broadcast([P, N, C])).then_inc(crow_in, 16)
            with pool.Fori(0, B // 2) as i:
                for u in range(2):
                    pool.wait_ge(ax_mm, SPB * (2 * i + u))
                    pool.dma_start(la[u][:, :, :], scr["la"][2 * i + u]).then_inc(la_in[u], 16)

        @block.tensor
        def _(pe):
            pe.sem_inc(ax_mm, SPB)
            pe.wait_ge(taps_in, 16 * TAPS * PH)
            with pe.Fori(0, N // BODY) as i:
                for u in range(BODY):
                    n = BODY * i + u
                    pe.wait_ge(x_in[u % 2], 16 * (BODY // 2 * i + u // 2 + 1))
                    for mc in range(MC):
                        pe.wait_ge(conv_out, MC * n + mc + 1)
                        for g in range(GROUPS):
                            for s in range(3):
                                mm = pe.matmul(ps[mc][:, g * P:(g + 1) * P],
                                               xb[u % 2][:, g, P * mc + s:P * (mc + 1) + s],
                                               taps[:, s, g, :], start=(s == 0), stop=(s == 2))
                        mm.then_inc(conv_mm, 1)
                    if u % SPB == 0:
                        pe.wait_ge(la_in[u // SPB], 16 * (i + 1))
                    pe.wait_ge(ax_out, n + 1)
                    for kc in range(KC):
                        if kc % PH == 0:
                            pe.wait_ge(conv_out, MC + MC * n + kc // PH + 1)
                        mm = pe.matmul(ps[4 + u % 2][0:2 * R, 0:P], la[u // SPB][:, kc, :], ct[u % 2][:, kc, :],
                                       start=(kc == 0), stop=(kc == KC - 1))
                    mm.then_inc(ax_mm, 1)

        @block.vector
        def _(dve):
            dve.memset(taps[:, :, :, :], 0.0).then_inc(zeroed, 1)
            for i in range(2):
                dve.memset(xb[i][:, :, 0:M + 2:M + 1], 0.0).then_inc(zeroed, 1)
            dve.sem_inc(conv_out, MC)
            dve.wait_ge(crow_in, 16)
            with dve.Fori(0, N // 2) as i:
                for u in range(2):
                    n = 2 * i + u
                    ctx_row = crow_bc[:, n, :].rearrange("p (g o) -> p g o", g=GROUPS)
                    ctx_row = ctx_row.unsqueeze(2).to_broadcast([P, GROUPS, PH, GC])
                    dve.wait_ge(ax_mm, SPB + n - 1)
                    dve.wait_ge(ct_st[u], 16 * (i + 1))
                    for mc in range(MC):
                        dve.wait_ge(conv_mm, MC * n + mc + 1)
                        dst = ct[u][:, PH * mc:PH * (mc + 1), :].rearrange("p q (g o) -> p g q o", g=GROUPS)
                        src = ps[mc][:, :].rearrange("p (g q o) -> p g q o", g=GROUPS, q=PH)
                        dve.tensor_tensor(dst, src, ctx_row, ALU.add).then_inc(conv_out, 1)

        @block.scalar
        def _(act):
            act.sem_inc(ax_out, 2)
            for i in range(2):
                act.sem_inc(ct_st[i], 16)
                act.sem_inc(ax_st[i], 16)
            with act.Fori(0, N // 2) as i:
                for u in range(2):
                    n = 2 * i + u
                    act.wait_ge(conv_out, MC + MC * (n + 1))
                    act.dma_start(scr["ct"][n], ct[u][:, :, :].rearrange("p k c -> p (k c)")).then_inc(ct_st[u], 16)
                    act.wait_ge(ax_mm, SPB + n + 1)
                    act.wait_ge(ax_st[u], 16 * (i + 1))
                    act.activation(axs[u][:, :], ps[4 + u][0:2 * R, 0:P], ACT.Copy).then_inc(ax_out, 1)
                    act.wait_ge(ax_out, 2 + n + 1)
                    act.dma_start(scr["ax"][n], axs[u][:, :]).then_inc(ax_st[u], 16)


def project(nc, ps, a, scr, half):
    c0 = half * HALF
    KR = 2 * R + 1
    QK = KC // 4
    with ExitStack() as ctx:
        at = Places(nc, ctx, f"proj{half}")
        khi = at.sb("khi", [P, KC, HALF], F32R)
        klo = at.sb("klo", [P, KC, HALF], F32R)
        kst = [at.sb(f"kst{i}", [P, HALF]) for i in range(2)]
        craw = [at.sb(f"craw{i}", [P, KC, C]) for i in range(2)]
        chi = at.sb("chi", [P, KC, C], F32R)
        clo = at.sb("clo", [P, KC, C], F32R)
        xr = [at.sb(f"xr{i}", [P, HALF]) for i in range(2)]
        yo = [at.sb(f"yo{i}", [P, HALF]) for i in range(2)]
        axr = [at.sb(f"axr{i}", [KR, P]) for i in range(2)]
        axh = [at.sb(f"axh{i}", [KR, P], F32R) for i in range(2)]
        axl = [at.sb(f"axl{i}", [KR, P], F32R) for i in range(2)]
        braw = at.sb("braw", [KR, HALF])
        bhi = at.sb("bhi", [KR, HALF], F32R)
        blo = at.sb("blo", [KR, HALF], F32R)

        k_in = [at.sem(f"k_in{i}") for i in range(2)]
        k_hi, k_lo = at.sem("k_hi"), at.sem("k_lo")
        c_in = [at.sem(f"c_in{i}") for i in range(2)]
        x_in = [at.sem(f"x_in{i}") for i in range(2)]
        ax_in = [at.sem(f"ax_in{i}") for i in range(2)]
        bs_in, b_in = at.sem("bs_in"), at.sem("b_in")
        one = at.sem("one")
        c_hi, c_lo = at.sem("c_hi"), at.sem("c_lo")
        ax_hi, ax_lo = at.sem("ax_hi"), at.sem("ax_lo")
        b_hi, b_lo = at.sem("b_hi"), at.sem("b_lo")
        c_used = at.sem("c_used")
        lora_mm = at.sem("lora_mm")
        y_out = at.sem("y_out")
        y_st = [at.sem(f"y_st{i}") for i in range(2)]
        block = ctx.enter_context(nc.Block())

        kern = a["kernel"].rearrange("(c m q) d -> c q m d", m=P, q=PH)

        @block.sync
        def _(sp):
            sp.dma_start(braw[R:2 * R, :], a["lbS"][:, c0:c0 + HALF]).then_inc(bs_in, 16)
            sp.dma_start(braw[2 * R:KR, :], a["ffn_bias"][:, c0:c0 + HALF]).then_inc(bs_in, 16)
            for kc in range(KC):
                if kc >= 2:
                    sp.wait_ge(k_lo, kc - 1)
                sp.dma_start(kst[kc % 2][:, :], kern[kc // PH, kc % PH, :, c0:c0 + HALF]).then_inc(k_in[kc % 2], 16)

            def load(n, u):
                sp.dma_start(craw[u % 2][:, :, :].rearrange("p k c -> p (k c)"), scr["ct"][n]).then_inc(c_in[u % 2], 16)
                sp.dma_start(axr[u % 2][0:2 * R, :], scr["ax"][n]).then_inc(ax_in[u % 2], 16)
                sp.dma_start(xr[u % 2][:, :], a["x"][n, :, c0:c0 + HALF]).then_inc(x_in[u % 2], 16)

            load(0, 0)
            load(1, 1)
            with sp.Fori(1, N // 2) as i:
                for u in range(2):
                    n = 2 * i + u
                    sp.wait_ge(y_out, 2 + n - 1)
                    load(n, u)

        @block.gpsimd
        def _(pool):
            with pool.Fori(0, B) as b:
                pool.wait_ge(b_lo, b + 1)
                pool.dma_start(braw[0:R, :], scr["lb"][b][:, c0:c0 + HALF]).then_inc(b_in, 16)
            for i in range(2):
                pool.wait_ge(y_st[i], 16 + 16 * N // 2)

        def high(act, n, b, u, j):
            if j == 0:
                act.wait_ge(c_in[u % 2], 16 * (b * (SPB // 2) + u // 2 + 1))
            act.wait_ge(c_used, 4 * n + j + 1)
            act.activation(chi[:, QK * j:QK * (j + 1), :], craw[u % 2][:, QK * j:QK * (j + 1), :],
                           ACT.Copy).then_inc(c_hi, 1)
            if j == 1:
                act.wait_ge(ax_in[u % 2], 16 * (b * (SPB // 2) + u // 2 + 1))
                act.wait_ge(lora_mm, n + 1)
                act.activation(axh[u % 2][:, :], axr[u % 2][:, :], ACT.Copy).then_inc(ax_hi, 1)
                if u == 0:
                    act.wait_ge(b_in, 16 * (b + 1))
                    act.wait_ge(lora_mm, 2 + n)
                    act.activation(bhi[:, :], braw[:, :], ACT.Copy).then_inc(b_hi, 1)

        def low(dve, n, b, u, j):
            s = slice(QK * j, QK * (j + 1))
            dve.wait_ge(c_hi, 4 * n + j + 1)
            dve.tensor_tensor(clo[:, s, :], craw[u % 2][:, s, :], chi[:, s, :].bitcast(F32),
                              ALU.subtract).then_inc(c_lo, 1)
            if j == 1:
                dve.wait_ge(ax_hi, n + 1)
                dve.tensor_tensor(axl[u % 2][:, :], axr[u % 2][:, :], axh[u % 2][:, :].bitcast(F32),
                                  ALU.subtract).then_inc(ax_lo, 1)
                if u == 0:
                    dve.wait_ge(b_hi, b + 1)
                    dve.tensor_tensor(blo[:, :], braw[:, :], bhi[:, :].bitcast(F32),
                                      ALU.subtract).then_inc(b_lo, 1)

        def y_sum(dve, n, b, u):
            dve.wait_ge(c_used, 4 + 4 * (n + 1))
            dve.wait_ge(x_in[u % 2], 16 * (b * (SPB // 2) + u // 2 + 1))
            dve.wait_ge(y_st[u % 2], 16 * (b * (SPB // 2) + u // 2 + 1))
            for h in range(2):
                s = slice(h * BANK, (h + 1) * BANK)
                add = dve.tensor_tensor(yo[u % 2][:, s], ps[2 * (u % 2) + h][:, :], xr[u % 2][:, s], ALU.add)
            add.then_inc(y_out, 1)

        def y_store(act, n, u):
            act.wait_ge(y_out, 2 + n + 1)
            act.dma_start(scr["y"][n, :, c0:c0 + HALF], yo[u % 2][:, :]).then_inc(y_st[u % 2], 16)

        @block.scalar
        def _(act):
            for i in range(2):
                act.sem_inc(y_st[i], 16)
            act.wait_ge(one, 2)
            act.wait_ge(bs_in, 32)
            for kc in range(KC):
                act.wait_ge(k_in[kc % 2], 16 * (kc // 2 + 1))
                act.activation(khi[:, kc, :], kst[kc % 2][:, :], ACT.Copy).then_inc(k_hi, 1)
            for j in range(4):
                high(act, 0, 0, 0, j)
            with act.Fori(0, B - 1) as b:
                for u in range(SPB):
                    n = SPB * b + u
                    v, w = (b, u + 1) if u + 1 < SPB else (b + 1, 0)
                    for j in range(4):
                        high(act, n + 1, v, w, j)
                    y_store(act, n, u)
            for u in range(SPB):
                n = SPB * (B - 1) + u
                if u + 1 < SPB:
                    for j in range(4):
                        high(act, n + 1, B - 1, u + 1, j)
                y_store(act, n, u)

        @block.vector
        def _(dve):
            for i in range(2):
                dve.memset(axr[i][2 * R:KR, :], 1.0).then_inc(one, 1)
            dve.sem_inc(y_out, 2)
            dve.sem_inc(b_lo, 1)
            for kc in range(KC):
                dve.wait_ge(k_hi, kc + 1)
                dve.tensor_tensor(klo[:, kc, :], kst[kc % 2][:, :], khi[:, kc, :].bitcast(F32),
                                  ALU.subtract).then_inc(k_lo, 1)
            for j in range(4):
                low(dve, 0, 0, 0, j)
            with dve.Fori(0, B - 1) as b:
                for u in range(SPB):
                    n = SPB * b + u
                    v, w = (b, u + 1) if u + 1 < SPB else (b + 1, 0)
                    for j in range(4):
                        if j == 3:
                            y_sum(dve, n, b, u)
                        low(dve, n + 1, v, w, j)
            for u in range(SPB):
                n = SPB * (B - 1) + u
                if u + 1 < SPB:
                    for j in range(3):
                        low(dve, n + 1, B - 1, u + 1, j)
                y_sum(dve, n, B - 1, u)
                if u + 1 < SPB:
                    low(dve, n + 1, B - 1, u + 1, 3)

        @block.tensor
        def _(pe):
            pe.sem_inc(c_used, 4)
            pe.sem_inc(lora_mm, 2)
            pe.wait_ge(k_lo, KC)
            with pe.Fori(0, B) as b:
                for u in range(SPB):
                    n = SPB * b + u
                    out = [ps[2 * (u % 2) + h] for h in range(2)]
                    pe.wait_ge(y_out, n + 1)
                    for j in range(4):
                        pe.wait_ge(c_lo, 4 * n + j + 1)
                        for kc in range(QK * j, QK * (j + 1)):
                            for lhs, parts in ((chi, (khi, klo)), (clo, (khi,))):
                                for h in range(2):
                                    for rhs in parts:
                                        mm = pe.matmul(out[h][:, :], lhs[:, kc, :],
                                                       rhs[:, kc, h * BANK:(h + 1) * BANK],
                                                       start=(kc == 0 and lhs is chi and rhs is khi),
                                                       stop=(kc == KC - 1 and lhs is clo))
                        mm.then_inc(c_used, 1)
                        if j == 1:
                            pe.wait_ge(ax_lo, n + 1)
                            pe.wait_ge(b_lo, b + 2)
                            for lhs, parts in ((axh[u % 2], (bhi, blo)), (axl[u % 2], (bhi,))):
                                for h in range(2):
                                    for rhs in parts:
                                        mm = pe.matmul(out[h][:, :], lhs[:, :], rhs[:, h * BANK:(h + 1) * BANK],
                                                       start=False, stop=False)
                            mm.then_inc(lora_mm, 1)


def attend(nc, ps, a, scr, keep):
    tT, var_all, learned, esum = keep
    T4 = KC // 4
    z_ps, t_ps, u_ps, s_ps, a_ps, m_ps = ps[0:2], ps[2:4], ps[4], ps[5], ps[6], ps[7]
    Q, RQ = slice(0, P), slice(P, 2 * P)
    with ExitStack() as ctx:
        at = Places(nc, ctx, "att")
        ident = at.sb("ident", [P, P])
        wst = [at.sb(f"wst{i}", [P, 2, UH + BOT]) for i in range(2)]
        wh = at.sb("wh", [P, KC, UH + BOT], F32R)
        wl = at.sb("wl", [P, KC, UH + BOT], F32R)
        vp = at.sb("vp", [P, NS // P, VB])
        keysT = at.sb("keysT", [BOT, NS])
        wrT = at.sb("wrT", [BOT, P])
        rkT = at.sb("rkT", [RD, NS])
        lrel = at.sb("lrel", [P, NS])
        bu1 = at.sb("bu1", [P, UH])
        wu2 = at.sb("wu2", [P, UH])
        zb = [at.sb(f"zb{i}", [P, 1]) for i in range(2)]
        yb = [at.sb(f"yb{i}", [P, L]) for i in range(2)]
        ag = [at.sb(f"ag{i}", [P, C]) for i in range(2)]
        z = [at.sb(f"z{i}", [P, L]) for i in range(2)]
        yz = [at.sb(f"yz{i}", [P, L]) for i in range(2)]
        zh = at.sb("zh", [P, KC, P], F32R)
        zl = at.sb("zl", [P, KC, P], F32R)
        qT = at.sb("qT", [BOT, P])
        rqT = at.sb("rqT", [RD, P])
        sc = at.sb("sc", [P, NS])
        rest = at.sb("rest", [P, NS])
        out_of = at.sb("out_of", [P, NS])
        top = at.sb("top", [P, 8])
        lg = at.sb("lg", [P, NS])
        lgm = at.sb("lgm", [P, NS])
        nmx = at.sb("nmx", [P, 1])
        mx = at.sb("mx", [P, 1])
        ex = at.sb("ex", [P, NS])
        exT = at.sb("exT", [P, NS])
        ub = at.sb("ub", [P, UH])
        ug = at.sb("ug", [P, UH])
        st = at.sb("st", [P, 4, 6])
        row = at.sb("row", [P, 4])

        id0, id1, small_in, w_hi, w_lo, rk_in = (at.sem(s) for s in ("id0", "id1", "small_in", "w_hi", "w_lo", "rk_in"))
        w_in = [at.sem(f"w_in{i}") for i in range(2)]
        pre_in, pre_mm, pre_out = at.sem("pre_in"), at.sem("pre_mm"), at.sem("pre_out")
        y_in = [at.sem(f"y_in{i}") for i in range(2)]
        z_mm, z_out = at.sem("z_mm"), at.sem("z_out")
        t_mm, z_hi, z_lo = at.sem("t_mm"), at.sem("z_hi"), at.sem("z_lo")
        u_mm, u_add, u_act, u_sum = (at.sem(s) for s in ("u_mm", "u_add", "u_act", "u_sum"))
        q_out, rq_mm, rq_out, s_mm, a_mm = (at.sem(s) for s in ("q_out", "rq_mm", "rq_out", "s_mm", "a_mm"))
        step = at.sem("step")
        e_out, e_mm, e_cp, tt_mm, tt_out = (at.sem(s) for s in ("e_out", "e_mm", "e_cp", "tt_mm", "tt_out"))
        wr0 = at.sem("wr0")
        kept = at.sem("kept")
        yz_out, bn, stats = at.sem("yz_out"), at.sem("bn"), at.sem("stats")
        yz_st = [at.sem(f"yz_st{i}") for i in range(2)]
        block = ctx.enter_context(nc.Block())

        avT = (yb[0], yb[1], z[0], z[1])
        wvdT = yz[0]

        @block.sync
        def _(sp):
            sp.wait_ge(wr0, 1)
            small = [(keysT[:, :], a["keysT"]), (wrT[:, 0:RD], a["wrT"]),
                     (lrel[:, :], a["log_rel"].to_broadcast([P, NS])),
                     (bu1[:, :], a["bu1"].to_broadcast([P, UH])),
                     (wu2[:, :], a["wu2"].to_broadcast([P, UH]))]
            for dst, src in small:
                sp.dma_start(dst, src).then_inc(small_in, 16)
            for i in range(4):
                sp.dma_start(avT[i][:, :].rearrange("p (k n) -> p k n", n=NS),
                             a["avT"][4 * i * P:4 * (i + 1) * P, :].rearrange("(k p) n -> p k n", p=P)).then_inc(pre_in, 16)
            sp.dma_start(wvdT[:, :].rearrange("p (k v) -> p k v", v=VB),
                         a["wvdT"].rearrange("(k p) v -> p k v", p=P)).then_inc(pre_in, 16)
            for t in range(KC // 2):
                if t >= 2:
                    sp.wait_ge(w_lo, t - 1)
                sp.dma_start(wst[t % 2][:, :, :], a["wuq"][2 * t * P:2 * (t + 1) * P, :]
                             .rearrange("(k p) n -> p k n", p=P)).then_inc(w_in[t % 2], 16)
            sp.wait_ge(pre_mm, 5)

            def load(n, u):
                sp.dma_start(yb[u][:, :], scr["y"][n]).then_inc(y_in[u], 16)
                sp.dma_start(ag[u][:, :], scr["agg"][n].rearrange("(i o) -> i o", o=C)).then_inc(y_in[u], 16)
                sp.dma_start(zb[u][:, :], scr["aggb"][n].unsqueeze(1)).then_inc(y_in[u], 16)

            load(0, 0)
            load(1, 1)
            with sp.Fori(1, N // 2) as i:
                for u in range(2):
                    sp.wait_ge(z_mm, 4 * (2 * i + u - 1))
                    sp.wait_ge(yz_out, 2 * i + u - 1)
                    sp.wait_ge(z_out, 4 * (2 * i + u - 1))
                    load(2 * i + u, u)
            for i in range(2):
                sp.wait_ge(yz_st[i], 16 * N // 2)

        @block.gpsimd
        def _(pool):
            pool.memset(ident[:, :], 0.0).then_inc(id0, 1)
            pool.wait_ge(id0, 1)
            pool.affine_select(out=ident[:, :], in_=ident[:, :], compare_op=ALU.not_equal, fill=1.0,
                               base=0, pattern=[[-1, P]], channel_multiplier=1).then_inc(id1, 1)
            def sum_yz(n, i, u, first=False):
                pool.wait_ge(z_out, 4 * (n + 1))
                if not first:
                    pool.wait_ge(yz_st[u], 16 * i)
                pool.tensor_tensor(yz[u][:, :], z[u][:, :], yb[u][:, :], ALU.add).then_inc(yz_out, 1)
                pool.wait_ge(yz_out, n + 1)
                pool.dma_start(scr["yz"][n], yz[u][:, :]).then_inc(yz_st[u], 16)

            sum_yz(0, 0, 0, True)
            sum_yz(1, 0, 1, True)
            with pool.Fori(1, N // 2) as i:
                for u in range(2):
                    sum_yz(2 * i + u, i, u)

        @block.tensor
        def _(pe):
            pe.wait_ge(pre_in, 80)
            for c in range(NS // P):
                for k in range(KC):
                    mm = pe.matmul(ps[0][:, c * VB:(c + 1) * VB],
                                   avT[k // 4][:, (k % 4) * NS + c * P:(k % 4) * NS + (c + 1) * P],
                                   wvdT[:, k * VB:(k + 1) * VB], start=(k == 0), stop=(k == KC - 1))
                mm.then_inc(pre_mm, 1)
            pe.wait_ge(small_in, 16 * 5)
            pe.matmul(ps[1][0:RD, 0:NS], wrT[:, 0:RD], keysT[:, :], start=True, stop=True).then_inc(pre_mm, 1)
            pe.wait_ge(pre_out, 2)
            pe.wait_ge(id1, 1)

            def z_of(n, i, u):
                pe.wait_ge(y_in[u], 48 * (i + 1))
                for h in range(4):
                    if h >= 2:
                        pe.wait_ge(z_out, 4 * n + h - 1)
                    pe.matmul(z_ps[h % 2][:, :], ag[u][:, :], yb[u][:, h * BANK:(h + 1) * BANK],
                              start=True, stop=True).then_inc(z_mm, 1)

            def turn(n, u, j, first):
                pe.wait_ge(z_out, 4 * n + j + 1)
                if not (first and j < 2):
                    pe.wait_ge(z_lo, 4 * n + j - 1)
                for k in range(4):
                    mm = pe.transpose(t_ps[j % 2][:, k * P:(k + 1) * P],
                                      z[u][:, (4 * j + k) * P:(4 * j + k + 1) * P], ident[:, :])
                mm.then_inc(t_mm, 1)

            def heads(n, j, first):
                if j == 0 and not first:
                    pe.wait_ge(u_add, n)
                    pe.wait_ge(rq_out, n)
                pe.wait_ge(z_lo, 4 * n + j + 1)
                for k in range(T4 * j, T4 * (j + 1)):
                    for lhs, parts in ((zh, (wh, wl)), (zl, (wh,))):
                        for w in parts:
                            edge = dict(start=(k == 0 and lhs is zh and w is wh),
                                        stop=(k == KC - 1 and lhs is zl))
                            pe.matmul(u_ps[:, :], lhs[:, k, :], w[:, k, 0:UH], **edge)
                            mm = pe.matmul(m_ps[0:BOT, Q], w[:, k, UH:UH + BOT], lhs[:, k, :], **edge)
                mm.then_inc(u_mm, 1)

            def router_query(n):
                pe.wait_ge(q_out, n + 1)
                pe.matmul(m_ps[:, RQ], wrT[:, :], qT[:, :], start=True, stop=True).then_inc(rq_mm, 1)

            def scores(n, first):
                if not first:
                    pe.wait_ge(tt_out, n)
                    pe.wait_ge(e_cp, n)
                pe.matmul(a_ps[:, :], qT[:, :], keysT[:, :], start=True, stop=True).then_inc(a_mm, 1)
                pe.wait_ge(rq_out, n + 1)
                pe.matmul(s_ps[:, :], rqT[:, :], rkT[:, :], start=True, stop=True).then_inc(s_mm, 1)

            def turn_e(n):
                pe.wait_ge(step, STEPS * n + 2)
                pe.wait_ge(e_out, n + 2)
                for k in range(4):
                    mm = pe.transpose(s_ps[:, k * P:(k + 1) * P], ex[:, k * P:(k + 1) * P], ident[:, :])
                mm.then_inc(e_mm, 1)

            def read(n):
                pe.wait_ge(step, STEPS * n + 1)
                pe.wait_ge(e_cp, n + 1)
                for k in range(4):
                    mm = pe.matmul(a_ps[:, 0:P], vp[:, k, :], exT[:, k * P:(k + 1) * P], start=(k == 0), stop=(k == 3))
                mm.then_inc(tt_mm, 1)

            def sample(n, u, i, w, first=False, last=False):
                turn(n, u, 0, first)
                turn(n, u, 1, first)
                heads(n, 0, first)
                turn(n, u, 2, first)
                heads(n, 1, first)
                turn(n, u, 3, first)
                if not first:
                    turn_e(n - 1)
                heads(n, 2, first)
                if not first:
                    read(n - 1)
                heads(n, 3, first)
                router_query(n)
                if not last:
                    z_of(n + 1, i, w)
                scores(n, first)

            pe.wait_ge(w_lo, KC // 2)
            z_of(0, 0, 0)
            sample(0, 0, 0, 1, first=True)
            with pe.Fori(1, N // 2) as i:
                sample(2 * i - 1, 1, i, 0)
                sample(2 * i, 0, i, 1)
            sample(N - 1, 1, 0, 0, last=True)
            turn_e(N - 1)
            read(N - 1)

        @block.scalar
        def _(act):
            for t in range(KC // 2):
                act.wait_ge(w_in[t % 2], 16 * (t // 2 + 1))
                act.activation(wh[:, 2 * t:2 * t + 2, :], wst[t % 2][:, :, :], ACT.Copy).then_inc(w_hi, 1)

            act.sem_inc(e_out, 1)

            def z_copy(n, u, first=False):
                if not first:
                    act.wait_ge(stats, n - 1)
                    act.wait_ge(yz_out, n - 1)
                    act.wait_ge(t_mm, 4 * (n - 1))
                for h in range(4):
                    act.wait_ge(z_mm, 4 * n + h + 1)
                    act.activation(z[u][:, h * BANK:(h + 1) * BANK], z_ps[h % 2][:, :], ACT.Identity,
                                   bias=zb[u][:, 0:1]).then_inc(z_out, 1)

            def high(n, j, first):
                act.wait_ge(t_mm, 4 * n + j + 1)
                if not first:
                    act.wait_ge(u_mm, 4 * (n - 1) + j + 1)
                act.activation(zh[:, T4 * j:T4 * (j + 1), :],
                               t_ps[j % 2][:, :].rearrange("p (k c) -> p k c", c=P), ACT.Copy).then_inc(z_hi, 1)

            def numerators(n):
                act.wait_ge(step, STEPS * (n + 1))
                act.wait_ge(kept, 3 * (n + 1))
                act.activation(ex[:, :], lgm[:, :], ACT.Exp, bias=nmx[:, 0:1],
                               accum_out=row[:, 3:4]).then_inc(e_out, 1)

            def copy_e(n):
                act.wait_ge(e_mm, n + 1)
                act.activation(exT[:, :], s_ps[:, :], ACT.Copy).then_inc(e_cp, 1)

            def sample(n, w, first=False, last=False):
                for j in range(3):
                    high(n, j, first)
                if not first:
                    numerators(n - 1)
                high(n, 3, first)
                if not first:
                    copy_e(n - 1)
                    act.wait_ge(s_mm, n)
                act.wait_ge(u_mm, 4 * (n + 1))
                act.activation(qT[:, :], m_ps[0:BOT, Q], ACT.Copy).then_inc(q_out, 1)
                act.wait_ge(rq_mm, n + 1)
                act.activation(rqT[:, :], m_ps[0:RD, RQ], ACT.Copy).then_inc(rq_out, 1)
                if not last:
                    z_copy(n + 1, w, first)
                act.wait_ge(u_add, n + 1)
                if not first:
                    act.wait_ge(u_sum, n)
                act.activation(ug[:, :], ub[:, :], ACT.Gelu_apprx_tanh).then_inc(u_act, 1)

            z_copy(0, 0, first=True)
            sample(0, 1, first=True)
            with act.Fori(1, N // 2) as i:
                sample(2 * i - 1, 0)
                sample(2 * i, 1)
            sample(N - 1, 0, last=True)
            numerators(N - 1)
            copy_e(N - 1)

        @block.vector
        def _(dve):
            dve.memset(wrT[:, :], 0.0).then_inc(wr0, 1)
            for t in range(KC // 2):
                dve.wait_ge(w_hi, t + 1)
                dve.tensor_tensor(wl[:, 2 * t:2 * t + 2, :], wst[t % 2][:, :, :], wh[:, 2 * t:2 * t + 2, :].bitcast(F32),
                                  ALU.subtract).then_inc(w_lo, 1)
            dve.wait_ge(pre_mm, 4)
            dve.tensor_copy(vp[:, :, :], ps[0][:, :].rearrange("p (c v) -> p c v", v=VB)).then_inc(pre_out, 1)
            dve.wait_ge(pre_mm, 5)
            dve.tensor_copy(rkT[:, :], ps[1][0:RD, 0:NS]).then_inc(pre_out, 1)

            dve.sem_inc(kept, 3)

            def low(n, j):
                dve.wait_ge(z_hi, 4 * n + j + 1)
                s = slice(T4 * j, T4 * (j + 1))
                dve.tensor_tensor(zl[:, s, :], t_ps[j % 2][:, :].rearrange("p (k c) -> p k c", c=P),
                                  zh[:, s, :].bitcast(F32), ALU.subtract).then_inc(z_lo, 1)

            def choose(n):
                done = STEPS * n
                dve.wait_ge(a_mm, n + 1)
                dve.scalar_tensor_tensor(out=lg[:, :], in0=a_ps[:, :], scalar=float(BOT) ** -0.5, in1=lrel[:, :],
                                         op0=ALU.mult, op1=ALU.add).then_inc(step, 1)
                dve.wait_ge(s_mm, n + 1)
                dve.scalar_tensor_tensor(out=sc[:, :], in0=s_ps[:, :], scalar=float(RD) ** -0.5, in1=lrel[:, :],
                                         op0=ALU.mult, op1=ALU.add).then_inc(step, 1)
                dve.wait_ge(step, done + 2)
                dve.wait_ge(u_act, n + 1)
                dve.wait_ge(kept, 3 * (n + 1))
                dve.tensor_tensor_reduce(ug[:, :], ug[:, :], wu2[:, :], 1.0, 0.0, ALU.mult, ALU.add,
                                         row[:, 2:3]).then_inc(u_sum, 1)
                dve.max(top[:, :], sc[:, :]).then_inc(step, 1)
                dve.wait_ge(step, done + 3)
                dve.wait_ge(u_sum, n + 1)
                dve.tensor_scalar(learned[:, bass.ds(n, 1)], row[:, 2:3], 1.0, None, ALU.mult).then_inc(kept, 1)
                dve.match_replace(rest[:, :], top[:, :], sc[:, :], FAR).then_inc(step, 1)
                dve.wait_ge(step, done + 4)
                dve.tensor_tensor(out_of[:, :], rest[:, :], sc[:, :], ALU.is_equal).then_inc(step, 1)
                dve.wait_ge(step, done + 5)
                dve.wait_ge(e_out, n + 1)
                dve.scalar_tensor_tensor(out=lgm[:, :], in0=out_of[:, :], scalar=FAR, in1=lg[:, :],
                                         op0=ALU.mult, op1=ALU.add).then_inc(step, 1)
                dve.wait_ge(step, done + 6)
                dve.tensor_reduce(mx[:, :], lgm[:, :], AX_X, ALU.max).then_inc(step, 1)
                dve.wait_ge(step, done + 7)
                dve.tensor_scalar(nmx[:, :], mx[:, :], -1.0, None, ALU.mult).then_inc(step, 1)

            def keep_read(n):
                dve.wait_ge(e_out, n + 2)
                dve.tensor_scalar(esum[:, bass.ds(n, 1)], row[:, 3:4], 1.0, None, ALU.mult).then_inc(kept, 1)
                dve.wait_ge(tt_mm, n + 1)
                dve.tensor_scalar(tT[:, n, :], a_ps[:, 0:P], 1.0, None, ALU.mult).then_inc(tt_out, 1)

            def sample(n, u, first=False):
                low(n, 0)
                low(n, 1)
                if not first:
                    choose(n - 1)
                low(n, 2)
                low(n, 3)
                dve.wait_ge(stats, n)
                for h in range(4):
                    dve.bn_stats(st[:, h, :], z[u][:, h * BANK:(h + 1) * BANK]).then_inc(bn, 1)
                if not first:
                    keep_read(n - 1)
                dve.wait_ge(u_mm, 4 * (n + 1))
                if not first:
                    dve.wait_ge(u_act, n)
                dve.wait_ge(bn, 4 * (n + 1))
                dve.tensor_tensor(ub[:, :], u_ps[:, :], bu1[:, :], ALU.add).then_inc(u_add, 1)
                dve.bn_aggr(row[:, 0:2], st[:, :, :].rearrange("p h s -> p (h s)")).then_inc(stats, 1)
                dve.wait_ge(stats, n + 1)
                dve.tensor_scalar(var_all[:, bass.ds(n, 1)], row[:, 1:2], 1.0, None, ALU.mult).then_inc(kept, 1)

            sample(0, 0, first=True)
            with dve.Fori(1, N // 2) as i:
                sample(2 * i - 1, 1)
                sample(2 * i, 0)
            sample(N - 1, 1)
            choose(N - 1)
            keep_read(N - 1)


def finish(nc, ps, a, scr, keep, out):
    tT, var_all, learned, esum = keep
    with ExitStack() as ctx:
        at = Places(nc, ctx, "fin")
        wst = at.sb("wst", [P, L])
        wh = at.sb("wh", [P, L], F32R)
        wl = at.sb("wl", [P, L], F32R)
        sc2 = at.sb("sc2", [P, 3])
        logv = at.sb("logv", [P, N])
        lsum = at.sb("lsum", [P, 1])
        total = at.sb("total", [P, 1])
        rmean = at.sb("rmean", [P, 1])
        sig = at.sb("sig", [P, N])
        g = [at.sb(f"g{i}", [P, N]) for i in range(2)]
        u_norm = at.sb("u_norm", [P, N])
        gate = at.sb("gate", [P, N])
        res = at.sb("res", [P, N])
        th = [at.sb(f"th{i}", [P, P], F32R) for i in range(2)]
        tl = [at.sb(f"tl{i}", [P, P], F32R) for i in range(2)]
        yz = [at.sb(f"yz{i}", [P, L]) for i in range(4)]

        small_in, w_in, w_hi, w_lo = (at.sem(s) for s in ("small_in", "w_in", "w_hi", "w_lo"))
        log_ok, tot_ok, sig_ok, chain, gate_ok = (at.sem(s) for s in ("log_ok", "tot_ok", "sig_ok", "chain", "gate_ok"))
        yz_in = [at.sem(f"yz_in{i}") for i in range(4)]
        t_hi, t_lo, mm_ok, add_ok = (at.sem(s) for s in ("t_hi", "t_lo", "mm_ok", "add_ok"))
        o_st = [at.sem(f"o_st{i}") for i in range(4)]
        block = ctx.enter_context(nc.Block())

        @block.sync
        def _(sp):
            for k, name in enumerate(("bu2", "gate_w1", "gate_bias")):
                sp.dma_start(sc2[:, k:k + 1], a[name].to_broadcast([P, 1])).then_inc(small_in, 16)
            sp.dma_start(wst[:, :], a["wvuT"]).then_inc(w_in, 16)
            with sp.Fori(0, N // 4) as i:
                for u in range(4):
                    sp.wait_ge(o_st[u], 16 * (i + 1))
                    sp.dma_start(yz[u][:, :], scr["yz"][4 * i + u]).then_inc(yz_in[u], 16)

        @block.gpsimd
        def _(pool):
            pool.wait_ge(log_ok, 1)
            pool.partition_all_reduce(total[:, :], lsum[:, :], P, bass.bass_isa.ReduceOp.add).then_inc(tot_ok, 1)

        @block.scalar
        def _(act):
            for u in range(4):
                act.sem_inc(o_st[u], 16)
            act.activation(logv[:, :], var_all[:, :], ACT.Ln, bias=1.0, accum_out=lsum[:, :]).then_inc(log_ok, 1)
            act.wait_ge(w_in, 16)
            act.activation(wh[:, :], wst[:, :], ACT.Copy).then_inc(w_hi, 1)
            act.wait_ge(small_in, 48)
            act.activation(sig[:, :], learned[:, :], ACT.Sigmoid, bias=sc2[:, 0:1]).then_inc(sig_ok, 1)
            act.wait_ge(chain, 7)
            act.activation(gate[:, :], u_norm[:, :], ACT.Sigmoid, scale=sc2[:, 1:2], bias=sc2[:, 2:3]).then_inc(gate_ok, 1)
            with act.Fori(0, N // 4) as i:
                for u in range(4):
                    n = 4 * i + u
                    act.wait_ge(add_ok, 2 + n + 1)
                    act.dma_start(out[n], yz[u][:, :]).then_inc(o_st[u], 16)
            for u in range(4):
                act.wait_ge(o_st[u], 16 + 16 * N // 4)

        @block.tensor
        def _(pe):
            pe.wait_ge(w_lo, 1)
            pe.wait_ge(chain, 10)
            with pe.Fori(0, N // 4) as i:
                for u in range(4):
                    n = 4 * i + u
                    pe.wait_ge(t_lo, n + 1)
                    pe.wait_ge(add_ok, n + 1)
                    for h in range(4):
                        s = slice(h * BANK, (h + 1) * BANK)
                        for k, (lhs, w) in enumerate(((th, wh), (th, wl), (tl, wh))):
                            mm = pe.matmul(ps[4 * (u % 2) + h][:, :], lhs[u % 2][:, :], w[:, s],
                                           start=(k == 0), stop=(k == 2))
                    mm.then_inc(mm_ok, 1)

        @block.vector
        def _(dve):
            dve.wait_ge(w_hi, 1)
            dve.tensor_tensor(wl[:, :], wst[:, :], wh[:, :].bitcast(F32), ALU.subtract).then_inc(w_lo, 1)

            def link(k, ins):
                ins.then_inc(chain, 1)
                dve.wait_ge(chain, k)

            dve.wait_ge(tot_ok, 1)
            link(1, dve.tensor_scalar(total[:, :], total[:, :], 1.0 / (N * C), 1e-6, ALU.mult, ALU.add))
            link(2, dve.reciprocal(rmean[:, :], total[:, :]))
            link(3, dve.tensor_scalar(g[0][:, :], logv[:, :], rmean[:, 0:1], 0.5, ALU.mult, ALU.mult))
            dve.wait_ge(sig_ok, 1)
            link(4, dve.scalar_tensor_tensor(out=g[1][:, :], in0=sig[:, :], scalar=2.5, in1=g[0][:, :],
                                             op0=ALU.mult, op1=ALU.add))
            link(5, dve.tensor_scalar(g[0][:, :], g[1][:, :], 0.0, 5.0, ALU.max, ALU.min))
            link(6, dve.tensor_scalar(g[1][:, :], g[0][:, :], TAU_LOW, 1.0 / (TAU_HIGH - TAU_LOW),
                                      ALU.subtract, ALU.mult))
            link(7, dve.tensor_scalar(u_norm[:, :], g[1][:, :], 0.0, 1.0, ALU.max, ALU.min))
            link(8, dve.reciprocal(res[:, :], esum[:, :]))
            dve.wait_ge(gate_ok, 1)
            link(9, dve.scalar_tensor_tensor(out=g[0][:, :], in0=gate[:, :], scalar=EARLY_EXIT, in1=gate[:, :],
                                              op0=ALU.is_ge, op1=ALU.mult))
            link(10, dve.tensor_tensor(g[1][:, :], g[0][:, :], res[:, :], ALU.mult))

            dve.sem_inc(add_ok, 2)

            def split(n, u):
                dve.tensor_scalar(th[u % 2][:, :], tT[:, n, :], 1.0, None, ALU.mult).then_inc(t_hi, 1)
                dve.wait_ge(t_hi, n + 1)
                dve.tensor_tensor(tl[u % 2][:, :], tT[:, n, :], th[u % 2][:, :].bitcast(F32),
                                  ALU.subtract).then_inc(t_lo, 1)

            with dve.Fori(0, N // 4) as i:
                for u in range(4):
                    n = 4 * i + u
                    split(n, u)
                    dve.wait_ge(yz_in[u], 16 * (i + 1))
                    dve.wait_ge(mm_ok, n + 1)
                    for h in range(4):
                        s = slice(h * BANK, (h + 1) * BANK)
                        add = dve.scalar_tensor_tensor(out=yz[u][:, s], in0=ps[4 * (u % 2) + h][:, :],
                                                       scalar=g[1][:, bass.ds(n, 1)], in1=yz[u][:, s],
                                                       op0=ALU.mult, op1=ALU.add)
                    add.then_inc(add_ok, 1)


def program(nc, a, out):
    def dram(name, shape):
        return nc.dram_tensor(name, shape, F32, kind="Internal").ap()

    scr = {
        "crow": dram("scr_crow", (N, C)), "aggb": dram("scr_aggb", (N, C)),
        "agg": dram("scr_agg", (N, C * C)), "la": dram("scr_la", (B, P, KC, 2 * R)),
        "lb": dram("scr_lb", (B, R, L)), "ct": dram("scr_ct", (N, P, KC * C)),
        "ax": dram("scr_ax", (N, 2 * R, P)), "y": dram("scr_y", (N, C, L)), "yz": dram("scr_yz", (N, C, L)),
    }
    with ExitStack() as ctx:
        ps = [ctx.enter_context(nc.psum_tensor(f"bank{i}", [P, BANK], F32)) for i in range(8)]
        prologue(nc, ps, a, scr)
        convolve(nc, ps, a, scr)
        for half in range(2):
            project(nc, ps, a, scr, half)
        keep = [ctx.enter_context(nc.sbuf_tensor(name, shape, F32)) for name, shape in
                (("tT", [P, N, P]), ("var_all", [P, N]), ("learned", [P, N]), ("esum", [P, N]))]
        attend(nc, ps, a, scr, keep)
        finish(nc, ps, a, scr, keep, out)


def kernel(**inputs):
    import numpy as np
    import concourse.bacc as bacc
    from concourse.bass_utils import run_bass_kernel_spmd

    x = np.asarray(inputs["x"])
    v = {k: np.asarray(w) for k, w in inputs.items()}
    laid = {
        "x": x,
        "xph": x.reshape(N, GROUPS, GC, M, PH).transpose(0, 4, 2, 1, 3).reshape(N, P, GROUPS * M),
        "taps": v["L0_cond_weight"].reshape(GROUPS, GC, GC, TAPS).transpose(3, 2, 0, 1),
        "condT": v["cond_128"].T,
        "cwT": v["L0_cond_c_weight"].T,
        "conv_bias": v["fside_S_0"].reshape(1, C),
        "gateT": v["L0_ffn_gate"].T,
        "kernel": v["L0_ffn_kernel"],
        "ffn_bias": v["L0_ffn_bias"].reshape(1, L),
        "loraA": v["L0_ffn_lora_A"].reshape(NL * R, L),
        "loraB": v["L0_ffn_lora_B"].transpose(0, 2, 1).reshape(NL * R, L),
        "laS": v["L0_ffn_lora_A_shared"].T,
        "lbS": v["L0_ffn_lora_B_shared"].T,
        "W0": v["L1_cond_W0"], "W1": v["L1_cond_W1"], "W2": v["L1_cond_W2"],
        "b0": v["L1_cond_b0"], "b1": v["L1_cond_b1"], "b2": v["L1_cond_b2"].reshape(1, NE),
        "wk": v["L1_cond_weight"][..., 0].transpose(0, 2, 1).reshape(NE, C * C),
        "bias_k": v["L1_cond_bias_k"],
        "wuq": np.concatenate([v["L1_ffn_Wu1"].T, v["L1_ffn_Wq"].T], axis=1),
        "wrT": v["L1_ffn_Wr"].T,
        "keysT": v["L1_ffn_aux_keys"].T,
        "avT": v["L1_ffn_aux_values"].T,
        "wvdT": v["L1_ffn_Wvd"].T,
        "wvuT": v["L1_ffn_Wvu"].T,
        "log_rel": v["L1_ffn_log_rel"].reshape(1, NS),
        "bu1": v["L1_ffn_bu1"].reshape(1, UH),
        "wu2": v["L1_ffn_Wu2"].reshape(1, UH),
        "bu2": v["L1_ffn_bu2"].reshape(1, 1),
        "gate_w1": v["L1_ffn_gate_w1"].reshape(1, 1),
        "gate_bias": v["L1_ffn_gate_bias"].reshape(1, 1),
    }
    nc = bacc.Bacc("TRN2", target_bir_lowering=False, num_devices=1)
    arrays, a = {}, {}
    for name, w in laid.items():
        w = np.ascontiguousarray(w)
        arrays[f"in_{name}"] = w
        a[name] = nc.dram_tensor(f"in_{name}", w.shape, mybir.dt.from_np(w.dtype), kind="ExternalInput").ap()
    out = nc.dram_tensor("out", (N, C, L), F32, kind="ExternalOutput").ap()
    program(nc, a, out)
    r = run_bass_kernel_spmd(nc, [arrays], core_ids=[0])
    return r.results[0]["out"]
```

```python
from contextlib import ExitStack

import concourse.bass as bass
from concourse import mybir

P = 128
N, C, L = 32, 128, 2048
TAPS, PAD, GROUPS = 9, 4, 4
GC = C // GROUPS
PH = P // GC
M = L // PH
MC = M // P
KC = L // P
B, SPB = 8, N // 8
NL, R = 16, 32
NJ = NL * R // P
HALF = L // 2
NE = 8
BOT, RD, NS, VB, UH = 64, 48, 512, 128, 512
TAU_LOW, TAU_HIGH, EARLY_EXIT = 0.5, 2.0, 0.05
STEPS = 8
GSTEPS, GHALF = 10, 6
FAR = -3.0e38
BANK = 512

F32 = mybir.dt.float32
F32R = mybir.dt.float32r
ALU = mybir.AluOpType
ACT = mybir.ActivationFunctionType
AX_X = mybir.AxisListType.X


class Places:

    def __init__(self, nc, ctx, stage):
        self.nc, self.ctx, self.stage = nc, ctx, stage

    def sb(self, name, shape, dt=F32):
        return self.ctx.enter_context(self.nc.sbuf_tensor(f"{self.stage}_{name}", shape, dt))

    def sem(self, name):
        return self.ctx.enter_context(self.nc.semaphore(f"{self.stage}_{name}"))


def prologue(nc, ps, a, scr):
    with ExitStack() as ctx:
        at = Places(nc, ctx, "pro")
        ident = at.sb("ident", [P, P])
        mask = at.sb("mask", [P, R])
        gcol = at.sb("gcol", [P, NJ, B])
        G = at.sb("G", [P, NJ, B * R])
        condT = at.sb("condT", [P, N])
        cwT = at.sb("cwT", [P, C])
        bias_bc = at.sb("bias_bc", [N, C])
        crow = at.sb("crow", [N, C])
        W0 = at.sb("W0", [P, P])
        W1 = at.sb("W1", [P, P])
        W2 = at.sb("W2", [P, NE])
        b0 = at.sb("b0", [P, 1])
        b1 = at.sb("b1", [P, 1])
        b2_bc = at.sb("b2_bc", [N, NE])
        bias_k = at.sb("bias_k", [NE, C])
        h1 = at.sb("h1", [P, N])
        h2 = at.sb("h2", [P, N])
        lg = at.sb("lg", [N, NE])
        mx = at.sb("mx", [N, 1])
        nmx = at.sb("nmx", [N, 1])
        ex = at.sb("ex", [N, NE])
        sm = at.sb("sm", [N, 1])
        rs = at.sb("rs", [N, 1])
        att = at.sb("att", [N, NE])
        attT = at.sb("attT", [NE, N])
        aggb = at.sb("aggb", [N, C])
        wk = at.sb("wk", [NE, C * C])
        aggst = at.sb("aggst", [N, 2, 4 * BANK])
        loraA = at.sb("loraA", [P, NJ, L])
        loraB = at.sb("loraB", [P, NJ, L])
        ash = at.sb("ash", [P, KC, R])
        aout = at.sb("aout", [P, KC, B, 2 * R])
        bout = at.sb("bout", [P, 2, L // 2])

        small_in, gate_in, la_in, lb_in, wk_in, ash_in = (
            at.sem(s) for s in ("small_in", "gate_in", "la_in", "lb_in", "wk_in", "ash_in"))
        id0, id1, mask_ok, G_ok = (at.sem(s) for s in ("id0", "id1", "mask_ok", "G_ok"))
        mlp_mm, mlp_act, soft, soft_act, crow_mm, crow_ok = (
            at.sem(s) for s in ("mlp_mm", "mlp_act", "soft", "soft_act", "crow_mm", "crow_ok"))
        fa_mm, fa_ok, shared_ok, fb_mm, fb_ok, ag_mm, ag_ok = (
            at.sem(s) for s in ("fa_mm", "fa_ok", "shared_ok", "fb_mm", "fb_ok", "ag_mm", "ag_ok"))
        stored = at.sem("stored")
        bst = [at.sem(f"bst{i}") for i in range(2)]
        gst = [at.sem(f"gst{i}") for i in range(2)]
        block = ctx.enter_context(nc.Block())

        @block.sync
        def _(sp):
            small = [(condT[:, :], a["condT"]), (cwT[:, :], a["cwT"]),
                     (bias_bc[:, :], a["conv_bias"].to_broadcast([N, C])),
                     (W0[:, :], a["W0"]), (W1[:, :], a["W1"]), (W2[:, :], a["W2"]),
                     (b0[:, :], a["b0"].unsqueeze(1)), (b1[:, :], a["b1"].unsqueeze(1)),
                     (b2_bc[:, :], a["b2"].to_broadcast([N, NE])),
                     (bias_k[:, :], a["bias_k"])]
            for dst, src in small:
                sp.dma_start(dst, src).then_inc(small_in, 16)
            sp.dma_start(loraA[:, :, :], a["loraA"].rearrange("(j p) l -> p j l", p=P)).then_inc(la_in, 16)
            sp.dma_start(wk[:, :], a["wk"]).then_inc(wk_in, 16)
            sp.dma_start(loraB[:, :, :], a["loraB"].rearrange("(j p) l -> p j l", p=P)).then_inc(lb_in, 16)
            sp.wait_ge(crow_ok, 1)
            sp.dma_start(scr["crow"], crow[:, :]).then_inc(stored, 16)
            sp.wait_ge(fa_ok, KC)
            sp.wait_ge(shared_ok, B)
            for b in range(B):
                sp.dma_start(scr["la"][b], aout[:, :, b, :]).then_inc(stored, 16)
            lb = scr["lb"].rearrange("b r l -> (b r) l")
            for t in range(4):
                sp.wait_ge(fb_ok, 2 * (t + 1))
                sp.dma_start(lb[(t // 2) * P:(t // 2 + 1) * P, (t % 2) * (L // 2):(t % 2 + 1) * (L // 2)],
                             bout[:, t % 2, :]).then_inc(bst[t % 2], 16)
            sp.wait_ge(soft, 9)
            sp.dma_start(scr["aggb"], aggb[:, :]).then_inc(stored, 16)
            for t in range(8):
                sp.wait_ge(ag_ok, 4 * (t + 1))
                sp.dma_start(scr["agg"][:, t * 4 * BANK:(t + 1) * 4 * BANK],
                             aggst[:, t % 2, :]).then_inc(gst[t % 2], 16)
            sp.wait_ge(stored, 16 * (B + 2))
            for i in range(2):
                sp.wait_ge(bst[i], 32)
                sp.wait_ge(gst[i], 64)

        @block.gpsimd
        def _(pool):
            pool.memset(ident[:, :], 0.0).then_inc(id0, 1)
            for j in range(NJ):
                for n in range(P // R):
                    k = j * (P // R) + n
                    pool.dma_start(gcol[n * R:(n + 1) * R, j, :],
                                   a["gateT"][k:k + 1, :].to_broadcast([R, B])).then_inc(gate_in, 16)
            pool.dma_start(ash[:, :, :].rearrange("p (c q) r -> p c q r", q=PH),
                           a["laS"].rearrange("(c m q) r -> m c q r", m=P, q=PH)).then_inc(ash_in, 16)
            pool.wait_ge(id0, 1)
            pool.affine_select(out=ident[:, :], in_=ident[:, :], compare_op=ALU.not_equal, fill=1.0,
                               base=0, pattern=[[-1, P]], channel_multiplier=1).then_inc(id1, 1)

        @block.scalar
        def _(act):
            act.wait_ge(mlp_mm, 1)
            act.activation(h1[:, :], ps[0][:, 0:N], ACT.Gelu, bias=b0[:, 0:1]).then_inc(mlp_act, 1)
            act.wait_ge(mlp_mm, 2)
            act.activation(h2[:, :], ps[1][:, 0:N], ACT.Gelu, bias=b1[:, 0:1]).then_inc(mlp_act, 1)
            act.wait_ge(soft, 3)
            act.activation(ex[:, :], lg[:, :], ACT.Exp, bias=nmx[:, 0:1]).then_inc(soft_act, 1)

        @block.tensor
        def _(pe):
            pe.wait_ge(small_in, 160)
            pe.matmul(ps[0][:, 0:N], W0[:, :], condT[:, :], start=True, stop=True).then_inc(mlp_mm, 1)
            pe.matmul(ps[2][0:N, 0:C], condT[:, :], cwT[:, :], start=True, stop=True).then_inc(crow_mm, 1)
            pe.wait_ge(mlp_act, 1)
            pe.matmul(ps[1][:, 0:N], W1[:, :], h1[:, :], start=True, stop=True).then_inc(mlp_mm, 1)
            pe.wait_ge(mlp_act, 2)
            pe.matmul(ps[3][0:N, 0:NE], h2[:, :], W2[:, :], start=True, stop=True).then_inc(mlp_mm, 1)
            pe.wait_ge(G_ok, NJ * B)
            pe.wait_ge(la_in, 16)
            for kc in range(KC):
                if kc >= 2:
                    pe.wait_ge(fa_ok, kc - 1)
                mc, q = divmod(kc, PH)
                for j in range(NJ):
                    lhs = loraA[:, j, :].rearrange("p (c m q) -> p c q m", m=P, q=PH)[:, mc, q, :]
                    mm = pe.matmul(ps[4 + kc % 2][:, 0:B * R], lhs, G[:, j, :], start=(j == 0), stop=(j == NJ - 1))
                mm.then_inc(fa_mm, 1)
            pe.wait_ge(lb_in, 16)
            for t in range(8):
                if t >= 2:
                    pe.wait_ge(fb_ok, t - 1)
                for j in range(NJ):
                    mm = pe.matmul(ps[6 + t % 2][:, :], G[:, j, (t // 4) * P:(t // 4 + 1) * P],
                                   loraB[:, j, (t % 4) * BANK:(t % 4 + 1) * BANK],
                                   start=(j == 0), stop=(j == NJ - 1))
                mm.then_inc(fb_mm, 1)
            pe.wait_ge(soft, 7)
            pe.transpose(ps[0][0:NE, 0:N], att[:, :], ident[0:N, 0:N]).then_inc(mlp_mm, 1)
            pe.wait_ge(soft, 8)
            pe.matmul(ps[1][0:N, 0:C], attT[:, :], bias_k[:, :], start=True, stop=True).then_inc(mlp_mm, 1)
            pe.wait_ge(wk_in, 16)
            for t in range(C * C // BANK):
                if t >= 2:
                    pe.wait_ge(ag_ok, t - 1)
                pe.matmul(ps[2 + t % 2][0:N, :], attT[:, :], wk[:, t * BANK:(t + 1) * BANK],
                          start=True, stop=True).then_inc(ag_mm, 1)

        @block.vector
        def _(dve):
            dve.wait_ge(id1, 1)
            dve.tensor_reduce(mask[:, :], ident[:, :].rearrange("p (n r) -> p r n", r=R), AX_X,
                              ALU.add).then_inc(mask_ok, 1)
            dve.wait_ge(mask_ok, 1)
            dve.wait_ge(gate_in, 16 * NL)
            for j in range(NJ):
                for b in range(B):
                    dve.tensor_scalar(G[:, j, b * R:(b + 1) * R], mask[:, :], gcol[:, j, b:b + 1], None,
                                      ALU.mult).then_inc(G_ok, 1)
            dve.wait_ge(crow_mm, 1)
            dve.tensor_tensor(crow[:, :], ps[2][0:N, 0:C], bias_bc[:, :], ALU.add).then_inc(crow_ok, 1)
            dve.wait_ge(mlp_mm, 3)
            dve.tensor_tensor(lg[:, :], ps[3][0:N, 0:NE], b2_bc[:, :], ALU.add).then_inc(soft, 1)
            dve.wait_ge(soft, 1)
            dve.tensor_reduce(mx[:, :], lg[:, :], AX_X, ALU.max).then_inc(soft, 1)
            dve.wait_ge(soft, 2)
            dve.tensor_scalar(nmx[:, :], mx[:, :], -1.0, None, ALU.mult).then_inc(soft, 1)
            dve.wait_ge(soft_act, 1)
            dve.tensor_reduce(sm[:, :], ex[:, :], AX_X, ALU.add).then_inc(soft, 1)
            dve.wait_ge(soft, 4)
            dve.reciprocal(rs[:, :], sm[:, :]).then_inc(soft, 1)
            dve.wait_ge(soft, 5)
            dve.tensor_scalar(att[:, :], ex[:, :], rs[:, 0:1], None, ALU.mult).then_inc(soft, 2)
            dve.wait_ge(ash_in, 16)
            for b in range(B):
                dve.tensor_copy(aout[:, :, b, R:2 * R], ash[:, :, :]).then_inc(shared_ok, 1)
            for kc in range(KC):
                dve.wait_ge(fa_mm, kc + 1)
                dve.tensor_copy(aout[:, kc, :, 0:R],
                                ps[4 + kc % 2][:, 0:B * R].rearrange("p (b r) -> p b r", r=R)).then_inc(fa_ok, 1)
            for t in range(8):
                dve.wait_ge(fb_mm, t + 1)
                if t >= 4:
                    dve.wait_ge(bst[(t // 2) % 2], 16)
                dve.tensor_copy(bout[:, (t // 2) % 2, (t % 2) * BANK:(t % 2 + 1) * BANK],
                                ps[6 + t % 2][:, :]).then_inc(fb_ok, 1)
            dve.wait_ge(mlp_mm, 4)
            dve.tensor_copy(attT[:, :], ps[0][0:NE, 0:N]).then_inc(soft, 1)
            dve.wait_ge(mlp_mm, 5)
            dve.tensor_copy(aggb[:, :], ps[1][0:N, 0:C]).then_inc(soft, 1)
            for t in range(C * C // BANK):
                dve.wait_ge(ag_mm, t + 1)
                if t // 4 >= 2:
                    dve.wait_ge(gst[(t // 4) % 2], 16 * (t // 8))
                dve.tensor_copy(aggst[:, (t // 4) % 2, (t % 4) * BANK:(t % 4 + 1) * BANK],
                                ps[2 + t % 2][0:N, :]).then_inc(ag_ok, 1)


def kernel_chunks(a, half):
    rows = a["kernel"].rearrange("(c m q) d -> c q m d", m=P, q=PH)
    return rows[:, :, :, half * HALF:(half + 1) * HALF]


def convolve(nc, ps, a, scr, khi, klo):
    BODY = 2 * SPB
    AHEAD = SPB
    with ExitStack() as ctx:
        at = Places(nc, ctx, "conv")
        taps = at.sb("taps", [P, 3, GROUPS, PH * GC])
        xb = [at.sb(f"xb{i}", [P, GROUPS, M + 2]) for i in range(2)]
        ct = [at.sb(f"ct{i}", [P, KC, C]) for i in range(2)]
        crow_bc = at.sb("crow_bc", [P, N, C])
        la = [at.sb(f"la{i}", [P, KC, 2 * R]) for i in range(2)]
        axs = [at.sb(f"axs{i}", [2 * R, P]) for i in range(2)]
        kst = [at.sb(f"kst{i}", [P, HALF]) for i in range(2)]

        k_in = [at.sem(f"k_in{i}") for i in range(2)]
        k_hi, k_lo = at.sem("k_hi"), at.sem("k_lo")
        zeroed, taps_in, crow_in = at.sem("zeroed"), at.sem("taps_in"), at.sem("crow_in")
        x_in = [at.sem(f"x_in{i}") for i in range(2)]
        la_in = [at.sem(f"la_in{i}") for i in range(2)]
        conv_mm = at.sem("conv_mm")
        conv_out = at.sem("conv_out")
        ax_mm = at.sem("ax_mm")
        ax_out = at.sem("ax_out")
        ct_st = [at.sem(f"ct_st{i}") for i in range(2)]
        ax_st = [at.sem(f"ax_st{i}") for i in range(2)]
        block = ctx.enter_context(nc.Block())

        @block.sync
        def _(sp):
            sp.wait_ge(zeroed, 3)
            for p in range(PH):
                for q in range(PH):
                    for s in (-1, 0, 1):
                        k = PH * s + p - q + PAD
                        if 0 <= k < TAPS:
                            sp.dma_start(taps[p * GC:(p + 1) * GC, s + 1, :, q * GC:(q + 1) * GC],
                                         a["taps"][k]).then_inc(taps_in, 16)

            def load_x(n, u):
                sp.dma_start(xb[u % 2][:, :, 1:M + 1],
                             a["xph"][n].rearrange("p (g m) -> p g m", g=GROUPS)).then_inc(x_in[u % 2], 16)

            load_x(0, 0)
            load_x(1, 1)
            with sp.Fori(1, N // 2) as i:
                for u in range(2):
                    sp.wait_ge(conv_mm, MC * (2 * i + u - 1))
                    load_x(2 * i + u, u)
            for i in range(2):
                sp.wait_ge(ct_st[i], 16 + 16 * N // 2)
                sp.wait_ge(ax_st[i], 16 + 16 * N // 2)

        @block.gpsimd
        def _(pool):
            pool.dma_start(crow_bc[:, :, :], scr["crow"].unsqueeze(0).to_broadcast([P, N, C])).then_inc(crow_in, 16)
            kern = kernel_chunks(a, 0)
            with pool.Fori(0, B // 2) as i:
                for u in range(2):
                    pool.wait_ge(ax_mm, SPB * (2 * i + u - 1) + AHEAD)
                    pool.dma_start(la[u][:, :, :], scr["la"][2 * i + u]).then_inc(la_in[u], 16)
                    for v in range(2):
                        pool.wait_ge(k_lo, PH * i + 2 * u + v + 1)
                        pool.dma_start(kst[v][:, :], kern[i, 2 * u + v]).then_inc(k_in[v], 16)

        @block.tensor
        def _(pe):
            pe.sem_inc(ax_mm, AHEAD)
            pe.wait_ge(taps_in, 16 * TAPS * PH)
            with pe.Fori(0, N // BODY) as i:
                for u in range(BODY):
                    n = BODY * i + u
                    pe.wait_ge(x_in[u % 2], 16 * (BODY // 2 * i + u // 2 + 1))
                    for mc in range(MC):
                        pe.wait_ge(conv_out, MC * n + mc + 1)
                        for g in range(GROUPS):
                            for s in range(3):
                                mm = pe.matmul(ps[mc][:, g * P:(g + 1) * P],
                                               xb[u % 2][:, g, P * mc + s:P * (mc + 1) + s],
                                               taps[:, s, g, :], start=(s == 0), stop=(s == 2))
                        mm.then_inc(conv_mm, 1)
                    if u % SPB == 0:
                        pe.wait_ge(la_in[u // SPB], 16 * (i + 1))
                    pe.wait_ge(ax_out, n + 1)
                    for kc in range(KC):
                        if kc % PH == 0:
                            pe.wait_ge(conv_out, MC + MC * n + kc // PH + 1)
                        mm = pe.matmul(ps[4 + u % 2][0:2 * R, 0:P], la[u // SPB][:, kc, :], ct[u % 2][:, kc, :],
                                       start=(kc == 0), stop=(kc == KC - 1))
                    mm.then_inc(ax_mm, 1)

        @block.vector
        def _(dve):
            dve.memset(taps[:, :, :, :], 0.0).then_inc(zeroed, 1)
            for i in range(2):
                dve.memset(xb[i][:, :, 0:M + 2:M + 1], 0.0).then_inc(zeroed, 1)
            dve.sem_inc(conv_out, MC)
            dve.wait_ge(crow_in, 16)
            dve.sem_inc(k_lo, 2)
            with dve.Fori(0, N // BODY) as i:
                for u in range(BODY):
                    n = BODY * i + u
                    ctx_row = crow_bc[:, n, :].rearrange("p (g o) -> p g o", g=GROUPS)
                    ctx_row = ctx_row.unsqueeze(2).to_broadcast([P, GROUPS, PH, GC])
                    dve.wait_ge(ax_mm, n - 1 + AHEAD)
                    dve.wait_ge(ct_st[u % 2], 16 * (BODY // 2 * i + u // 2 + 1))
                    for mc in range(MC):
                        dve.wait_ge(conv_mm, MC * n + mc + 1)
                        dst = ct[u % 2][:, PH * mc:PH * (mc + 1), :].rearrange("p q (g o) -> p g q o", g=GROUPS)
                        src = ps[mc][:, :].rearrange("p (g q o) -> p g q o", g=GROUPS, q=PH)
                        dve.tensor_tensor(dst, src, ctx_row, ALU.add).then_inc(conv_out, 1)
                    if u % 2:
                        v = u // 2
                        kc = PH * i + v
                        dve.wait_ge(k_in[v % 2], 16 * (2 * i + v // 2 + 1))
                        dve.tensor_scalar(khi[:, kc, :], kst[v % 2][:, :], 1.0, None, ALU.mult).then_inc(k_hi, 1)
                        dve.wait_ge(k_hi, kc + 1)
                        dve.tensor_tensor(klo[:, kc, :], kst[v % 2][:, :], khi[:, kc, :].bitcast(F32),
                                          ALU.subtract).then_inc(k_lo, 1)

        @block.scalar
        def _(act):
            act.sem_inc(ax_out, 2)
            for i in range(2):
                act.sem_inc(ct_st[i], 16)
                act.sem_inc(ax_st[i], 16)
            with act.Fori(0, N // 2) as i:
                for u in range(2):
                    n = 2 * i + u
                    act.wait_ge(conv_out, MC + MC * (n + 1))
                    act.dma_start(scr["ct"][n], ct[u][:, :, :].rearrange("p k c -> p (k c)")).then_inc(ct_st[u], 16)
                    act.wait_ge(ax_mm, n + 1 + AHEAD)
                    act.wait_ge(ax_st[u], 16 * (i + 1))
                    act.activation(axs[u][:, :], ps[4 + u][0:2 * R, 0:P], ACT.Copy).then_inc(ax_out, 1)
                    act.wait_ge(ax_out, 2 + n + 1)
                    act.dma_start(scr["ax"][n], axs[u][:, :]).then_inc(ax_st[u], 16)


def project(nc, ps, a, scr, khi, klo, st_all):
    KR = 2 * R + 1
    QK = KC // 4
    with ExitStack() as ctx:
        at = Places(nc, ctx, "proj")
        kst = [at.sb(f"kst{i}", [P, HALF]) for i in range(2)]
        craw = [at.sb(f"craw{i}", [P, KC, C]) for i in range(2)]
        chi = at.sb("chi", [P, KC, C], F32R)
        clo = at.sb("clo", [P, KC, C], F32R)
        yo = [at.sb(f"yo{i}", [P, HALF]) for i in range(2)]
        zo = [at.sb(f"zo{i}", [P, HALF]) for i in range(2)]
        ag = [at.sb(f"ag{i}", [P, C]) for i in range(2)]
        zb = [at.sb(f"zb{i}", [P, 1]) for i in range(2)]
        st = at.sb("st", [P, 2, 6])
        axr = [at.sb(f"axr{i}", [KR, P]) for i in range(2)]
        axh = [at.sb(f"axh{i}", [KR, P], F32R) for i in range(2)]
        axl = [at.sb(f"axl{i}", [KR, P], F32R) for i in range(2)]
        braw = at.sb("braw", [KR, HALF])
        bhi = at.sb("bhi", [KR, HALF], F32R)
        blo = at.sb("blo", [KR, HALF], F32R)

        k_in = [at.sem(f"k_in{i}") for i in range(2)]
        k_hi, k_lo = at.sem("k_hi"), at.sem("k_lo")
        c_in = [at.sem(f"c_in{i}") for i in range(2)]
        x_in = [at.sem(f"x_in{i}") for i in range(2)]
        ag_in = [at.sem(f"ag_in{i}") for i in range(2)]
        ax_in = [at.sem(f"ax_in{i}") for i in range(2)]
        b_in = at.sem("b_in")
        one = at.sem("one")
        c_hi, c_lo = at.sem("c_hi"), at.sem("c_lo")
        ax_hi, ax_lo = at.sem("ax_hi"), at.sem("ax_lo")
        b_hi, b_lo = at.sem("b_hi"), at.sem("b_lo")
        c_used = at.sem("c_used")
        lora_mm = at.sem("lora_mm")
        y_out = at.sem("y_out")
        z_mm = at.sem("z_mm")
        z_out = at.sem("z_out")
        stats, kept = at.sem("stats"), at.sem("kept")
        yz_out = at.sem("yz_out")
        z_st = [at.sem(f"z_st{i}") for i in range(2)]
        yz_st = [at.sem(f"yz_st{i}") for i in range(2)]
        block = ctx.enter_context(nc.Block())

        def turn_of(half, b, u):
            return N * half + SPB * b + u, N // 2 * half + SPB // 2 * b + u // 2

        def after(half, b, u):
            if u + 1 < SPB:
                return half, b, u + 1
            if isinstance(b, int) and b == B - 1:
                return half + 1, 0, 0
            return half, b + 1, 0

        def before(half, b, u):
            if u:
                return half, b, u - 1
            if isinstance(b, int) and b == 0:
                return half - 1, B - 1, SPB - 1
            return half, b - 1, SPB - 1

        def bodies(eng, body):
            for half in range(2):
                body(half, 0)
                with eng.Fori(1, B - 1) as b:
                    body(half, b)
                body(half, B - 1)

        @block.sync
        def _(sp):
            def load(half, b, u):
                t, t2 = turn_of(half, b, u)
                n = SPB * b + u
                first = half == 0 and isinstance(b, int) and b == 0 and u < 2
                if not first:
                    sp.wait_ge(y_out, 2 + t - 1)
                sp.dma_start(craw[u % 2][:, :, :].rearrange("p k c -> p (k c)"), scr["ct"][n]).then_inc(c_in[u % 2], 16)
                sp.dma_start(axr[u % 2][0:2 * R, :], scr["ax"][n]).then_inc(ax_in[u % 2], 16)
                if not first:
                    sp.wait_ge(yz_st[u % 2], 16 * (t2 + 1))
                sp.dma_start(yo[u % 2][:, :], a["x"][n, :, half * HALF:(half + 1) * HALF]).then_inc(x_in[u % 2], 16)
                sp.dma_start(ag[u % 2][:, :], scr["agg"][n].rearrange("(i o) -> i o", o=C)).then_inc(ag_in[u % 2], 16)
                sp.dma_start(zb[u % 2][:, :], scr["aggb"][n].unsqueeze(1)).then_inc(ag_in[u % 2], 16)

            def body(half, b):
                for u in range(SPB):
                    load(half, b, u)

            bodies(sp, body)
            for i in range(2):
                sp.wait_ge(yz_st[i], 16 + 16 * N)
                sp.wait_ge(z_st[i], 16 + 16 * N)

        @block.gpsimd
        def _(pool):
            def load_b(half, b):
                pool.wait_ge(b_lo, B * half + b + 1)
                cols = slice(half * HALF, (half + 1) * HALF)
                pool.dma_start(braw[0:R, :], scr["lb"][b][:, cols]).then_inc(b_in, 16)
                pool.dma_start(braw[R:2 * R, :], a["lbS"][:, cols]).then_inc(b_in, 16)
                pool.dma_start(braw[2 * R:KR, :], a["ffn_bias"][:, cols]).then_inc(b_in, 16)

            with pool.Fori(0, B) as b:
                load_b(0, b)
            load_b(1, 0)
            kern = kernel_chunks(a, 1)
            for kc in range(KC):
                if kc >= 2:
                    pool.wait_ge(k_lo, kc - 1)
                pool.dma_start(kst[kc % 2][:, :], kern[kc // PH, kc % PH]).then_inc(k_in[kc % 2], 16)
            with pool.Fori(1, B) as b:
                load_b(1, b)

        def kernel_high(act, j):
            for kc in range(QK * j, QK * (j + 1)):
                act.wait_ge(k_in[kc % 2], 16 * (kc // 2 + 1))
                act.wait_ge(c_used, 4 + 4 * (N - 1) + j + 1)
                act.activation(khi[:, kc, :], kst[kc % 2][:, :], ACT.Copy).then_inc(k_hi, 1)

        def kernel_low(dve, j):
            for kc in range(QK * j, QK * (j + 1)):
                dve.wait_ge(k_hi, kc + 1)
                dve.tensor_tensor(klo[:, kc, :], kst[kc % 2][:, :], khi[:, kc, :].bitcast(F32),
                                  ALU.subtract).then_inc(k_lo, 1)

        def high(act, half, b, u, j):
            t, t2 = turn_of(half, b, u)
            if j == 0:
                act.wait_ge(c_in[u % 2], 16 * (t2 + 1))
            act.wait_ge(c_used, 4 * t + j + 1)
            act.activation(chi[:, QK * j:QK * (j + 1), :], craw[u % 2][:, QK * j:QK * (j + 1), :],
                           ACT.Copy).then_inc(c_hi, 1)
            if j == 1:
                act.wait_ge(ax_in[u % 2], 16 * (t2 + 1))
                act.wait_ge(lora_mm, t + 1)
                act.activation(axh[u % 2][:, :], axr[u % 2][:, :], ACT.Copy).then_inc(ax_hi, 1)
                if u == 0:
                    act.wait_ge(b_in, 48 * (B * half + b + 1))
                    act.wait_ge(lora_mm, 2 + t)
                    act.activation(bhi[:, :], braw[:, :], ACT.Copy).then_inc(b_hi, 1)

        def low(dve, half, b, u, j):
            t, t2 = turn_of(half, b, u)
            s = slice(QK * j, QK * (j + 1))
            dve.wait_ge(c_hi, 4 * t + j + 1)
            dve.tensor_tensor(clo[:, s, :], craw[u % 2][:, s, :], chi[:, s, :].bitcast(F32),
                              ALU.subtract).then_inc(c_lo, 1)
            if j == 1:
                dve.wait_ge(ax_hi, t + 1)
                dve.tensor_tensor(axl[u % 2][:, :], axr[u % 2][:, :], axh[u % 2][:, :].bitcast(F32),
                                  ALU.subtract).then_inc(ax_lo, 1)
                if u == 0:
                    dve.wait_ge(b_hi, B * half + b + 1)
                    dve.tensor_tensor(blo[:, :], braw[:, :], bhi[:, :].bitcast(F32),
                                      ALU.subtract).then_inc(b_lo, 1)

        def y_sum(dve, half, b, u):
            t, t2 = turn_of(half, b, u)
            dve.wait_ge(c_used, 4 + 4 * (t + 1))
            dve.wait_ge(x_in[u % 2], 16 * (t2 + 1))
            for h in range(2):
                s = slice(h * BANK, (h + 1) * BANK)
                add = dve.tensor_tensor(yo[u % 2][:, s], ps[2 * (u % 2) + h][:, :], yo[u % 2][:, s], ALU.add)
            add.then_inc(y_out, 1)

        def z_copy(act, half, b, u):
            t, t2 = turn_of(half, b, u)
            act.wait_ge(z_st[u % 2], 16 * (t2 + 1))
            act.wait_ge(yz_out, t - 1 + 2)
            act.wait_ge(z_mm, t + 1)
            for h in range(2):
                copy = act.activation(zo[u % 2][:, h * BANK:(h + 1) * BANK], ps[4 + h][:, :], ACT.Identity,
                                      bias=zb[u % 2][:, 0:1])
            copy.then_inc(z_out, 1)
            act.wait_ge(z_out, 1 + t + 1)
            act.dma_start(scr["z"][SPB * b + u, :, half * HALF:(half + 1) * HALF], zo[u % 2][:, :])\
               .then_inc(z_st[u % 2], 16)

        def z_use(dve, half, b, u):
            t, t2 = turn_of(half, b, u)
            dve.wait_ge(z_out, 1 + t + 1)
            for h in range(2):
                dve.bn_stats(st[:, h, :], zo[u % 2][:, h * BANK:(h + 1) * BANK]).then_inc(stats, 1)
            dve.tensor_tensor(yo[u % 2][:, :], yo[u % 2][:, :], zo[u % 2][:, :], ALU.add).then_inc(yz_out, 1)
            dve.wait_ge(stats, 2 * (t + 1))
            dve.tensor_scalar(st_all[:, SPB * b + u, 12 * half:12 * (half + 1)],
                              st[:, :, :].rearrange("p h s -> p (h s)"), 1.0, None, ALU.mult).then_inc(kept, 1)
            dve.wait_ge(kept, t + 1)

        def yz_store(act, half, b, u):
            t, t2 = turn_of(half, b, u)
            act.wait_ge(yz_out, 2 + t + 1)
            act.dma_start(scr["yz"][SPB * b + u, :, half * HALF:(half + 1) * HALF], yo[u % 2][:, :])\
               .then_inc(yz_st[u % 2], 16)

        def edges(half, b, u):
            first = half == 0 and isinstance(b, int) and b == 0 and u == 0
            last = half == 1 and isinstance(b, int) and b == B - 1 and u == SPB - 1
            seam = half == 0 and isinstance(b, int) and b == B - 1 and u == SPB - 1
            return first, last, seam

        @block.scalar
        def _(act):
            for i in range(2):
                act.sem_inc(z_st[i], 16)
                act.sem_inc(yz_st[i], 16)
            act.sem_inc(z_out, 1)
            act.wait_ge(one, 2)
            for j in range(4):
                high(act, 0, 0, 0, j)

            def body(half, b):
                for u in range(SPB):
                    first, last, seam = edges(half, b, u)
                    for j in range(4):
                        if seam:
                            kernel_high(act, j)
                        if not last:
                            high(act, *after(half, b, u), j)
                        if j == 0 and not first:
                            z_copy(act, *before(half, b, u))
                        if j == 1 and not first:
                            yz_store(act, *before(half, b, u))

            bodies(act, body)
            z_copy(act, 1, B - 1, SPB - 1)
            yz_store(act, 1, B - 1, SPB - 1)

        @block.vector
        def _(dve):
            for i in range(2):
                dve.memset(axr[i][2 * R:KR, :], 1.0).then_inc(one, 1)
            dve.sem_inc(y_out, 2)
            dve.sem_inc(b_lo, 1)
            dve.sem_inc(yz_out, 2)
            for j in range(4):
                low(dve, 0, 0, 0, j)

            def body(half, b):
                for u in range(SPB):
                    first, last, seam = edges(half, b, u)
                    for j in range(4):
                        if j == 2 and not first:
                            z_use(dve, *before(half, b, u))
                        if j == 3:
                            y_sum(dve, half, b, u)
                        if seam:
                            kernel_low(dve, j)
                        if not last:
                            low(dve, *after(half, b, u), j)

            bodies(dve, body)
            z_use(dve, 1, B - 1, SPB - 1)

        @block.tensor
        def _(pe):
            pe.sem_inc(c_used, 4)
            pe.sem_inc(lora_mm, 2)

            def z_of(half, b, u):
                t, t2 = turn_of(half, b, u)
                pe.wait_ge(ag_in[u % 2], 32 * (t2 + 1))
                pe.wait_ge(z_out, t + 1)
                pe.wait_ge(y_out, 2 + t + 1)
                for h in range(2):
                    mm = pe.matmul(ps[4 + h][:, :], ag[u % 2][:, :], yo[u % 2][:, h * BANK:(h + 1) * BANK],
                                   start=True, stop=True)
                mm.then_inc(z_mm, 1)

            def turn(half, b, u):
                t, t2 = turn_of(half, b, u)
                first, last, seam = edges(half, b, u)
                out = [ps[2 * (u % 2) + h] for h in range(2)]
                pe.wait_ge(y_out, t + 1)
                for j in range(4):
                    if half == 1 and isinstance(b, int) and b == 0 and u == 0:
                        pe.wait_ge(k_lo, QK * (j + 1))
                    pe.wait_ge(c_lo, 4 * t + j + 1)
                    for kc in range(QK * j, QK * (j + 1)):
                        for lhs, parts in ((chi, (khi, klo)), (clo, (khi,))):
                            for h in range(2):
                                for rhs in parts:
                                    mm = pe.matmul(out[h][:, :], lhs[:, kc, :],
                                                   rhs[:, kc, h * BANK:(h + 1) * BANK],
                                                   start=(kc == 0 and lhs is chi and rhs is khi),
                                                   stop=(kc == KC - 1 and lhs is clo))
                    mm.then_inc(c_used, 1)
                    if j == 0 and not first:
                        z_of(*before(half, b, u))
                    if j == 1:
                        pe.wait_ge(ax_lo, t + 1)
                        pe.wait_ge(b_lo, B * half + b + 2)
                        for lhs, parts in ((axh[u % 2], (bhi, blo)), (axl[u % 2], (bhi,))):
                            for h in range(2):
                                for rhs in parts:
                                    mm = pe.matmul(out[h][:, :], lhs[:, :], rhs[:, h * BANK:(h + 1) * BANK],
                                                   start=False, stop=False)
                        mm.then_inc(lora_mm, 1)

            def body(half, b):
                for u in range(SPB):
                    turn(half, b, u)

            bodies(pe, body)
            z_of(1, B - 1, SPB - 1)


def attend(nc, ps, a, scr, st_all, out):
    T4 = KC // 4
    t_ps, o_ps, u_ps, s_ps, a_ps, m_ps = ps[0:2], ps[2:4], ps[4], ps[5], ps[6], ps[7]
    Q, RQ = slice(0, P), slice(P, 2 * P)
    with ExitStack() as ctx:
        at = Places(nc, ctx, "att")
        ident = at.sb("ident", [P, P])
        wst = [at.sb(f"wst{i}", [P, 2, UH + BOT]) for i in range(2)]
        wh = at.sb("wh", [P, KC, UH + BOT], F32R)
        wl = at.sb("wl", [P, KC, UH + BOT], F32R)
        vst = at.sb("vst", [P, L])
        vh = at.sb("vh", [P, L], F32R)
        vl = at.sb("vl", [P, L], F32R)
        vp = at.sb("vp", [P, NS // P, VB])
        keysT = at.sb("keysT", [BOT, NS])
        wrT = at.sb("wrT", [BOT, P])
        rkT = at.sb("rkT", [RD, NS])
        lrel = at.sb("lrel", [P, NS])
        bu1 = at.sb("bu1", [P, UH])
        wu2 = at.sb("wu2", [P, UH])
        cst = at.sb("cst", [P, 3])
        half = at.sb("half", [P, 3])
        mv = at.sb("mv", [P, N, 2])
        logv = at.sb("logv", [P, N])
        lsum = at.sb("lsum", [P, 1])
        total = at.sb("total", [P, 1])
        mean = at.sb("mean", [P, 1])
        rmean = at.sb("rmean", [P, 1])
        nv = at.sb("nv", [P, N])
        z = [at.sb(f"z{i}", [P, L]) for i in range(2)]
        yz = [at.sb(f"yz{i}", [P, L]) for i in range(2)]
        zh = at.sb("zh", [P, KC, P], F32R)
        zl = at.sb("zl", [P, KC, P], F32R)
        qT = at.sb("qT", [BOT, P])
        rqT = at.sb("rqT", [RD, P])
        sc = at.sb("sc", [P, NS])
        rest = at.sb("rest", [P, NS])
        out_of = at.sb("out_of", [P, NS])
        top = at.sb("top", [P, 8])
        lg = at.sb("lg", [P, NS])
        lgm = at.sb("lgm", [P, NS])
        mx = at.sb("mx", [P, 1])
        nmx = at.sb("nmx", [P, 1])
        ex = at.sb("ex", [P, NS])
        exT = at.sb("exT", [P, NS])
        esum = at.sb("esum", [P, 1])
        ub = at.sb("ub", [P, UH])
        ug = at.sb("ug", [P, UH])
        learned = at.sb("learned", [P, 1])
        g = [at.sb(f"g{i}", [P, 1]) for i in range(12)]
        rh = at.sb("rh", [P, P], F32R)
        rl = at.sb("rl", [P, P], F32R)

        id0, id1, small_in, wr0 = (at.sem(s) for s in ("id0", "id1", "small_in", "wr0"))
        w_in = [at.sem(f"w_in{i}") for i in range(2)]
        w_hi, w_lo, v_in, v_hi, v_lo = (at.sem(s) for s in ("w_hi", "w_lo", "v_in", "v_hi", "v_lo"))
        pre_in, pre_mm, pre_out = at.sem("pre_in"), at.sem("pre_mm"), at.sem("pre_out")
        var_ok, log_ok, tot_ok, mean_ok, half_ok = (at.sem(s) for s in ("var_ok", "log_ok", "tot_ok", "mean_ok", "half_ok"))
        z_in = [at.sem(f"z_in{i}") for i in range(2)]
        yz_in = [at.sem(f"yz_in{i}") for i in range(2)]
        t_mm, z_hi, z_lo = at.sem("t_mm"), at.sem("z_hi"), at.sem("z_lo")
        u_mm, u_add, u_act, u_sum = (at.sem(s) for s in ("u_mm", "u_add", "u_act", "u_sum"))
        q_out, rq_mm, rq_out, s_mm, a_mm = (at.sem(s) for s in ("q_out", "rq_mm", "rq_out", "s_mm", "a_mm"))
        step = at.sem("step")
        gst = at.sem("gst")
        g_t1, g_t2 = at.sem("g_t1"), at.sem("g_t2")
        e_out = at.sem("e_out")
        e_mm, e_cp, r_mm, r_hi, r_lo = (at.sem(s) for s in ("e_mm", "e_cp", "r_mm", "r_hi", "r_lo"))
        o_mm, o_add = at.sem("o_mm"), at.sem("o_add")
        o_st = [at.sem(f"o_st{i}") for i in range(2)]
        block = ctx.enter_context(nc.Block())

        avT = (z[0], z[1], yz[0], yz[1])
        wvdT = vst

        @block.sync
        def _(sp):
            sp.wait_ge(wr0, 1)
            small = [(keysT[:, :], a["keysT"]), (wrT[:, 0:RD], a["wrT"]),
                     (lrel[:, :], a["log_rel"].to_broadcast([P, NS])),
                     (bu1[:, :], a["bu1"].to_broadcast([P, UH])),
                     (wu2[:, :], a["wu2"].to_broadcast([P, UH]))]
            small += [(cst[:, k:k + 1], a[name].to_broadcast([P, 1]))
                      for k, name in enumerate(("bu2", "gate_w1", "gate_bias"))]
            for i in range(4):
                sp.dma_start(avT[i][:, :].rearrange("p (k n) -> p k n", n=NS),
                             a["avT"][4 * i * P:4 * (i + 1) * P, :].rearrange("(k p) n -> p k n", p=P)).then_inc(pre_in, 16)
            sp.dma_start(wvdT[:, :].rearrange("p (k v) -> p k v", v=VB),
                         a["wvdT"].rearrange("(k p) v -> p k v", p=P)).then_inc(pre_in, 16)
            for dst, src in small:
                sp.dma_start(dst, src).then_inc(small_in, 16)
            for t in range(KC // 2):
                if t >= 2:
                    sp.wait_ge(w_lo, t - 1)
                sp.dma_start(wst[t % 2][:, :, :], a["wuq"][2 * t * P:2 * (t + 1) * P, :]
                             .rearrange("(k p) n -> p k n", p=P)).then_inc(w_in[t % 2], 16)
            sp.wait_ge(pre_mm, 5)

            def load(n, i, u, first=False):
                if not first:
                    sp.wait_ge(t_mm, 4 * (n - 1))
                sp.dma_start(z[u][:, :], scr["z"][n]).then_inc(z_in[u], 16)
                if not first:
                    sp.wait_ge(o_st[u], 16 * (i + 1))
                sp.dma_start(yz[u][:, :], scr["yz"][n]).then_inc(yz_in[u], 16)

            load(0, 0, 0, True)
            load(1, 0, 1, True)
            sp.dma_start(vst[:, :], a["wvuT"]).then_inc(v_in, 16)
            with sp.Fori(1, N // 2) as i:
                for u in range(2):
                    load(2 * i + u, i, u)
            for i in range(2):
                sp.wait_ge(o_st[i], 16 + 16 * N // 2)

        @block.gpsimd
        def _(pool):
            pool.memset(ident[:, :], 0.0).then_inc(id0, 1)
            pool.wait_ge(id0, 1)
            pool.affine_select(out=ident[:, :], in_=ident[:, :], compare_op=ALU.not_equal, fill=1.0,
                               base=0, pattern=[[-1, P]], channel_multiplier=1).then_inc(id1, 1)
            pool.wait_ge(log_ok, 1)
            pool.partition_all_reduce(total[:, :], lsum[:, :], P, bass.bass_isa.ReduceOp.add).then_inc(tot_ok, 1)

        @block.tensor
        def _(pe):
            pe.wait_ge(pre_in, 80)
            for c in range(NS // P):
                for k in range(KC):
                    mm = pe.matmul(ps[0][:, c * VB:(c + 1) * VB],
                                   avT[k // 4][:, (k % 4) * NS + c * P:(k % 4) * NS + (c + 1) * P],
                                   wvdT[:, k * VB:(k + 1) * VB], start=(k == 0), stop=(k == KC - 1))
                mm.then_inc(pre_mm, 1)
            pe.wait_ge(small_in, 16 * 8)
            pe.matmul(ps[1][0:RD, 0:NS], wrT[:, 0:RD], keysT[:, :], start=True, stop=True).then_inc(pre_mm, 1)
            pe.wait_ge(pre_out, 2)
            pe.wait_ge(id1, 1)

            def turn(n, i, u, j, first=False):
                if j == 0:
                    pe.wait_ge(z_in[u], 16 * (i + 1))
                if not (first and j < 2):
                    pe.wait_ge(z_lo, 4 * n + j - 1)
                for k in range(4):
                    mm = pe.transpose(t_ps[j % 2][:, k * P:(k + 1) * P],
                                      z[u][:, (4 * j + k) * P:(4 * j + k + 1) * P], ident[:, :])
                mm.then_inc(t_mm, 1)

            def heads(n, j, first):
                if j == 0 and not first:
                    pe.wait_ge(u_add, n)
                    pe.wait_ge(rq_out, n)
                pe.wait_ge(z_lo, 4 * n + j + 1)
                for k in range(T4 * j, T4 * (j + 1)):
                    for lhs, parts in ((zh, (wh, wl)), (zl, (wh,))):
                        for w in parts:
                            edge = dict(start=(k == 0 and lhs is zh and w is wh),
                                        stop=(k == KC - 1 and lhs is zl))
                            pe.matmul(u_ps[:, :], lhs[:, k, :], w[:, k, 0:UH], **edge)
                            mm = pe.matmul(m_ps[0:BOT, Q], w[:, k, UH:UH + BOT], lhs[:, k, :], **edge)
                mm.then_inc(u_mm, 1)

            def router_query(n):
                pe.wait_ge(q_out, n + 1)
                pe.matmul(m_ps[:, RQ], wrT[:, :], qT[:, :], start=True, stop=True).then_inc(rq_mm, 1)

            def scores(n, first):
                if not first:
                    pe.wait_ge(r_lo, n)
                    pe.wait_ge(e_cp, n)
                pe.matmul(a_ps[:, :], qT[:, :], keysT[:, :], start=True, stop=True).then_inc(a_mm, 1)
                pe.wait_ge(rq_out, n + 1)
                pe.matmul(s_ps[:, :], rqT[:, :], rkT[:, :], start=True, stop=True).then_inc(s_mm, 1)

            def turn_e(n):
                pe.wait_ge(step, STEPS * n + 2)
                pe.wait_ge(e_out, n + 2)
                for k in range(4):
                    mm = pe.transpose(s_ps[:, k * P:(k + 1) * P], ex[:, k * P:(k + 1) * P], ident[:, :])
                mm.then_inc(e_mm, 1)

            def read(n):
                pe.wait_ge(step, STEPS * n + 1)
                pe.wait_ge(e_cp, n + 1)
                for k in range(4):
                    mm = pe.matmul(a_ps[:, 0:P], vp[:, k, :], exT[:, k * P:(k + 1) * P], start=(k == 0), stop=(k == 3))
                mm.then_inc(r_mm, 1)

            def expand(n, hs):
                pe.wait_ge(r_lo, n + 1)
                for h in hs:
                    pe.wait_ge(o_add, 4 * n + h + 1)
                    s = slice(h * BANK, (h + 1) * BANK)
                    for k, (lhs, w) in enumerate(((rh, vh), (rh, vl), (rl, vh))):
                        mm = pe.matmul(o_ps[h % 2][:, :], lhs[:, :], w[:, s], start=(k == 0), stop=(k == 2))
                    mm.then_inc(o_mm, 1)

            def sample(n, i, w, first=False, last=False):
                here = 0 if first else i - 1 + w if not isinstance(i, int) else N // 2 - 1
                heads(n, 0, first)
                turn(n, here, 1 - w, 2)
                heads(n, 1, first)
                turn(n, here, 1 - w, 3)
                if not first:
                    turn_e(n - 1)
                heads(n, 2, first)
                if not first:
                    read(n - 1)
                heads(n, 3, first)
                if not last:
                    turn(n + 1, i, w, 0)
                    turn(n + 1, i, w, 1)
                router_query(n)
                if not first:
                    expand(n - 1, (0, 1))
                scores(n, first)
                if not first:
                    expand(n - 1, (2, 3))

            turn(0, 0, 0, 0, first=True)
            turn(0, 0, 0, 1, first=True)
            pe.wait_ge(w_lo, KC // 2)
            sample(0, 0, 1, first=True)
            pe.wait_ge(v_lo, 1)
            with pe.Fori(1, N // 2) as i:
                sample(2 * i - 1, i, 0)
                sample(2 * i, i, 1)
            sample(N - 1, N // 2, 0, last=True)
            turn_e(N - 1)
            read(N - 1)
            expand(N - 1, range(4))

        @block.scalar
        def _(act):
            for i in range(2):
                act.sem_inc(o_st[i], 16)
            act.sem_inc(e_out, 1)
            act.wait_ge(var_ok, N)
            act.activation(logv[:, :], mv[:, :, 1], ACT.Ln, bias=1.0, accum_out=lsum[:, :]).then_inc(log_ok, 1)

            def high(n, j, first=False):
                act.wait_ge(t_mm, 4 * n + j + 1)
                if not first:
                    act.wait_ge(u_mm, 4 * (n - 1) + j + 1)
                act.activation(zh[:, T4 * j:T4 * (j + 1), :],
                               t_ps[j % 2][:, :].rearrange("p (k c) -> p k c", c=P), ACT.Copy).then_inc(z_hi, 1)

            def numerators(n):
                act.wait_ge(step, STEPS * (n + 1))
                act.activation(ex[:, :], lgm[:, :], ACT.Exp, bias=nmx[:, 0:1],
                               accum_out=esum[:, 0:1]).then_inc(e_out, 1)

            def copy_e(n):
                act.wait_ge(e_mm, n + 1)
                act.activation(exT[:, :], s_ps[:, :], ACT.Copy).then_inc(e_cp, 1)

            def gate_1(n):
                act.wait_ge(u_sum, n + 1)
                act.activation(g[0][:, :], learned[:, :], ACT.Tanh, scale=0.5, bias=half[:, 0:1]).then_inc(g_t1, 1)

            def gate_2(n):
                act.wait_ge(gst, GSTEPS * n + GHALF)
                act.activation(g[7][:, :], g[6][:, :], ACT.Tanh, scale=half[:, 1:2], bias=half[:, 2:3]).then_inc(g_t2, 1)

            def read_high(n):
                act.wait_ge(r_mm, n + 1)
                act.activation(rh[:, :], a_ps[:, 0:P], ACT.Copy).then_inc(r_hi, 1)

            def store(n, u):
                act.wait_ge(o_add, 2 + 4 * (n + 1))
                act.dma_start(out[n], yz[u][:, :]).then_inc(o_st[u], 16)

            def sample(n, w, first=False, last=False):
                high(n, 2, first)
                if not first:
                    numerators(n - 1)
                    gate_1(n - 1)
                high(n, 3, first)
                if not first:
                    copy_e(n - 1)
                    gate_2(n - 1)
                    act.wait_ge(o_mm, 4 * (n - 1)) if not (isinstance(n, int) and n == 1) else None
                    read_high(n - 1)
                    act.wait_ge(s_mm, n)
                act.wait_ge(u_mm, 4 * (n + 1))
                act.activation(qT[:, :], m_ps[0:BOT, Q], ACT.Copy).then_inc(q_out, 1)
                if not last:
                    high(n + 1, 0)
                act.wait_ge(rq_mm, n + 1)
                act.activation(rqT[:, :], m_ps[0:RD, RQ], ACT.Copy).then_inc(rq_out, 1)
                if not last:
                    high(n + 1, 1)
                act.wait_ge(u_add, n + 1)
                if not first:
                    act.wait_ge(u_sum, n)
                act.activation(ug[:, :], ub[:, :], ACT.Gelu_apprx_tanh).then_inc(u_act, 1)
                if not first:
                    store(n - 1, w)

            high(0, 0, first=True)
            high(0, 1, first=True)
            act.wait_ge(v_in, 16)
            act.activation(vh[:, :], vst[:, :], ACT.Copy).then_inc(v_hi, 1)
            act.wait_ge(half_ok, 1)
            sample(0, 1, first=True)
            with act.Fori(1, N // 2) as i:
                sample(2 * i - 1, 0)
                sample(2 * i, 1)
            sample(N - 1, 0, last=True)
            numerators(N - 1)
            gate_1(N - 1)
            copy_e(N - 1)
            gate_2(N - 1)
            act.wait_ge(o_mm, 4 * (N - 1))
            read_high(N - 1)
            store(N - 1, 1)

        @block.vector
        def _(dve):
            dve.memset(wrT[:, :], 0.0).then_inc(wr0, 1)
            for n in range(N):
                dve.bn_aggr(mv[:, n, :], st_all[:, n, :]).then_inc(var_ok, 1)
            for t in range(KC // 2):
                dve.wait_ge(w_in[t % 2], 16 * (t // 2 + 1))
                dve.tensor_scalar(wh[:, 2 * t:2 * t + 2, :], wst[t % 2][:, :, :], 1.0, None, ALU.mult).then_inc(w_hi, 1)
                dve.wait_ge(w_hi, t + 1)
                dve.tensor_tensor(wl[:, 2 * t:2 * t + 2, :], wst[t % 2][:, :, :], wh[:, 2 * t:2 * t + 2, :].bitcast(F32),
                                  ALU.subtract).then_inc(w_lo, 1)
                if t == 3:
                    dve.wait_ge(pre_mm, 4)
                    dve.tensor_copy(vp[:, :, :], ps[0][:, :].rearrange("p (c v) -> p c v", v=VB)).then_inc(pre_out, 1)
                    dve.wait_ge(pre_mm, 5)
                    dve.tensor_copy(rkT[:, :], ps[1][0:RD, 0:NS]).then_inc(pre_out, 1)
            dve.wait_ge(small_in, 16 * 8)
            dve.tensor_scalar(half[:, :], cst[:, :], 0.5, None, ALU.mult).then_inc(half_ok, 1)
            dve.sem_inc(o_add, 2)

            def low(n, j):
                dve.wait_ge(z_hi, 4 * n + j + 1)
                s = slice(T4 * j, T4 * (j + 1))
                dve.tensor_tensor(zl[:, s, :], t_ps[j % 2][:, :].rearrange("p (k c) -> p k c", c=P),
                                  zh[:, s, :].bitcast(F32), ALU.subtract).then_inc(z_lo, 1)

            def choose(n):
                done = STEPS * n
                dve.wait_ge(a_mm, n + 1)
                dve.scalar_tensor_tensor(out=lg[:, :], in0=a_ps[:, :], scalar=float(BOT) ** -0.5, in1=lrel[:, :],
                                         op0=ALU.mult, op1=ALU.add).then_inc(step, 1)
                dve.wait_ge(s_mm, n + 1)
                dve.scalar_tensor_tensor(out=sc[:, :], in0=s_ps[:, :], scalar=float(RD) ** -0.5, in1=lrel[:, :],
                                         op0=ALU.mult, op1=ALU.add).then_inc(step, 1)
                dve.wait_ge(step, done + 2)
                dve.wait_ge(u_act, n + 1)
                dve.tensor_tensor_reduce(ug[:, :], ug[:, :], wu2[:, :], 1.0, 0.0, ALU.mult, ALU.add,
                                         learned[:, :]).then_inc(u_sum, 1)
                dve.max(top[:, :], sc[:, :]).then_inc(step, 1)
                dve.wait_ge(step, done + 3)
                dve.tensor_scalar(g[3][:, :], nv[:, bass.ds(n, 1)], 1.0, None, ALU.mult).then_inc(gst, 1)
                dve.match_replace(rest[:, :], top[:, :], sc[:, :], FAR).then_inc(step, 1)
                dve.wait_ge(step, done + 4)
                dve.tensor_tensor(out_of[:, :], rest[:, :], sc[:, :], ALU.is_equal).then_inc(step, 1)
                dve.wait_ge(step, done + 5)
                dve.wait_ge(e_out, n + 1)
                dve.scalar_tensor_tensor(out=lgm[:, :], in0=out_of[:, :], scalar=FAR, in1=lg[:, :],
                                         op0=ALU.mult, op1=ALU.add).then_inc(step, 1)
                dve.wait_ge(step, done + 6)
                dve.tensor_reduce(mx[:, :], lgm[:, :], AX_X, ALU.max).then_inc(step, 1)
                dve.wait_ge(step, done + 7)
                dve.tensor_scalar(nmx[:, :], mx[:, :], -1.0, None, ALU.mult).then_inc(step, 1)

            def gate(n):
                done = GSTEPS * n + 1

                def link(k, ins):
                    ins.then_inc(gst, 1)
                    dve.wait_ge(gst, done + k)

                dve.wait_ge(g_t1, n + 1)
                link(1, dve.tensor_scalar(g[1][:, :], g[0][:, :], 1.25, 1.25, ALU.mult, ALU.add))
                link(2, dve.tensor_scalar(g[2][:, :], g[1][:, :], g[3][:, 0:1], 0.0, ALU.add, ALU.max))
                link(3, dve.tensor_scalar(g[4][:, :], g[2][:, :], 5.0, TAU_LOW, ALU.min, ALU.subtract))
                link(4, dve.tensor_scalar(g[5][:, :], g[4][:, :], 1.0 / (TAU_HIGH - TAU_LOW), 0.0, ALU.mult, ALU.max))
                link(5, dve.tensor_scalar(g[6][:, :], g[5][:, :], 1.0, None, ALU.min))

            def gate_end(n):
                done = GSTEPS * n + GHALF

                def link(k, ins):
                    ins.then_inc(gst, 1)
                    dve.wait_ge(gst, done + k)

                dve.wait_ge(g_t2, n + 1)
                dve.wait_ge(e_out, n + 2)
                link(1, dve.tensor_scalar(g[8][:, :], g[7][:, :], 0.5, 0.5, ALU.mult, ALU.add))
                link(2, dve.scalar_tensor_tensor(out=g[9][:, :], in0=g[8][:, :], scalar=EARLY_EXIT, in1=g[8][:, :],
                                                 op0=ALU.is_ge, op1=ALU.mult))
                link(3, dve.reciprocal(g[10][:, :], esum[:, :]))
                link(4, dve.tensor_scalar(g[11][:, :], g[9][:, :], g[10][:, 0:1], None, ALU.mult))

            def read_low(n):
                dve.wait_ge(r_hi, n + 1)
                dve.tensor_tensor(rl[:, :], a_ps[:, 0:P], rh[:, :].bitcast(F32), ALU.subtract).then_inc(r_lo, 1)

            def add(n, i, u):
                dve.wait_ge(yz_in[u], 16 * (i + 1))
                for h in range(4):
                    s = slice(h * BANK, (h + 1) * BANK)
                    dve.wait_ge(o_mm, 4 * n + h + 1)
                    dve.scalar_tensor_tensor(out=yz[u][:, s], in0=o_ps[h % 2][:, :], scalar=g[11][:, 0:1],
                                             in1=yz[u][:, s], op0=ALU.mult, op1=ALU.add).then_inc(o_add, 1)

            def hidden(n, first=False):
                dve.wait_ge(u_mm, 4 * (n + 1))
                if not first:
                    dve.wait_ge(u_act, n)
                dve.tensor_tensor(ub[:, :], u_ps[:, :], bu1[:, :], ALU.add).then_inc(u_add, 1)

            def sample(n, i, u, first=False, last=False):
                if not first:
                    choose(n - 1)
                low(n, 2)
                if not first:
                    gate(n - 1)
                low(n, 3)
                if not first:
                    gate_end(n - 1)
                    read_low(n - 1)
                hidden(n, first)
                if not last:
                    low(n + 1, 0)
                    low(n + 1, 1)
                if not first:
                    add(n - 1, i, u)

            low(0, 0)
            low(0, 1)
            dve.wait_ge(tot_ok, 1)
            dve.tensor_scalar(mean[:, :], total[:, :], 1.0 / (N * C), 1e-6, ALU.mult, ALU.add).then_inc(mean_ok, 1)
            dve.wait_ge(mean_ok, 1)
            dve.reciprocal(rmean[:, :], mean[:, :]).then_inc(mean_ok, 1)
            dve.wait_ge(mean_ok, 2)
            dve.tensor_scalar(nv[:, :], logv[:, :], rmean[:, 0:1], 0.5, ALU.mult, ALU.mult).then_inc(mean_ok, 1)
            dve.wait_ge(mean_ok, 3)
            dve.wait_ge(v_hi, 1)
            dve.tensor_tensor(vl[:, :], vst[:, :], vh[:, :].bitcast(F32), ALU.subtract).then_inc(v_lo, 1)
            sample(0, 0, 0, first=True)
            with dve.Fori(1, N // 2) as i:
                sample(2 * i - 1, i - 1, 0)
                sample(2 * i, i - 1, 1)
            sample(N - 1, N // 2 - 1, 0, last=True)
            choose(N - 1)
            gate(N - 1)
            gate_end(N - 1)
            read_low(N - 1)
            add(N - 1, N // 2 - 1, 1)


def program(nc, a, out):
    def dram(name, shape):
        return nc.dram_tensor(name, shape, F32, kind="Internal").ap()

    scr = {
        "crow": dram("scr_crow", (N, C)), "aggb": dram("scr_aggb", (N, C)),
        "agg": dram("scr_agg", (N, C * C)), "la": dram("scr_la", (B, P, KC, 2 * R)),
        "lb": dram("scr_lb", (B, R, L)), "ct": dram("scr_ct", (N, P, KC * C)),
        "ax": dram("scr_ax", (N, 2 * R, P)), "z": dram("scr_z", (N, C, L)), "yz": dram("scr_yz", (N, C, L)),
    }
    with ExitStack() as ctx:
        ps = [ctx.enter_context(nc.psum_tensor(f"bank{i}", [P, BANK], F32)) for i in range(8)]
        prologue(nc, ps, a, scr)
        st_all = ctx.enter_context(nc.sbuf_tensor("st_all", [P, N, 24], F32))
        with ExitStack() as kctx:
            khi = kctx.enter_context(nc.sbuf_tensor("khi", [P, KC, HALF], F32R))
            klo = kctx.enter_context(nc.sbuf_tensor("klo", [P, KC, HALF], F32R))
            convolve(nc, ps, a, scr, khi, klo)
            project(nc, ps, a, scr, khi, klo, st_all)
        attend(nc, ps, a, scr, st_all, out)


def kernel(**inputs):
    import numpy as np
    import concourse.bacc as bacc
    from concourse.bass_utils import run_bass_kernel_spmd

    x = np.asarray(inputs["x"])
    v = {k: np.asarray(w) for k, w in inputs.items()}
    laid = {
        "x": x,
        "xph": x.reshape(N, GROUPS, GC, M, PH).transpose(0, 4, 2, 1, 3).reshape(N, P, GROUPS * M),
        "taps": v["L0_cond_weight"].reshape(GROUPS, GC, GC, TAPS).transpose(3, 2, 0, 1),
        "condT": v["cond_128"].T,
        "cwT": v["L0_cond_c_weight"].T,
        "conv_bias": v["fside_S_0"].reshape(1, C),
        "gateT": v["L0_ffn_gate"].T,
        "kernel": v["L0_ffn_kernel"],
        "ffn_bias": v["L0_ffn_bias"].reshape(1, L),
        "loraA": v["L0_ffn_lora_A"].reshape(NL * R, L),
        "loraB": v["L0_ffn_lora_B"].transpose(0, 2, 1).reshape(NL * R, L),
        "laS": v["L0_ffn_lora_A_shared"].T,
        "lbS": v["L0_ffn_lora_B_shared"].T,
        "W0": v["L1_cond_W0"], "W1": v["L1_cond_W1"], "W2": v["L1_cond_W2"],
        "b0": v["L1_cond_b0"], "b1": v["L1_cond_b1"], "b2": v["L1_cond_b2"].reshape(1, NE),
        "wk": v["L1_cond_weight"][..., 0].transpose(0, 2, 1).reshape(NE, C * C),
        "bias_k": v["L1_cond_bias_k"],
        "wuq": np.concatenate([v["L1_ffn_Wu1"].T, v["L1_ffn_Wq"].T], axis=1),
        "wrT": v["L1_ffn_Wr"].T,
        "keysT": v["L1_ffn_aux_keys"].T,
        "avT": v["L1_ffn_aux_values"].T,
        "wvdT": v["L1_ffn_Wvd"].T,
        "wvuT": v["L1_ffn_Wvu"].T,
        "log_rel": v["L1_ffn_log_rel"].reshape(1, NS),
        "bu1": v["L1_ffn_bu1"].reshape(1, UH),
        "wu2": v["L1_ffn_Wu2"].reshape(1, UH),
        "bu2": v["L1_ffn_bu2"].reshape(1, 1),
        "gate_w1": v["L1_ffn_gate_w1"].reshape(1, 1),
        "gate_bias": v["L1_ffn_gate_bias"].reshape(1, 1),
    }
    nc = bacc.Bacc("TRN2", target_bir_lowering=False, num_devices=1)
    arrays, a = {}, {}
    for name, w in laid.items():
        w = np.ascontiguousarray(w)
        arrays[f"in_{name}"] = w
        a[name] = nc.dram_tensor(f"in_{name}", w.shape, mybir.dt.from_np(w.dtype), kind="ExternalInput").ap()
    out = nc.dram_tensor("out", (N, C, L), F32, kind="ExternalOutput").ap()
    program(nc, a, out)
    r = run_bass_kernel_spmd(nc, [arrays], core_ids=[0])
    return r.results[0]["out"]
```

```python
from contextlib import ExitStack

import numpy as np

import concourse.bass as bass
from concourse import mybir

P = 128
N, C, L = 32, 128, 2048
TAPS, PAD, GROUPS = 9, 4, 4
GC = C // GROUPS
PH = P // GC
M = L // PH
MC = M // P
KC = L // P
B, SPB = 8, N // 8
NL, R = 16, 32
NJ = NL * R // P
HALF = L // 2
NE = 8
BOT, RD, NS, VB, UH = 64, 48, 512, 128, 512
TAU_LOW, TAU_HIGH, EARLY_EXIT = 0.5, 2.0, 0.05
STEPS = 8
GSTEPS, GHALF = 10, 6
FAR = -3.0e38
BANK = 512

F32 = mybir.dt.float32
F32R = mybir.dt.float32r
ALU = mybir.AluOpType
ACT = mybir.ActivationFunctionType
AX_X = mybir.AxisListType.X


class Places:

    def __init__(self, nc, ctx, stage):
        self.nc, self.ctx, self.stage = nc, ctx, stage

    def sb(self, name, shape, dt=F32):
        return self.ctx.enter_context(self.nc.sbuf_tensor(f"{self.stage}_{name}", shape, dt))

    def sem(self, name):
        return self.ctx.enter_context(self.nc.semaphore(f"{self.stage}_{name}"))


def load_taps(sp, a, taps, taps_in):
    for p in range(PH):
        for q in range(PH):
            for s in (-1, 0, 1):
                k = PH * s + p - q + PAD
                if 0 <= k < TAPS:
                    sp.dma_start(taps[p * GC:(p + 1) * GC, s + 1, :, q * GC:(q + 1) * GC],
                                 a["taps"][k]).then_inc(taps_in, 16)


def load_x(sp, a, xb, x_in, n, u):
    sp.dma_start(xb[u % 2][:, :, 1:M + 1],
                 a["xph"][n].rearrange("p (g m) -> p g m", g=GROUPS)).then_inc(x_in[u % 2], 16)


def prologue(nc, ps, a, scr, taps, xb, crow_bc):
    PIECE = 4 * BANK
    with ExitStack() as ctx:
        at = Places(nc, ctx, "pro")
        ident = at.sb("ident", [P, P])
        mask = at.sb("mask", [P, R])
        loraA = at.sb("loraA", [P, NJ, L])
        loraB = at.sb("loraB", [P, NJ, L])
        aout = at.sb("aout", [P, KC, B, 2 * R])
        avT = at.sb("avT", [P, KC, NS])
        wk = [loraA[0:NE, i, :] for i in range(2)]
        aggst = [loraA[0:N, 2 + i, :] for i in range(2)]
        vpo, rko = loraB[:, 0, 0:NS // P * VB], loraB[0:RD, 1, 0:NS]
        gcol = at.sb("gcol", [P, NJ, B])
        wvd = at.sb("wvd", [P, KC, VB])
        keysT = at.sb("keysT", [BOT, NS])
        wrT = at.sb("wrT", [BOT, RD])
        G = at.sb("G", [P, NJ, B * R])
        condT = at.sb("condT", [P, N])
        cwT = at.sb("cwT", [P, C])
        bias_bc = at.sb("bias_bc", [N, C])
        crow = at.sb("crow", [N, C])
        W0 = at.sb("W0", [P, P])
        W1 = at.sb("W1", [P, P])
        W2 = at.sb("W2", [P, NE])
        b0 = at.sb("b0", [P, 1])
        b1 = at.sb("b1", [P, 1])
        b2_bc = at.sb("b2_bc", [N, NE])
        bias_k = at.sb("bias_k", [NE, C])
        h1 = at.sb("h1", [P, N])
        h2 = at.sb("h2", [P, N])
        lg = at.sb("lg", [N, NE])
        mx = at.sb("mx", [N, 1])
        nmx = at.sb("nmx", [N, 1])
        ex = at.sb("ex", [N, NE])
        sm = at.sb("sm", [N, 1])
        rs = at.sb("rs", [N, 1])
        att = at.sb("att", [N, NE])
        attT = at.sb("attT", [NE, N])
        aggb = at.sb("aggb", [N, C])
        ash = at.sb("ash", [P, KC, R])
        bout = at.sb("bout", [P, 4, L // 2])

        small_in, gate_in, la_in, lb_in, av_in, ash_in, rk_in = (
            at.sem(s) for s in ("small_in", "gate_in", "la_in", "lb_in", "av_in", "ash_in", "rk_in"))
        wk_in = [at.sem(f"wk_in{i}") for i in range(2)]
        zeroed, taps_in, crow_in = at.sem("zeroed"), at.sem("taps_in"), at.sem("crow_in")
        x_in = [at.sem(f"x_in{i}") for i in range(2)]
        vp_mm, vp_ok, rk_mm, rk_ok = (at.sem(s) for s in ("vp_mm", "vp_ok", "rk_mm", "rk_ok"))
        id0, id1, mask_ok, G_ok = (at.sem(s) for s in ("id0", "id1", "mask_ok", "G_ok"))
        mlp_mm, mlp_act, soft, soft_act, crow_mm, crow_ok = (
            at.sem(s) for s in ("mlp_mm", "mlp_act", "soft", "soft_act", "crow_mm", "crow_ok"))
        fa_mm, fa_ok, shared_ok, fb_mm, fb_ok, ag_mm, ag_ok = (
            at.sem(s) for s in ("fa_mm", "fa_ok", "shared_ok", "fb_mm", "fb_ok", "ag_mm", "ag_ok"))
        stored = at.sem("stored")
        bst = at.sem("bst")
        gst = [at.sem(f"gst{i}") for i in range(2)]
        block = ctx.enter_context(nc.Block())

        @block.sync
        def _(sp):
            small = [(condT[:, :], a["condT"]), (cwT[:, :], a["cwT"]),
                     (bias_bc[:, :], a["conv_bias"].to_broadcast([N, C])),
                     (W0[:, :], a["W0"]), (W1[:, :], a["W1"]), (W2[:, :], a["W2"]),
                     (b0[:, :], a["b0"].unsqueeze(1)), (b1[:, :], a["b1"].unsqueeze(1)),
                     (b2_bc[:, :], a["b2"].to_broadcast([N, NE])),
                     (bias_k[:, :], a["bias_k"])]
            sp.dma_start(gcol[:, :, :], a["gate_rows"].rearrange("(j p) b -> p j b", p=P)).then_inc(gate_in, 16)
            for j in range(NJ):
                sp.dma_start(loraA[:, j, :], a["loraA"][j * P:(j + 1) * P, :]).then_inc(la_in, 16)
            for dst, src in small:
                sp.dma_start(dst, src).then_inc(small_in, 16)
            sp.dma_start(ash[:, :, :].rearrange("p (c q) r -> p c q r", q=PH),
                         a["laS"].rearrange("(c m q) r -> m c q r", m=P, q=PH)).then_inc(ash_in, 16)
            sp.dma_start(loraB[:, :, :], a["loraB"].rearrange("(j p) l -> p j l", p=P)).then_inc(lb_in, 16)
            sp.dma_start(keysT[:, :], a["keysT"]).then_inc(rk_in, 16)
            sp.dma_start(wrT[:, :], a["wrT"]).then_inc(rk_in, 16)
            sp.wait_ge(crow_ok, 1)
            sp.dma_start(scr["crow"], crow[:, :]).then_inc(stored, 16)
            sp.dma_start(avT[:, :, :], a["avT"].rearrange("(k p) n -> p k n", p=P)).then_inc(av_in, 16)
            sp.dma_start(wvd[:, :, :], a["wvdT"].rearrange("(k p) v -> p k v", p=P)).then_inc(av_in, 16)
            sp.wait_ge(zeroed, 3)
            load_taps(sp, a, taps, taps_in)
            sp.wait_ge(stored, 16)
            sp.dma_start(crow_bc[:, :, :], scr["crow"].unsqueeze(0).to_broadcast([P, N, C])).then_inc(crow_in, 16)
            sp.wait_ge(fa_mm, KC)
            for t in range(2):
                sp.dma_start(wk[t], a["wk"][:, t * PIECE:(t + 1) * PIECE]).then_inc(wk_in[t], 16)
            sp.wait_ge(fa_ok, KC)
            sp.wait_ge(shared_ok, B)
            for b in range(B):
                sp.dma_start(scr["la"][b], aout[:, :, b, :]).then_inc(stored, 16)
            sp.wait_ge(soft, 9)
            sp.dma_start(scr["aggb"], aggb[:, :]).then_inc(stored, 16)
            sp.wait_ge(rk_ok, 1)
            sp.dma_start(scr["rkT"], rko).then_inc(stored, 16)
            sp.wait_ge(vp_ok, 1)
            sp.dma_start(scr["vp"], vpo).then_inc(stored, 16)
            for u in range(2):
                load_x(sp, a, xb, x_in, u, u)
            for t in range(C * C // PIECE):
                sp.wait_ge(ag_ok, 4 * (t + 1))
                sp.dma_start(scr["agg"][:, t * PIECE:(t + 1) * PIECE], aggst[t % 2]).then_inc(gst[t % 2], 16)
                if t + 2 < C * C // PIECE:
                    sp.dma_start(wk[t % 2], a["wk"][:, (t + 2) * PIECE:(t + 3) * PIECE]).then_inc(wk_in[t % 2], 16)
            sp.wait_ge(stored, 16 * (B + 4))
            sp.wait_ge(taps_in, 16 * TAPS * PH)
            sp.wait_ge(crow_in, 16)
            sp.wait_ge(bst, 64)
            for i in range(2):
                sp.wait_ge(x_in[i], 16)
                sp.wait_ge(gst[i], 64)

        @block.gpsimd
        def _(pool):
            pool.memset(ident[:, :], 0.0).then_inc(id0, 1)
            pool.wait_ge(id0, 1)
            pool.affine_select(out=ident[:, :], in_=ident[:, :], compare_op=ALU.not_equal, fill=1.0,
                               base=0, pattern=[[-1, P]], channel_multiplier=1).then_inc(id1, 1)

        @block.scalar
        def _(act):
            act.wait_ge(mlp_mm, 1)
            act.activation(h1[:, :], ps[0][:, 0:N], ACT.Gelu, bias=b0[:, 0:1]).then_inc(mlp_act, 1)
            act.wait_ge(mlp_mm, 2)
            act.activation(h2[:, :], ps[1][:, 0:N], ACT.Gelu, bias=b1[:, 0:1]).then_inc(mlp_act, 1)
            act.wait_ge(soft, 3)
            act.activation(ex[:, :], lg[:, :], ACT.Exp, bias=nmx[:, 0:1]).then_inc(soft_act, 1)
            lb = scr["lb"].rearrange("b r l -> (b r) l")
            for t in range(4):
                act.wait_ge(fb_ok, 2 * (t + 1))
                act.dma_start(lb[(t // 2) * P:(t // 2 + 1) * P, (t % 2) * (L // 2):(t % 2 + 1) * (L // 2)],
                              bout[:, t, :]).then_inc(bst, 16)

        @block.tensor
        def _(pe):
            def lora_a(kc):
                if kc >= 2:
                    pe.wait_ge(fa_ok, kc - 1)
                mc, q = divmod(kc, PH)
                for j in range(NJ):
                    lhs = loraA[:, j, :].rearrange("p (c m q) -> p c q m", m=P, q=PH)[:, mc, q, :]
                    mm = pe.matmul(ps[4 + kc % 2][:, 0:B * R], lhs, G[:, j, :], start=(j == 0), stop=(j == NJ - 1))
                mm.then_inc(fa_mm, 1)

            pe.wait_ge(small_in, 160)
            pe.matmul(ps[0][:, 0:N], W0[:, :], condT[:, :], start=True, stop=True).then_inc(mlp_mm, 1)
            pe.matmul(ps[2][0:N, 0:C], condT[:, :], cwT[:, :], start=True, stop=True).then_inc(crow_mm, 1)
            pe.wait_ge(mlp_act, 1)
            pe.matmul(ps[1][:, 0:N], W1[:, :], h1[:, :], start=True, stop=True).then_inc(mlp_mm, 1)
            pe.wait_ge(mlp_act, 2)
            pe.matmul(ps[3][0:N, 0:NE], h2[:, :], W2[:, :], start=True, stop=True).then_inc(mlp_mm, 1)
            pe.wait_ge(G_ok, NJ)
            pe.wait_ge(la_in, 16 * NJ)
            for kc in range(KC):
                lora_a(kc)
            pe.wait_ge(lb_in, 16)
            for t in range(8):
                if t >= 2:
                    pe.wait_ge(fb_ok, t - 1)
                for j in range(NJ):
                    mm = pe.matmul(ps[6 + t % 2][:, :], G[:, j, (t // 4) * P:(t // 4 + 1) * P],
                                   loraB[:, j, (t % 4) * BANK:(t % 4 + 1) * BANK],
                                   start=(j == 0), stop=(j == NJ - 1))
                mm.then_inc(fb_mm, 1)
            pe.wait_ge(soft, 7)
            pe.transpose(ps[0][0:NE, 0:N], att[:, :], ident[0:N, 0:N]).then_inc(mlp_mm, 1)
            pe.wait_ge(soft, 8)
            pe.matmul(ps[1][0:N, 0:C], attT[:, :], bias_k[:, :], start=True, stop=True).then_inc(mlp_mm, 1)
            pe.wait_ge(rk_in, 32)
            pe.wait_ge(fa_ok, KC)
            pe.matmul(ps[4][0:RD, :], wrT[:, :], keysT[:, :], start=True, stop=True).then_inc(rk_mm, 1)
            pe.wait_ge(av_in, 32)
            for c in range(NS // P):
                for k in range(KC):
                    mm = pe.matmul(ps[5][:, c * VB:(c + 1) * VB], avT[:, k, c * P:(c + 1) * P], wvd[:, k, :],
                                   start=(k == 0), stop=(k == KC - 1))
            mm.then_inc(vp_mm, 1)
            for t in range(C * C // BANK):
                if t % 4 == 0:
                    pe.wait_ge(wk_in[(t // 4) % 2], 16 * (t // 8 + 1))
                if t >= 2:
                    pe.wait_ge(ag_ok, t - 1)
                pe.matmul(ps[2 + t % 2][0:N, :], attT[:, :], wk[(t // 4) % 2][:, (t % 4) * BANK:(t % 4 + 1) * BANK],
                          start=True, stop=True).then_inc(ag_mm, 1)

        @block.vector
        def _(dve):
            dve.wait_ge(id1, 1)
            dve.tensor_reduce(mask[:, :], ident[:, :].rearrange("p (n r) -> p r n", r=R), AX_X,
                              ALU.add).then_inc(mask_ok, 1)
            dve.wait_ge(mask_ok, 1)
            dve.wait_ge(gate_in, 16)
            for j in range(NJ):
                dve.tensor_tensor(G[:, j, :].rearrange("p (b r) -> p b r", r=R),
                                  gcol[:, j, :].unsqueeze(2).to_broadcast([P, B, R]),
                                  mask[:, :].unsqueeze(1).to_broadcast([P, B, R]), ALU.mult).then_inc(G_ok, 1)
            dve.wait_ge(crow_mm, 1)
            dve.tensor_tensor(crow[:, :], ps[2][0:N, 0:C], bias_bc[:, :], ALU.add).then_inc(crow_ok, 1)
            dve.memset(taps[:, :, :, :], 0.0).then_inc(zeroed, 1)
            for i in range(2):
                dve.memset(xb[i][:, :, 0:M + 2:M + 1], 0.0).then_inc(zeroed, 1)
            dve.wait_ge(mlp_mm, 3)
            dve.tensor_tensor(lg[:, :], ps[3][0:N, 0:NE], b2_bc[:, :], ALU.add).then_inc(soft, 1)
            dve.wait_ge(soft, 1)
            dve.tensor_reduce(mx[:, :], lg[:, :], AX_X, ALU.max).then_inc(soft, 1)
            dve.wait_ge(soft, 2)
            dve.tensor_scalar(nmx[:, :], mx[:, :], -1.0, None, ALU.mult).then_inc(soft, 1)
            dve.wait_ge(soft_act, 1)
            dve.tensor_reduce(sm[:, :], ex[:, :], AX_X, ALU.add).then_inc(soft, 1)
            dve.wait_ge(soft, 4)
            dve.reciprocal(rs[:, :], sm[:, :]).then_inc(soft, 1)
            dve.wait_ge(soft, 5)
            dve.tensor_scalar(att[:, :], ex[:, :], rs[:, 0:1], None, ALU.mult).then_inc(soft, 2)
            dve.wait_ge(ash_in, 16)
            for b in range(B):
                dve.tensor_copy(aout[:, :, b, R:2 * R], ash[:, :, :]).then_inc(shared_ok, 1)
            for kc in range(KC):
                dve.wait_ge(fa_mm, kc + 1)
                dve.tensor_copy(aout[:, kc, :, 0:R],
                                ps[4 + kc % 2][:, 0:B * R].rearrange("p (b r) -> p b r", r=R)).then_inc(fa_ok, 1)
            for t in range(8):
                dve.wait_ge(fb_mm, t + 1)
                dve.tensor_copy(bout[:, t // 2, (t % 2) * BANK:(t % 2 + 1) * BANK],
                                ps[6 + t % 2][:, :]).then_inc(fb_ok, 1)
            dve.wait_ge(mlp_mm, 4)
            dve.tensor_copy(attT[:, :], ps[0][0:NE, 0:N]).then_inc(soft, 1)
            dve.wait_ge(mlp_mm, 5)
            dve.tensor_copy(aggb[:, :], ps[1][0:N, 0:C]).then_inc(soft, 1)
            dve.wait_ge(rk_mm, 1)
            dve.tensor_copy(rko, ps[4][0:RD, :]).then_inc(rk_ok, 1)
            dve.wait_ge(vp_mm, 1)
            dve.tensor_copy(vpo, ps[5][:, :]).then_inc(vp_ok, 1)
            for t in range(C * C // BANK):
                dve.wait_ge(ag_mm, t + 1)
                if t // 4 >= 2:
                    dve.wait_ge(gst[(t // 4) % 2], 16 * (t // 8))
                dve.tensor_copy(aggst[(t // 4) % 2][:, (t % 4) * BANK:(t % 4 + 1) * BANK],
                                ps[2 + t % 2][0:N, :]).then_inc(ag_ok, 1)


def kernel_chunks(a, half):
    rows = a["kernel"].rearrange("(c m q) d -> c q m d", m=P, q=PH)
    return rows[:, :, :, half * HALF:(half + 1) * HALF]


def convolve(nc, ps, a, scr, khi, klo, kraw, taps, xb, crow_bc):
    BODY = 2 * SPB
    AHEAD = SPB
    with ExitStack() as ctx:
        at = Places(nc, ctx, "conv")
        ct = [at.sb(f"ct{i}", [P, KC, C]) for i in range(2)]
        la = [at.sb(f"la{i}", [P, KC, 2 * R]) for i in range(2)]
        axs = [at.sb(f"axs{i}", [2 * R, P]) for i in range(2)]

        k_in = [at.sem(f"k_in{i}") for i in range(2)]
        k_hi, k_lo = at.sem("k_hi"), at.sem("k_lo")
        x_in = [at.sem(f"x_in{i}") for i in range(2)]
        la_in = [at.sem(f"la_in{i}") for i in range(2)]
        conv_mm = at.sem("conv_mm")
        conv_out = at.sem("conv_out")
        ax_mm = at.sem("ax_mm")
        ax_out = at.sem("ax_out")
        ct_st = [at.sem(f"ct_st{i}") for i in range(2)]
        ax_st = [at.sem(f"ax_st{i}") for i in range(2)]
        block = ctx.enter_context(nc.Block())

        @block.sync
        def _(sp):
            with sp.Fori(1, N // 2) as i:
                for u in range(2):
                    sp.wait_ge(conv_mm, MC * (2 * i + u - 1))
                    load_x(sp, a, xb, x_in, 2 * i + u, u)
            for i in range(2):
                sp.wait_ge(ct_st[i], 16 + 16 * N // 2)
                sp.wait_ge(ax_st[i], 16 + 16 * N // 2)

        @block.gpsimd
        def _(pool):
            kern = kernel_chunks(a, 0)
            with pool.Fori(0, B // 2) as i:
                for u in range(2):
                    pool.wait_ge(ax_mm, SPB * (2 * i + u - 1) + AHEAD)
                    pool.dma_start(la[u][:, :, :], scr["la"][2 * i + u]).then_inc(la_in[u], 16)
                    for v in range(2):
                        pool.wait_ge(k_lo, PH * i + 2 * u + v + 1)
                        pool.dma_start(kraw[:, PH * i + 2 * u + v, :], kern[i, 2 * u + v]).then_inc(k_in[v], 16)

        @block.tensor
        def _(pe):
            pe.sem_inc(ax_mm, AHEAD)
            for i in range(2):
                pe.sem_inc(x_in[i], 16)
            with pe.Fori(0, N // BODY) as i:
                for u in range(BODY):
                    n = BODY * i + u
                    pe.wait_ge(x_in[u % 2], 16 * (BODY // 2 * i + u // 2 + 1))
                    for mc in range(MC):
                        pe.wait_ge(conv_out, MC * n + mc + 1)
                        for g in range(GROUPS):
                            for s in range(3):
                                mm = pe.matmul(ps[mc][:, g * P:(g + 1) * P],
                                               xb[u % 2][:, g, P * mc + s:P * (mc + 1) + s],
                                               taps[:, s, g, :], start=(s == 0), stop=(s == 2))
                        mm.then_inc(conv_mm, 1)
                    if u % SPB == 0:
                        pe.wait_ge(la_in[u // SPB], 16 * (i + 1))
                    pe.wait_ge(ax_out, n + 1)
                    for kc in range(KC):
                        if kc % PH == 0:
                            pe.wait_ge(conv_out, MC + MC * n + kc // PH + 1)
                        mm = pe.matmul(ps[4 + u % 2][0:2 * R, 0:P], la[u // SPB][:, kc, :], ct[u % 2][:, kc, :],
                                       start=(kc == 0), stop=(kc == KC - 1))
                    mm.then_inc(ax_mm, 1)

        @block.vector
        def _(dve):
            dve.sem_inc(conv_out, MC)
            dve.sem_inc(k_lo, 2)
            with dve.Fori(0, N // BODY) as i:
                for u in range(BODY):
                    n = BODY * i + u
                    ctx_row = crow_bc[:, n, :].rearrange("p (g o) -> p g o", g=GROUPS)
                    ctx_row = ctx_row.unsqueeze(2).to_broadcast([P, GROUPS, PH, GC])
                    dve.wait_ge(ax_mm, n - 1 + AHEAD)
                    dve.wait_ge(ct_st[u % 2], 16 * (BODY // 2 * i + u // 2 + 1))
                    for mc in range(MC):
                        dve.wait_ge(conv_mm, MC * n + mc + 1)
                        dst = ct[u % 2][:, PH * mc:PH * (mc + 1), :].rearrange("p q (g o) -> p g q o", g=GROUPS)
                        src = ps[mc][:, :].rearrange("p (g q o) -> p g q o", g=GROUPS, q=PH)
                        dve.tensor_tensor(dst, src, ctx_row, ALU.add).then_inc(conv_out, 1)
                    if u % 2:
                        v = u // 2
                        kc = PH * i + v
                        dve.wait_ge(k_in[v % 2], 16 * (2 * i + v // 2 + 1))
                        dve.tensor_scalar(khi[:, kc, :], kraw[:, kc, :], 1.0, None, ALU.mult).then_inc(k_hi, 1)
                        dve.wait_ge(k_hi, kc + 1)
                        dve.tensor_tensor(klo[:, kc, :], kraw[:, kc, :], khi[:, kc, :].bitcast(F32),
                                          ALU.subtract).then_inc(k_lo, 1)

        @block.scalar
        def _(act):
            act.sem_inc(ax_out, 2)
            for i in range(2):
                act.sem_inc(ct_st[i], 16)
                act.sem_inc(ax_st[i], 16)
            with act.Fori(0, N // 2) as i:
                for u in range(2):
                    n = 2 * i + u
                    act.wait_ge(conv_out, MC + MC * (n + 1))
                    act.dma_start(scr["ct"][n], ct[u][:, :, :].rearrange("p k c -> p (k c)")).then_inc(ct_st[u], 16)
                    act.wait_ge(ax_mm, n + 1 + AHEAD)
                    act.wait_ge(ax_st[u], 16 * (i + 1))
                    act.activation(axs[u][:, :], ps[4 + u][0:2 * R, 0:P], ACT.Copy).then_inc(ax_out, 1)
                    act.wait_ge(ax_out, 2 + n + 1)
                    act.dma_start(scr["ax"][n], axs[u][:, :]).then_inc(ax_st[u], 16)


def project(nc, ps, a, scr, khi, klo, kraw, st_all, raw, wh, wl, wraw):
    AR = 2 * R
    QK = KC // 4
    with ExitStack() as ctx:
        at = Places(nc, ctx, "proj")
        craw = [raw[i][:, :].rearrange("p (k c) -> p k c", c=C) for i in range(2)]
        chi = at.sb("chi", [P, KC, C], F32R)
        clo = at.sb("clo", [P, KC, C], F32R)
        yo = [at.sb(f"yo{i}", [P, HALF]) for i in range(2)]
        yh = at.sb("yh", [P, HALF], F32R)
        yl = at.sb("yl", [P, HALF], F32R)
        zo = at.sb("zo", [P, HALF])
        ag = [at.sb(f"ag{i}", [P, C]) for i in range(2)]
        agh = at.sb("agh", [P, C], F32R)
        agl = at.sb("agl", [P, C], F32R)
        zb = [at.sb(f"zb{i}", [P, 1]) for i in range(2)]
        st = at.sb("st", [P, 2, 6])
        axr = [at.sb(f"axr{i}", [P, P]) for i in range(2)]
        axp = [at.sb(f"axp{i}", [P, P], F32R) for i in range(2)]
        bhi = at.sb("bhi", [P, HALF], F32R)
        blo_at = -(-nc.sbuf_base // 32) * 32
        blo = at.sb("blo", [P, HALF], F32R)
        braw = nc.alloc_sbuf_tensor_at("proj_braw", [P, HALF], F32, offset=blo_at)
        bias = at.sb("bias", [P, HALF])

        k_in = [at.sem(f"k_in{t}") for t in range(KC // 2)]
        k_hi, k_lo = at.sem("k_hi"), at.sem("k_lo")
        w_in = [at.sem(f"w_in{t}") for t in range(KC // 2)]
        w_hi, w_lo, z0_in = at.sem("w_hi"), at.sem("w_lo"), at.sem("z0_in")
        bias_in, biased = at.sem("bias_in"), at.sem("biased")
        c_in = [at.sem(f"c_in{i}") for i in range(2)]
        x_in = [at.sem(f"x_in{i}") for i in range(2)]
        ag_in = [at.sem(f"ag_in{i}") for i in range(2)]
        ax_in = [at.sem(f"ax_in{i}") for i in range(2)]
        b_in = at.sem("b_in")
        c_hi, c_lo = at.sem("c_hi"), at.sem("c_lo")
        ax_hi, ax_lo = at.sem("ax_hi"), at.sem("ax_lo")
        b_hi, b_lo = at.sem("b_hi"), at.sem("b_lo")
        c_used = at.sem("c_used")
        lora_mm = at.sem("lora_mm")
        y_out = at.sem("y_out")
        y_hi, y_lo = at.sem("y_hi"), at.sem("y_lo")
        z_mm = at.sem("z_mm")
        z_out = at.sem("z_out")
        stats, kept = at.sem("stats"), at.sem("kept")
        yz_out = at.sem("yz_out")
        z_st = at.sem("z_st")
        yz_st = [at.sem(f"yz_st{i}") for i in range(2)]
        block = ctx.enter_context(nc.Block())

        def turn_of(half, b, u):
            return N * half + SPB * b + u, N // 2 * half + SPB // 2 * b + u // 2

        def after(half, b, u):
            if u + 1 < SPB:
                return half, b, u + 1
            if isinstance(b, int) and b == B - 1:
                return half + 1, 0, 0
            return half, b + 1, 0

        def before(half, b, u):
            if u:
                return half, b, u - 1
            if isinstance(b, int) and b == 0:
                return half - 1, B - 1, SPB - 1
            return half, b - 1, SPB - 1

        def weights_after(t):
            return (2 * (t + 1) * (UH + BOT) - 1) // (QK * HALF)

        def bodies(eng, body):
            for half in range(2):
                body(half, 0)
                with eng.Fori(1, B - 1) as b:
                    body(half, b)
                body(half, B - 1)

        @block.sync
        def _(sp):
            def load(half, b, u):
                t, t2 = turn_of(half, b, u)
                n = SPB * b + u
                first = half == 0 and isinstance(b, int) and b == 0 and u < 2
                if not first:
                    sp.wait_ge(y_out, 2 + t - 1)
                sp.dma_start(craw[u % 2][:, :, :].rearrange("p k c -> p (k c)"), scr["ct"][n]).then_inc(c_in[u % 2], 16)
                for i in range(2):
                    sp.dma_start(axr[u % 2][i * AR:(i + 1) * AR, :], scr["ax"][n]).then_inc(ax_in[u % 2], 16)
                if not first:
                    sp.wait_ge(yz_st[u % 2], 16 * (t2 + 1))
                sp.dma_start(yo[u % 2][:, :], a["x"][n, :, half * HALF:(half + 1) * HALF]).then_inc(x_in[u % 2], 16)
                sp.dma_start(ag[u % 2][:, :], scr["agg"][n].rearrange("(i o) -> i o", o=C)).then_inc(ag_in[u % 2], 16)
                sp.dma_start(zb[u % 2][:, :], scr["aggb"][n].unsqueeze(1)).then_inc(ag_in[u % 2], 16)

            def body(half, b):
                for u in range(SPB):
                    load(half, b, u)

            bodies(sp, body)
            sp.wait_ge(y_out, 2 + 2 * N - 1)
            sp.wait_ge(z_st, 16 + 16 * (N + 1))
            sp.dma_start(raw[0][:, :], scr["z"][0]).then_inc(z0_in, 16)
            sp.wait_ge(z0_in, 16)
            for i in range(2):
                sp.wait_ge(yz_st[i], 16 + 16 * N)
            sp.wait_ge(z_st, 16 + 16 * 2 * N)

        @block.gpsimd
        def _(pool):
            def load_b(half, b):
                if not (half == 0 and isinstance(b, int)):
                    pool.wait_ge(lora_mm, 2 + N * half + SPB * b)
                cols = slice(half * HALF, (half + 1) * HALF)
                for i in range(2):
                    pool.dma_start(braw[i * AR:i * AR + R, :], scr["lb"][b][:, cols]).then_inc(b_in, 16)
                    pool.dma_start(braw[i * AR + R:(i + 1) * AR, :], a["lbS"][:, cols]).then_inc(b_in, 16)

            def load_bias(half):
                pool.dma_start(bias[:, :], a["ffn_bias"][:, half * HALF:(half + 1) * HALF]
                               .to_broadcast([P, HALF])).then_inc(bias_in, 16)

            load_bias(0)
            load_b(0, 0)
            with pool.Fori(1, B) as b:
                load_b(0, b)
            load_b(1, 0)
            kern = kernel_chunks(a, 1)
            for t in range(KC // 2):
                if t % 2 == 0:
                    pool.wait_ge(c_used, 4 + 4 * (N - 1) + t // 2 + 1)
                mc, q = divmod(2 * t, PH)
                pool.dma_start(kraw[:, 2 * t:2 * t + 2, :],
                               kern[mc, q:q + 2].rearrange("q m d -> m q d")).then_inc(k_in[t], 16)
                if t == 5:
                    pool.wait_ge(biased, N)
                    load_bias(1)
            with pool.Fori(1, B) as b:
                load_b(1, b)
            for t in range(KC // 2):
                pool.wait_ge(c_used, 4 + 4 * (2 * N - 1) + weights_after(t) + 1)
                pool.dma_start(wraw[:, 2 * t:2 * t + 2, :], a["wuq"][2 * t * P:2 * (t + 1) * P, :]
                               .rearrange("(k p) n -> p k n", p=P)).then_inc(w_in[t], 16)

        def weights_high(act, j):
            for t in range(KC // 2):
                if weights_after(t) == j - 1:
                    s = slice(2 * t, 2 * t + 2)
                    act.wait_ge(w_in[t], 16)
                    act.activation(wh[:, s, :], wraw[:, s, :], ACT.Copy).then_inc(w_hi, 1)

        def weights_low(dve, j):
            for t in range(KC // 2):
                if weights_after(t) == j - 1:
                    s = slice(2 * t, 2 * t + 2)
                    dve.wait_ge(w_hi, t + 1)
                    dve.tensor_tensor(wl[:, s, :], wraw[:, s, :], wh[:, s, :].bitcast(F32),
                                      ALU.subtract).then_inc(w_lo, 1)

        def kernel_high(act, j):
            for kc in range(QK * j, QK * (j + 1)):
                if kc % 2 == 0:
                    act.wait_ge(k_in[kc // 2], 16)
                act.activation(khi[:, kc, :], kraw[:, kc, :], ACT.Copy).then_inc(k_hi, 1)

        def kernel_low(dve, j):
            for kc in range(QK * j, QK * (j + 1)):
                dve.wait_ge(k_hi, kc + 1)
                dve.tensor_tensor(klo[:, kc, :], kraw[:, kc, :], khi[:, kc, :].bitcast(F32),
                                  ALU.subtract).then_inc(k_lo, 1)

        def high(act, half, b, u, j):
            t, t2 = turn_of(half, b, u)
            if j == 0:
                act.wait_ge(c_in[u % 2], 16 * (t2 + 1))
            act.wait_ge(c_used, 4 * t + j + 1)
            act.activation(chi[:, QK * j:QK * (j + 1), :], craw[u % 2][:, QK * j:QK * (j + 1), :],
                           ACT.Copy).then_inc(c_hi, 1)
            if j == 1:
                act.wait_ge(ax_in[u % 2], 32 * (t2 + 1))
                act.wait_ge(lora_mm, t + 1)
                act.activation(axp[u % 2][:, :], axr[u % 2][:, :], ACT.Copy).then_inc(ax_hi, 1)
                if u == 0:
                    act.wait_ge(b_in, 64 * (B * half + b + 1))
                    act.wait_ge(lora_mm, 2 + t)
                    act.activation(bhi[:, :], braw[:, :], ACT.Copy).then_inc(b_hi, 1)

        def low(dve, half, b, u, j):
            t, t2 = turn_of(half, b, u)
            s = slice(QK * j, QK * (j + 1))
            dve.wait_ge(c_hi, 4 * t + j + 1)
            dve.tensor_tensor(clo[:, s, :], craw[u % 2][:, s, :], chi[:, s, :].bitcast(F32),
                              ALU.subtract).then_inc(c_lo, 1)
            if j == 1:
                dve.wait_ge(ax_hi, t + 1)
                dve.tensor_tensor(axp[u % 2][AR:P, :], axr[u % 2][AR:P, :], axp[u % 2][AR:P, :].bitcast(F32),
                                  ALU.subtract).then_inc(ax_lo, 1)
                if u == 0:
                    dve.wait_ge(b_hi, B * half + b + 1)
                    dve.tensor_tensor(blo[:, :], braw[:, :], bhi[:, :].bitcast(F32),
                                      ALU.subtract).then_inc(b_lo, 1)

        def x_bias(dve, half, b, u):
            t, t2 = turn_of(half, b, u)
            if u == 0 and isinstance(b, int) and b == 0:
                dve.wait_ge(bias_in, 16 * (half + 1))
            dve.wait_ge(x_in[u % 2], 16 * (t2 + 1))
            dve.tensor_tensor(yo[u % 2][:, :], yo[u % 2][:, :], bias[:, :], ALU.add).then_inc(biased, 1)

        def y_sum(dve, half, b, u):
            t, t2 = turn_of(half, b, u)
            dve.wait_ge(c_used, 4 + 4 * (t + 1))
            dve.wait_ge(biased, t + 1)
            for h in range(2):
                s = slice(h * BANK, (h + 1) * BANK)
                add = dve.tensor_tensor(yo[u % 2][:, s], ps[2 * (u % 2) + h][:, :], yo[u % 2][:, s], ALU.add)
            add.then_inc(y_out, 1)

        def y_high(act, half, b, u):
            t, t2 = turn_of(half, b, u)
            act.wait_ge(z_mm, t + 1)
            act.wait_ge(ag_in[u % 2], 32 * (t2 + 1))
            act.activation(agh[:, :], ag[u % 2][:, :], ACT.Copy)
            act.wait_ge(y_out, 2 + t + 1)
            act.activation(yh[:, :], yo[u % 2][:, :], ACT.Copy).then_inc(y_hi, 1)

        def y_low(dve, half, b, u):
            t, t2 = turn_of(half, b, u)
            dve.wait_ge(y_hi, t + 1)
            dve.tensor_tensor(agl[:, :], ag[u % 2][:, :], agh[:, :].bitcast(F32), ALU.subtract)
            dve.tensor_tensor(yl[:, :], yo[u % 2][:, :], yh[:, :].bitcast(F32), ALU.subtract).then_inc(y_lo, 1)

        def z_copy(act, half, b, u):
            t, t2 = turn_of(half, b, u)
            act.wait_ge(z_st, 16 * (t + 1))
            act.wait_ge(yz_out, t + 2)
            act.wait_ge(z_mm, 1 + t + 1)
            for h in range(2):
                copy = act.activation(zo[:, h * BANK:(h + 1) * BANK], ps[4 + h][:, :], ACT.Identity,
                                      bias=zb[u % 2][:, 0:1])
            copy.then_inc(z_out, 1)
            act.wait_ge(z_out, 1 + t + 1)
            act.dma_start(scr["z"][SPB * b + u, :, half * HALF:(half + 1) * HALF], zo[:, :])\
               .then_inc(z_st, 16)

        def z_use(dve, half, b, u):
            t, t2 = turn_of(half, b, u)
            dve.wait_ge(z_out, 1 + t + 1)
            for h in range(2):
                dve.bn_stats(st[:, h, :], zo[:, h * BANK:(h + 1) * BANK]).then_inc(stats, 1)
            dve.tensor_tensor(yo[u % 2][:, :], yo[u % 2][:, :], zo[:, :], ALU.add).then_inc(yz_out, 1)
            dve.wait_ge(stats, 2 * (t + 1))
            dve.tensor_scalar(st_all[:, SPB * b + u, 12 * half:12 * (half + 1)],
                              st[:, :, :].rearrange("p h s -> p (h s)"), 1.0, None, ALU.mult).then_inc(kept, 1)
            dve.wait_ge(kept, t + 1)

        def yz_store(act, half, b, u):
            t, t2 = turn_of(half, b, u)
            act.wait_ge(yz_out, 2 + t + 1)
            act.dma_start(scr["yz"][SPB * b + u, :, half * HALF:(half + 1) * HALF], yo[u % 2][:, :])\
               .then_inc(yz_st[u % 2], 16)

        def edges(half, b, u):
            first = half == 0 and isinstance(b, int) and b == 0 and u == 0
            last = half == 1 and isinstance(b, int) and b == B - 1 and u == SPB - 1
            seam = half == 0 and isinstance(b, int) and b == B - 1 and u == SPB - 1
            return first, last, seam

        @block.scalar
        def _(act):
            act.sem_inc(z_st, 16)
            for i in range(2):
                act.sem_inc(yz_st[i], 16)
            act.sem_inc(z_out, 1)
            for j in range(4):
                high(act, 0, 0, 0, j)

            def body(half, b):
                for u in range(SPB):
                    first, last, seam = edges(half, b, u)
                    for j in range(4):
                        if j == 0 and not first:
                            y_high(act, *before(half, b, u))
                        if seam:
                            kernel_high(act, j)
                        if not last:
                            high(act, *after(half, b, u), j)
                        elif j:
                            weights_high(act, j)
                        if j == 1 and not first:
                            z_copy(act, *before(half, b, u))
                        if j == 2 and not first:
                            yz_store(act, *before(half, b, u))

            bodies(act, body)
            y_high(act, 1, B - 1, SPB - 1)
            z_copy(act, 1, B - 1, SPB - 1)
            yz_store(act, 1, B - 1, SPB - 1)

        @block.vector
        def _(dve):
            dve.sem_inc(y_out, 2)
            dve.sem_inc(b_lo, 1)
            dve.sem_inc(yz_out, 2)
            for j in range(4):
                low(dve, 0, 0, 0, j)

            def body(half, b):
                for u in range(SPB):
                    first, last, seam = edges(half, b, u)
                    for j in range(4):
                        if j == 0 and not first:
                            y_low(dve, *before(half, b, u))
                        if j == 1 - seam:
                            x_bias(dve, half, b, u)
                        if j == 2 and not first:
                            z_use(dve, *before(half, b, u))
                        if j == 3:
                            y_sum(dve, half, b, u)
                        if seam:
                            kernel_low(dve, j)
                        if not last:
                            low(dve, *after(half, b, u), j)
                        elif j == 1:
                            weights_low(dve, 1)
                        elif j == 3:
                            y_low(dve, half, b, u)
                            weights_low(dve, 2)

            bodies(dve, body)
            z_use(dve, 1, B - 1, SPB - 1)
            weights_low(dve, 3)

        @block.tensor
        def _(pe):
            pe.sem_inc(c_used, 4)
            pe.sem_inc(lora_mm, 2)
            pe.sem_inc(z_mm, 1)

            def z_of(half, b, u):
                t, t2 = turn_of(half, b, u)
                pe.wait_ge(z_out, t + 1)
                pe.wait_ge(y_lo, t + 1)
                for lhs, parts in ((agh, (yh, yl)), (agl, (yh,))):
                    for h in range(2):
                        for rhs in parts:
                            mm = pe.matmul(ps[4 + h][:, :], lhs[:, :], rhs[:, h * BANK:(h + 1) * BANK],
                                           start=(lhs is agh and rhs is yh), stop=(lhs is agl))
                mm.then_inc(z_mm, 1)

            def turn(half, b, u):
                t, t2 = turn_of(half, b, u)
                first, last, seam = edges(half, b, u)
                after_seam = half == 1 and isinstance(b, int) and b == 0 and u == 0
                out = [ps[2 * (u % 2) + h] for h in range(2)]
                pe.wait_ge(y_out, t + 1)
                for j in range(4):
                    if after_seam:
                        pe.wait_ge(k_lo, QK * (j + 1))
                    pe.wait_ge(c_lo, 4 * t + j + 1)
                    for kc in range(QK * j, QK * (j + 1)):
                        for lhs, parts in ((chi, (khi, klo)), (clo, (khi,))):
                            for h in range(2):
                                for rhs in parts:
                                    mm = pe.matmul(out[h][:, :], lhs[:, kc, :],
                                                   rhs[:, kc, h * BANK:(h + 1) * BANK],
                                                   start=(kc == 0 and lhs is chi and rhs is khi),
                                                   stop=(kc == KC - 1 and lhs is clo))
                    mm.then_inc(c_used, 1)
                    if j == (2 if after_seam else 0) and not first:
                        z_of(*before(half, b, u))
                    if j == 1:
                        pe.wait_ge(ax_lo, t + 1)
                        pe.wait_ge(b_lo, B * half + b + 2)
                        for h in range(2):
                            for rhs in (bhi, blo):
                                mm = pe.matmul(out[h][:, :], axp[u % 2][:, :], rhs[:, h * BANK:(h + 1) * BANK],
                                               start=False, stop=False)
                        mm.then_inc(lora_mm, 1)

            def body(half, b):
                for u in range(SPB):
                    turn(half, b, u)

            bodies(pe, body)
            z_of(1, B - 1, SPB - 1)


def attend(nc, ps, a, scr, st_all, z, wh, wl, zh, zl, vh, vl, vraw, out):
    T4 = KC // 4
    HP = P // 2
    HW = (UH + BOT) // 2
    t_ps, o_ps, u_ps, s_ps, a_ps = ps[0:2], ps[2:4], ps[4:6], ps[6], ps[7]
    Q, RQ = slice(0, P), slice(P, 2 * P)
    with ExitStack() as ctx:
        at = Places(nc, ctx, "att")
        ident = at.sb("ident", [P, P])
        vp = at.sb("vp", [P, NS // P, VB])
        keysT = at.sb("keysT", [P, NS])
        kh = at.sb("kh", [P, NS], F32R)
        kl = at.sb("kl", [P, NS], F32R)
        wrT = at.sb("wrT", [BOT, P])
        rkT = at.sb("rkT", [P, NS])
        rkh = at.sb("rkh", [P, NS], F32R)
        rkl = at.sb("rkl", [P, NS], F32R)
        lrel = at.sb("lrel", [P, NS])
        bu1 = at.sb("bu1", [P, UH])
        wu2 = at.sb("wu2", [P, UH])
        cst = at.sb("cst", [P, 3])
        half = at.sb("half", [P, 3])
        mv = at.sb("mv", [P, N, 2])
        logv = at.sb("logv", [P, N])
        lsum = at.sb("lsum", [P, 1])
        total = at.sb("total", [P, 1])
        mean = at.sb("mean", [P, 1])
        rmean = at.sb("rmean", [P, 1])
        nv = at.sb("nv", [P, N])
        yz = [at.sb(f"yz{i}", [P, L]) for i in range(2)]
        q = at.sb("q", [P, 2, BOT])
        qT = at.sb("qT", [P, P])
        qp = at.sb("qp", [P, P], F32R)
        rqp = at.sb("rqp", [P, P], F32R)
        sc = at.sb("sc", [P, NS])
        rest = at.sb("rest", [P, NS])
        out_of = at.sb("out_of", [P, NS])
        top = at.sb("top", [P, 8])
        lg = at.sb("lg", [P, NS])
        lgm = at.sb("lgm", [P, NS])
        mx = at.sb("mx", [P, 1])
        nmx = at.sb("nmx", [P, 1])
        ex = at.sb("ex", [P, NS])
        exT = at.sb("exT", [P, NS])
        esum = at.sb("esum", [P, 1])
        ub = at.sb("ub", [P, UH])
        ug = at.sb("ug", [P, UH])
        learned = at.sb("learned", [P, 1])
        g = [at.sb(f"g{i}", [P, 1]) for i in range(12)]
        rh = at.sb("rh", [P, P], F32R)
        rl = at.sb("rl", [P, P], F32R)

        SMALL = 13
        id0, id1, small_in, zeroed = (at.sem(s) for s in ("id0", "id1", "small_in", "zeroed"))
        v_in, v_hi, v_lo = at.sem("v_in"), at.sem("v_hi"), at.sem("v_lo")
        var_ok, log_ok, tot_ok, mean_ok, half_ok = (at.sem(s) for s in ("var_ok", "log_ok", "tot_ok", "mean_ok", "half_ok"))
        z_in = [at.sem(f"z_in{i}") for i in range(2)]
        yz_in = [at.sem(f"yz_in{i}") for i in range(2)]
        t_mm, z_hi, z_lo = at.sem("t_mm"), at.sem("z_hi"), at.sem("z_lo")
        u_mm, u_add, u_act, u_sum = (at.sem(s) for s in ("u_mm", "u_add", "u_act", "u_sum"))
        key_hi, q_hi, q_lo, rq_lo = (at.sem(s) for s in ("key_hi", "q_hi", "q_lo", "rq_lo"))
        q_ok, q_mm, q_out, rq_mm, rq_out, s_mm, a_mm = (
            at.sem(s) for s in ("q_ok", "q_mm", "q_out", "rq_mm", "rq_out", "s_mm", "a_mm"))
        step = at.sem("step")
        gst = at.sem("gst")
        g_t1, g_t2 = at.sem("g_t1"), at.sem("g_t2")
        e_out = at.sem("e_out")
        e_mm, e_cp, r_mm, r_hi, r_lo = (at.sem(s) for s in ("e_mm", "e_cp", "r_mm", "r_hi", "r_lo"))
        o_mm, o_add = at.sem("o_mm"), at.sem("o_add")
        o_st = [at.sem(f"o_st{i}") for i in range(2)]
        block = ctx.enter_context(nc.Block())

        @block.sync
        def _(sp):
            sp.dma_start(z[1][:, :], scr["z"][1]).then_inc(z_in[1], 16)
            sp.dma_start(vraw[:, :], a["wvuT"]).then_inc(v_in, 16)
            with sp.Fori(1, N // 2) as i:
                for u in range(2):
                    n = 2 * i + u
                    sp.wait_ge(t_mm, 4 * (n - 1))
                    sp.dma_start(z[u][:, :], scr["z"][n]).then_inc(z_in[u], 16)
            for i in range(2):
                sp.wait_ge(o_st[i], 16 + 16 * N // 2)

        @block.gpsimd
        def _(pool):
            pool.memset(ident[:, :], 0.0).then_inc(id0, 1)
            pool.wait_ge(id0, 1)
            pool.affine_select(out=ident[:, :], in_=ident[:, :], compare_op=ALU.not_equal, fill=1.0,
                               base=0, pattern=[[-1, P]], channel_multiplier=1).then_inc(id1, 1)
            small = [(bu1[:, :], a["bu1"].to_broadcast([P, UH])),
                     (wu2[:, :], a["wu2"].to_broadcast([P, UH]))]
            small += [(cst[:, k:k + 1], a[name].to_broadcast([P, 1]))
                      for k, name in enumerate(("bu2", "gate_w1", "gate_bias"))]
            small += [(keysT[i * HP:i * HP + BOT, :], a["keysT"]) for i in range(2)]
            small += [(rkT[i * HP:i * HP + RD, :], scr["rkT"]) for i in range(2)]
            small += [(wrT[:, i * HP:i * HP + RD], a["wrT"]) for i in range(2)]
            small += [
                      (lrel[:, :], a["log_rel"].to_broadcast([P, NS])),
                      (vp[:, :, :].rearrange("p c v -> p (c v)"), scr["vp"])]
            pool.wait_ge(zeroed, 2)
            for dst, src in small:
                pool.dma_start(dst, src).then_inc(small_in, 16)
            pool.wait_ge(log_ok, 1)
            pool.partition_all_reduce(total[:, :], lsum[:, :], P, bass.bass_isa.ReduceOp.add).then_inc(tot_ok, 1)
            for u in range(2):
                pool.dma_start(yz[u][:, :], scr["yz"][u]).then_inc(yz_in[u], 16)
            with pool.Fori(1, N // 2) as i:
                for u in range(2):
                    pool.wait_ge(o_st[u], 16 * (i + 1))
                    pool.dma_start(yz[u][:, :], scr["yz"][2 * i + u]).then_inc(yz_in[u], 16)

        @block.tensor
        def _(pe):
            pe.sem_inc(z_in[0], 16)
            pe.wait_ge(id1, 1)

            def turn(n, i, u, j, first=False):
                if j == 0:
                    pe.wait_ge(z_in[u], 16 * (i + 1))
                if not (first and j < 2):
                    pe.wait_ge(z_lo, 4 * n + j - 1)
                for k in range(4):
                    mm = pe.transpose(t_ps[j % 2][:, k * P:(k + 1) * P],
                                      z[u][:, (4 * j + k) * P:(4 * j + k + 1) * P], ident[:, :])
                mm.then_inc(t_mm, 1)

            def heads(n, j, first):
                if j == 0 and not first:
                    pe.wait_ge(u_add, n)
                pe.wait_ge(z_lo, 4 * n + j + 1)
                for k in range(T4 * j, T4 * (j + 1)):
                    for lhs, parts in ((zh, (wh, wl)), (zl, (wh,))):
                        for w in parts:
                            for h in range(2):
                                mm = pe.matmul(u_ps[h][:, 0:HW], lhs[:, k, :], w[:, k, h * HW:(h + 1) * HW],
                                               start=(k == 0 and lhs is zh and w is wh),
                                               stop=(k == KC - 1 and lhs is zl))
                mm.then_inc(u_mm, 1)

            def query(n, first):
                if not first:
                    pe.wait_ge(e_cp, n)
                pe.wait_ge(q_ok, n + 1)
                pe.transpose(s_ps[:, Q], q[:, :, :].rearrange("p i b -> p (i b)"), ident[:, :]).then_inc(q_mm, 1)

            def router_query(n):
                pe.wait_ge(q_out, n + 1)
                pe.matmul(s_ps[:, RQ], wrT[:, :], qT[0:BOT, :], start=True, stop=True).then_inc(rq_mm, 1)

            def scores(n, first):
                if not first:
                    pe.wait_ge(r_lo, n)
                pe.wait_ge(q_lo, n + 1)
                for keys in (kh, kl):
                    mm = pe.matmul(a_ps[:, :], qp[:, :], keys[:, :], start=(keys is kh), stop=(keys is kl))
                mm.then_inc(a_mm, 1)
                pe.wait_ge(rq_lo, n + 1)
                for keys in (rkh, rkl):
                    mm = pe.matmul(s_ps[:, :], rqp[:, :], keys[:, :], start=(keys is rkh), stop=(keys is rkl))
                mm.then_inc(s_mm, 1)

            def turn_e(n):
                pe.wait_ge(step, STEPS * n + 1)
                pe.wait_ge(e_out, n + 2)
                for k in range(4):
                    mm = pe.transpose(s_ps[:, k * P:(k + 1) * P], ex[:, k * P:(k + 1) * P], ident[:, :])
                mm.then_inc(e_mm, 1)

            def read(n):
                pe.wait_ge(step, STEPS * n + 2)
                pe.wait_ge(e_cp, n + 1)
                for k in range(4):
                    mm = pe.matmul(a_ps[:, 0:P], vp[:, k, :], exT[:, k * P:(k + 1) * P], start=(k == 0), stop=(k == 3))
                mm.then_inc(r_mm, 1)

            def expand(n, hs):
                pe.wait_ge(r_lo, n + 1)
                for h in hs:
                    pe.wait_ge(o_add, 4 * n + h + 1)
                    s = slice(h * BANK, (h + 1) * BANK)
                    for k, (lhs, w) in enumerate(((rh, vh), (rh, vl), (rl, vh))):
                        mm = pe.matmul(o_ps[h % 2][:, :], lhs[:, :], w[:, s], start=(k == 0), stop=(k == 2))
                    mm.then_inc(o_mm, 1)

            def sample(n, i, w, first=False, last=False):
                here = 0 if first else i - 1 + w if not isinstance(i, int) else N // 2 - 1
                heads(n, 0, first)
                turn(n, here, 1 - w, 2)
                heads(n, 1, first)
                turn(n, here, 1 - w, 3)
                if not first:
                    turn_e(n - 1)
                heads(n, 2, first)
                if not first:
                    read(n - 1)
                heads(n, 3, first)
                if not last:
                    turn(n + 1, i, w, 0)
                if not first:
                    expand(n - 1, (0,))
                if first:
                    pe.wait_ge(small_in, 16 * SMALL)
                query(n, first)
                if not last:
                    turn(n + 1, i, w, 1)
                router_query(n)
                if not first:
                    expand(n - 1, (1,))
                scores(n, first)
                if not first:
                    expand(n - 1, (2, 3))

            turn(0, 0, 0, 0, first=True)
            turn(0, 0, 0, 1, first=True)
            sample(0, 0, 1, first=True)
            with pe.Fori(1, N // 2) as i:
                sample(2 * i - 1, i, 0)
                sample(2 * i, i, 1)
            sample(N - 1, N // 2, 0, last=True)
            turn_e(N - 1)
            read(N - 1)
            expand(N - 1, range(4))

        @block.scalar
        def _(act):
            for i in range(2):
                act.sem_inc(o_st[i], 16)
            act.sem_inc(e_out, 1)
            def high(n, j, first=False):
                act.wait_ge(t_mm, 4 * n + j + 1)
                if not first:
                    act.wait_ge(u_mm, 4 * (n - 1) + j + 1)
                act.activation(zh[:, T4 * j:T4 * (j + 1), :],
                               t_ps[j % 2][:, :].rearrange("p (k c) -> p k c", c=P), ACT.Copy).then_inc(z_hi, 1)

            def numerators(n):
                act.wait_ge(step, STEPS * (n + 1))
                act.activation(ex[:, :], lgm[:, :], ACT.Exp, bias=nmx[:, 0:1],
                               accum_out=esum[:, 0:1]).then_inc(e_out, 1)

            def copy_e(n):
                act.wait_ge(e_mm, n + 1)
                act.activation(exT[:, :], s_ps[:, :], ACT.Copy).then_inc(e_cp, 1)

            def gate_1(n):
                act.wait_ge(u_sum, n + 1)
                act.activation(g[0][:, :], learned[:, :], ACT.Tanh, scale=0.5, bias=half[:, 0:1]).then_inc(g_t1, 1)

            def gate_2(n):
                act.wait_ge(gst, GSTEPS * n + GHALF)
                act.activation(g[7][:, :], g[6][:, :], ACT.Tanh, scale=half[:, 1:2], bias=half[:, 2:3]).then_inc(g_t2, 1)

            def read_high(n):
                act.wait_ge(r_mm, n + 1)
                act.activation(rh[:, :], a_ps[:, 0:P], ACT.Copy).then_inc(r_hi, 1)

            def store(n, u):
                act.wait_ge(o_add, 2 + 4 * (n + 1))
                act.dma_start(out[n], yz[u][:, :]).then_inc(o_st[u], 16)

            def after_heads(n, w, first=False, last=False):
                if not last:
                    high(n + 1, 0)
                act.wait_ge(q_mm, n + 1)
                if not first:
                    act.wait_ge(s_mm, n)
                act.activation(qT[:, :], s_ps[:, Q], ACT.Copy).then_inc(q_out, 1)
                act.wait_ge(q_out, n + 1)
                act.activation(qp[:, :], qT[:, :], ACT.Copy).then_inc(q_hi, 1)
                act.wait_ge(rq_mm, n + 1)
                act.activation(rqp[:, :], s_ps[:, RQ], ACT.Copy).then_inc(rq_out, 1)
                if not last:
                    high(n + 1, 1)
                if first:
                    act.wait_ge(v_in, 16)
                    act.activation(vh[:, :], vraw[:, :], ACT.Copy).then_inc(v_hi, 1)
                act.wait_ge(u_add, n + 1)
                if not first:
                    act.wait_ge(u_sum, n)
                act.activation(ug[:, :], ub[:, :], ACT.Gelu_apprx_tanh).then_inc(u_act, 1)
                if not last:
                    high(n + 1, 2)
                numerators(n)
                if not last:
                    high(n + 1, 3)
                copy_e(n)
                if not first:
                    store(n - 1, w)
                gate_1(n)
                if not first:
                    act.wait_ge(o_mm, 4 * n)
                read_high(n)
                gate_2(n)

            high(0, 0, first=True)
            high(0, 1, first=True)
            high(0, 2, first=True)
            high(0, 3, first=True)
            act.wait_ge(var_ok, N)
            act.activation(logv[:, :], mv[:, :, 1], ACT.Ln, bias=1.0, accum_out=lsum[:, :]).then_inc(log_ok, 1)
            act.wait_ge(small_in, 16 * SMALL)
            act.activation(kh[:, :], keysT[:, :], ACT.Copy).then_inc(key_hi, 1)
            act.activation(rkh[:, :], rkT[:, :], ACT.Copy).then_inc(key_hi, 1)
            act.wait_ge(half_ok, 1)
            after_heads(0, 1, first=True)
            with act.Fori(1, N // 2) as i:
                after_heads(2 * i - 1, 0)
                after_heads(2 * i, 1)
            after_heads(N - 1, 0, last=True)
            store(N - 1, 1)

        @block.vector
        def _(dve):
            dve.memset(wrT[:, :], 0.0).then_inc(zeroed, 1)
            dve.memset(rkT[:, :], 0.0).then_inc(zeroed, 1)
            dve.sem_inc(o_add, 2)

            def low(n, j):
                dve.wait_ge(z_hi, 4 * n + j + 1)
                s = slice(T4 * j, T4 * (j + 1))
                dve.tensor_tensor(zl[:, s, :], t_ps[j % 2][:, :].rearrange("p (k c) -> p k c", c=P),
                                  zh[:, s, :].bitcast(F32), ALU.subtract).then_inc(z_lo, 1)

            def choose(n):
                done = STEPS * n
                dve.wait_ge(s_mm, n + 1)
                dve.scalar_tensor_tensor(out=sc[:, :], in0=s_ps[:, :], scalar=float(RD) ** -0.5, in1=lrel[:, :],
                                         op0=ALU.mult, op1=ALU.add).then_inc(step, 1)
                dve.wait_ge(a_mm, n + 1)
                dve.wait_ge(step, done + 1)
                dve.scalar_tensor_tensor(out=lg[:, :], in0=a_ps[:, :], scalar=float(BOT) ** -0.5, in1=lrel[:, :],
                                         op0=ALU.mult, op1=ALU.add).then_inc(step, 1)
                dve.max(top[:, :], sc[:, :]).then_inc(step, 1)
                dve.wait_ge(step, done + 3)
                dve.tensor_scalar(g[3][:, :], nv[:, bass.ds(n, 1)], 1.0, None, ALU.mult).then_inc(gst, 1)
                dve.match_replace(rest[:, :], top[:, :], sc[:, :], FAR).then_inc(step, 1)
                dve.wait_ge(step, done + 4)
                dve.tensor_tensor(out_of[:, :], rest[:, :], sc[:, :], ALU.is_equal).then_inc(step, 1)
                dve.wait_ge(step, done + 5)
                dve.wait_ge(e_out, n + 1)
                dve.scalar_tensor_tensor(out=lgm[:, :], in0=out_of[:, :], scalar=FAR, in1=lg[:, :],
                                         op0=ALU.mult, op1=ALU.add).then_inc(step, 1)
                dve.wait_ge(step, done + 6)
                dve.tensor_reduce(mx[:, :], lgm[:, :], AX_X, ALU.max).then_inc(step, 1)
                dve.wait_ge(step, done + 7)
                dve.tensor_scalar(nmx[:, :], mx[:, :], -1.0, None, ALU.mult).then_inc(step, 1)

            def learn(n):
                dve.wait_ge(step, STEPS * (n + 1))
                dve.wait_ge(u_act, n + 1)
                dve.tensor_tensor_reduce(ug[:, :], ug[:, :], wu2[:, :], 1.0, 0.0, ALU.mult, ALU.add,
                                         learned[:, :]).then_inc(u_sum, 1)

            def gate(n):
                done = GSTEPS * n + 1

                def link(k, ins):
                    ins.then_inc(gst, 1)
                    dve.wait_ge(gst, done + k)

                dve.wait_ge(g_t1, n + 1)
                link(1, dve.tensor_scalar(g[1][:, :], g[0][:, :], 1.25, 1.25, ALU.mult, ALU.add))
                link(2, dve.tensor_scalar(g[2][:, :], g[1][:, :], g[3][:, 0:1], 0.0, ALU.add, ALU.max))
                link(3, dve.tensor_scalar(g[4][:, :], g[2][:, :], 5.0, TAU_LOW, ALU.min, ALU.subtract))
                link(4, dve.tensor_scalar(g[5][:, :], g[4][:, :], 1.0 / (TAU_HIGH - TAU_LOW), 0.0, ALU.mult, ALU.max))
                link(5, dve.tensor_scalar(g[6][:, :], g[5][:, :], 1.0, None, ALU.min))

            def gate_end(n):
                done = GSTEPS * n + GHALF

                def link(k, ins):
                    ins.then_inc(gst, 1)
                    dve.wait_ge(gst, done + k)

                dve.wait_ge(g_t2, n + 1)
                dve.wait_ge(e_out, n + 2)
                link(1, dve.tensor_scalar(g[8][:, :], g[7][:, :], 0.5, 0.5, ALU.mult, ALU.add))
                link(2, dve.scalar_tensor_tensor(out=g[9][:, :], in0=g[8][:, :], scalar=EARLY_EXIT, in1=g[8][:, :],
                                                 op0=ALU.is_ge, op1=ALU.mult))
                link(3, dve.reciprocal(g[10][:, :], esum[:, :]))
                link(4, dve.tensor_scalar(g[11][:, :], g[9][:, :], g[10][:, 0:1], None, ALU.mult))

            def read_low(n):
                dve.wait_ge(r_hi, n + 1)
                dve.tensor_tensor(rl[:, :], a_ps[:, 0:P], rh[:, :].bitcast(F32), ALU.subtract).then_inc(r_lo, 1)

            def add(n, i, u, hs):
                dve.wait_ge(yz_in[u], 16 * (i + 1))
                for h in hs:
                    s = slice(h * BANK, (h + 1) * BANK)
                    dve.wait_ge(o_mm, 4 * n + h + 1)
                    dve.scalar_tensor_tensor(out=yz[u][:, s], in0=o_ps[h % 2][:, :], scalar=g[11][:, 0:1],
                                             in1=yz[u][:, s], op0=ALU.mult, op1=ALU.add).then_inc(o_add, 1)

            def hidden(n, first=False):
                dve.wait_ge(u_mm, 4 * (n + 1))
                dve.tensor_scalar(q[:, :, :], u_ps[1][:, UH - HW:HW].unsqueeze(1).to_broadcast([P, 2, BOT]), 1.0, None, ALU.mult).then_inc(q_ok, 1)
                if not first:
                    dve.wait_ge(u_act, n)
                dve.tensor_tensor(ub[:, 0:HW], u_ps[0][:, 0:HW], bu1[:, 0:HW], ALU.add)
                dve.tensor_tensor(ub[:, HW:UH], u_ps[1][:, 0:UH - HW], bu1[:, HW:UH], ALU.add).then_inc(u_add, 1)

            def queries_low(n):
                dve.wait_ge(q_hi, n + 1)
                dve.tensor_tensor(qp[HP:P, :], qT[HP:P, :], qp[HP:P, :].bitcast(F32), ALU.subtract).then_inc(q_lo, 1)
                dve.wait_ge(rq_out, n + 1)
                dve.tensor_tensor(rqp[HP:P, :], s_ps[HP:P, RQ], rqp[HP:P, :].bitcast(F32),
                                  ALU.subtract).then_inc(rq_lo, 1)

            def settle():
                dve.wait_ge(tot_ok, 1)
                dve.tensor_scalar(mean[:, :], total[:, :], 1.0 / (N * C), 1e-6, ALU.mult, ALU.add).then_inc(mean_ok, 1)
                dve.wait_ge(mean_ok, 1)
                dve.reciprocal(rmean[:, :], mean[:, :]).then_inc(mean_ok, 1)
                dve.wait_ge(mean_ok, 2)
                dve.tensor_scalar(nv[:, :], logv[:, :], rmean[:, 0:1], 0.5, ALU.mult, ALU.mult).then_inc(mean_ok, 1)
                dve.wait_ge(mean_ok, 3)

            def after_heads(n, i, u, first=False, last=False):
                hidden(n, first)
                if not last:
                    low(n + 1, 0)
                queries_low(n)
                if not first:
                    add(n - 1, i, u, (0, 1))
                if not last:
                    low(n + 1, 1)
                if first:
                    settle()
                choose(n)
                if not last:
                    low(n + 1, 2)
                    low(n + 1, 3)
                if first:
                    dve.wait_ge(v_hi, 1)
                    dve.tensor_tensor(vl[:, :], vraw[:, :], vh[:, :].bitcast(F32), ALU.subtract).then_inc(v_lo, 1)
                if not first:
                    add(n - 1, i, u, (2, 3))
                learn(n)
                gate(n)
                read_low(n)
                gate_end(n)

            low(0, 0)
            low(0, 1)
            low(0, 2)
            low(0, 3)
            for n in range(N):
                dve.bn_aggr(mv[:, n, :], st_all[:, n, :]).then_inc(var_ok, 1)
            dve.wait_ge(small_in, 16 * SMALL)
            dve.tensor_scalar(half[:, :], cst[:, :], 0.5, None, ALU.mult).then_inc(half_ok, 1)
            dve.wait_ge(key_hi, 1)
            dve.tensor_tensor(kl[:, :], keysT[:, :], kh[:, :].bitcast(F32), ALU.subtract)
            dve.wait_ge(key_hi, 2)
            dve.tensor_tensor(rkl[:, :], rkT[:, :], rkh[:, :].bitcast(F32), ALU.subtract)
            after_heads(0, 0, 0, first=True)
            with dve.Fori(1, N // 2) as i:
                after_heads(2 * i - 1, i - 1, 0)
                after_heads(2 * i, i - 1, 1)
            after_heads(N - 1, N // 2 - 1, 0, last=True)
            add(N - 1, N // 2 - 1, 1, range(4))


def program(nc, a, out):
    def dram(name, shape):
        return nc.dram_tensor(name, shape, F32, kind="Internal").ap()

    scr = {
        "crow": dram("scr_crow", (N, C)), "aggb": dram("scr_aggb", (N, C)),
        "agg": dram("scr_agg", (N, C * C)), "la": dram("scr_la", (B, P, KC, 2 * R)),
        "lb": dram("scr_lb", (B, R, L)), "ct": dram("scr_ct", (N, P, KC * C)),
        "vp": dram("scr_vp", (P, NS // P * VB)), "rkT": dram("scr_rkT", (RD, NS)),
        "ax": dram("scr_ax", (N, 2 * R, P)), "z": dram("scr_z", (N, C, L)), "yz": dram("scr_yz", (N, C, L)),
    }
    with ExitStack() as ctx:
        ps = [ctx.enter_context(nc.psum_tensor(f"bank{i}", [P, BANK], F32)) for i in range(8)]
        st_all = ctx.enter_context(nc.sbuf_tensor("st_all", [P, N, 24], F32))
        with ExitStack() as kctx:
            with ExitStack() as cctx:
                taps = cctx.enter_context(nc.sbuf_tensor("taps", [P, 3, GROUPS, PH * GC], F32))
                xb = [cctx.enter_context(nc.sbuf_tensor(f"xb{i}", [P, GROUPS, M + 2], F32)) for i in range(2)]
                crow_bc = cctx.enter_context(nc.sbuf_tensor("crow_bc", [P, N, C], F32))
                prologue(nc, ps, a, scr, taps, xb, crow_bc)
                khi = kctx.enter_context(nc.sbuf_tensor("khi", [P, KC, HALF], F32R, side="right"))
                hi_at = nc.sbuf_top
                klo = kctx.enter_context(nc.sbuf_tensor("klo", [P, KC, HALF], F32R, side="right"))
                lo_at = nc.sbuf_top

                def over(name, shape, dt, at):
                    return nc.alloc_sbuf_tensor_at(name, shape, dt, offset=at), at + 4 * int(np.prod(shape[1:]))

                kraw, _ = over("kraw", [P, KC, HALF], F32, lo_at)
                wh, end = over("wh", [P, KC, UH + BOT], F32R, hi_at)
                zh, end = over("zh", [P, KC, P], F32R, end)
                vh, end = over("vh", [P, L], F32R, end)
                wraw, _ = over("wraw", [P, KC, UH + BOT], F32, lo_at)
                wl, end = over("wl", [P, KC, UH + BOT], F32R, lo_at)
                zl, end = over("zl", [P, KC, P], F32R, end)
                vraw, _ = over("vraw", [P, L], F32, end)
                vl, end = over("vl", [P, L], F32R, end)
                convolve(nc, ps, a, scr, khi, klo, kraw, taps, xb, crow_bc)
            raw = [kctx.enter_context(nc.sbuf_tensor(f"raw{i}", [P, L], F32)) for i in range(2)]
            project(nc, ps, a, scr, khi, klo, kraw, st_all, raw, wh, wl, wraw)
            attend(nc, ps, a, scr, st_all, raw, wh, wl, zh, zl, vh, vl, vraw, out)


def kernel(**inputs):
    import concourse.bacc as bacc
    from concourse.bass_utils import run_bass_kernel_spmd

    x = np.asarray(inputs["x"])
    v = {k: np.asarray(w) for k, w in inputs.items()}
    laid = {
        "x": x,
        "xph": x.reshape(N, GROUPS, GC, M, PH).transpose(0, 4, 2, 1, 3).reshape(N, P, GROUPS * M),
        "taps": v["L0_cond_weight"].reshape(GROUPS, GC, GC, TAPS).transpose(3, 2, 0, 1),
        "condT": v["cond_128"].T,
        "cwT": v["L0_cond_c_weight"].T,
        "conv_bias": v["fside_S_0"].reshape(1, C),
        "gate_rows": np.repeat(v["L0_ffn_gate"].T, R, axis=0),
        "kernel": v["L0_ffn_kernel"],
        "ffn_bias": v["L0_ffn_bias"].reshape(1, L),
        "loraA": v["L0_ffn_lora_A"].reshape(NL * R, L),
        "loraB": v["L0_ffn_lora_B"].transpose(0, 2, 1).reshape(NL * R, L),
        "laS": v["L0_ffn_lora_A_shared"].T,
        "lbS": v["L0_ffn_lora_B_shared"].T,
        "W0": v["L1_cond_W0"], "W1": v["L1_cond_W1"], "W2": v["L1_cond_W2"],
        "b0": v["L1_cond_b0"], "b1": v["L1_cond_b1"], "b2": v["L1_cond_b2"].reshape(1, NE),
        "wk": v["L1_cond_weight"][..., 0].transpose(0, 2, 1).reshape(NE, C * C),
        "bias_k": v["L1_cond_bias_k"],
        "wuq": np.concatenate([v["L1_ffn_Wu1"].T, v["L1_ffn_Wq"].T], axis=1),
        "wrT": v["L1_ffn_Wr"].T,
        "keysT": v["L1_ffn_aux_keys"].T,
        "avT": v["L1_ffn_aux_values"].T,
        "wvdT": v["L1_ffn_Wvd"].T,
        "wvuT": v["L1_ffn_Wvu"].T,
        "log_rel": v["L1_ffn_log_rel"].reshape(1, NS),
        "bu1": v["L1_ffn_bu1"].reshape(1, UH),
        "wu2": v["L1_ffn_Wu2"].reshape(1, UH),
        "bu2": v["L1_ffn_bu2"].reshape(1, 1),
        "gate_w1": v["L1_ffn_gate_w1"].reshape(1, 1),
        "gate_bias": v["L1_ffn_gate_bias"].reshape(1, 1),
    }
    nc = bacc.Bacc("TRN2", target_bir_lowering=False, num_devices=1)
    arrays, a = {}, {}
    for name, w in laid.items():
        w = np.ascontiguousarray(w)
        arrays[f"in_{name}"] = w
        a[name] = nc.dram_tensor(f"in_{name}", w.shape, mybir.dt.from_np(w.dtype), kind="ExternalInput").ap()
    out = nc.dram_tensor("out", (N, C, L), F32, kind="ExternalOutput").ap()
    program(nc, a, out)
    r = run_bass_kernel_spmd(nc, [arrays], core_ids=[0])
    return r.results[0]["out"]
```
